# Optimizing a Trainium2 kernel written in Bass

```python
import numpy as np
import jax
import jax.numpy as jnp

def _softmax(x, axis=-1):
    return jax.nn.softmax(x, axis=axis)

def _gelu(x):
    return jax.nn.gelu(x, approximate=True)

def _silu(x):
    return jax.nn.silu(x)

def _sigmoid(x):
    return jax.nn.sigmoid(x)

def _layernorm(x, axis=-1, eps=1e-05):
    m = jnp.mean(x, axis=axis, keepdims=True)
    v = jnp.var(x, axis=axis, keepdims=True)
    return (x - m) / jnp.sqrt(v + eps)

def _scatter_add(tgt, idx, src, axis=0):
    return tgt.at[idx].add(src)

def _segment_sum(src, seg, n):
    return jax.ops.segment_sum(src, seg, n)
kernel_name = 'mk_decoder_preln_d2_seqx_r4_22b0cf'

def setup_inputs(seed: int=0):
    np.random.seed(seed)
    _w = jnp.asarray

    def _rec_inputs():
        import jax
        import jax.numpy as jnp
        _rk = jax.random.key(seed)
        x = 7.22e-05 + 1 * jax.random.normal(jax.random.fold_in(_rk, 1), (4, 1024, 256), jnp.float32)
        _lenS = 1024 - jax.random.randint(jax.random.fold_in(_rk, 7), (4,), 0, max(1, 1024 // 4) + 1, jnp.int32)
        _lenS2 = 154 - jax.random.randint(jax.random.fold_in(_rk, 8), (4,), 0, max(1, 154 // 4) + 1, jnp.int32)
        _ctx_1024P = jax.random.normal(jax.random.fold_in(_rk, 11), (4, 16, 256), jnp.float32)
        _ctx_1024c = jax.random.dirichlet(jax.random.fold_in(_rk, 511), 0.3 * jnp.ones((16,), jnp.float32), (4, 154))
        _ctx_1024t = jnp.einsum('bsk,bkd->bsd', _ctx_1024c, _ctx_1024P)
        _ctx_1024t = _ctx_1024t * jax.lax.rsqrt(jnp.mean(jnp.square(_ctx_1024t)) + 1e-12) * 0.953939
        ctx_1024 = 4.13588e-05 + 0.999923 * (_ctx_1024t + 0.3 * jax.random.normal(jax.random.fold_in(_rk, 611), (4, 154, 256), jnp.float32))
        return (x, ctx_1024)
    x, ctx_1024 = _rec_inputs()

    def _L0_attn_setup():
        import jax, jax.numpy as jnp
        import numpy as np
        B, T, D, H, PD = (1, 512, 256, 16, 4)
        DH = D // H
        SCALE = DH ** (-0.5)
        _PI = jnp.array([0, 0, 0, 1, 1, 2])
        _PJ = jnp.array([1, 2, 3, 2, 3, 3])
        J6 = jnp.array([[0, 0, 0, 0, 0, 1], [0, 0, 0, 0, -1, 0], [0, 0, 0, 1, 0, 0], [0, 0, 1, 0, 0, 0], [0, -1, 0, 0, 0, 0], [1, 0, 0, 0, 0, 0]], dtype=jnp.float32)

        def exterior(p1, p2):
            L = p1[..., _PI] * p2[..., _PJ] - p1[..., _PJ] * p2[..., _PI]
            n = jnp.clip(jnp.linalg.norm(L, axis=-1, keepdims=True), 1e-12)
            return L / n
        key = jax.random.key(seed)
        ks = jax.random.split(key, 10)
        s = 0.02
        return {'x': jax.random.normal(ks[0], (B, T, D), dtype=jnp.float32), 'qkv_w': jax.random.normal(ks[1], (D, 3 * D), dtype=jnp.float32) * s, 'qkv_b': jnp.zeros((3 * D,), dtype=jnp.float32), 'w1_write': jax.random.normal(ks[2], (D, PD * H), dtype=jnp.float32) * s, 'w2_write': jax.random.normal(ks[3], (D, PD * H), dtype=jnp.float32) * s, 'w1_read': jax.random.normal(ks[4], (D, PD * H), dtype=jnp.float32) * s, 'w2_read': jax.random.normal(ks[5], (D, PD * H), dtype=jnp.float32) * s, 'kv_geo_w': jax.random.normal(ks[6], (D, 2 * D), dtype=jnp.float32) * s, 'out_w': jax.random.normal(ks[7], (D, D), dtype=jnp.float32) * s, 'out_b': jnp.zeros((D,), dtype=jnp.float32), 'kv_gate': jnp.asarray(0.01, dtype=jnp.float32), 'mem_scale': jnp.full((H,), 0.1, dtype=jnp.float32), 'decay_logits': jnp.full((H,), 4.6, dtype=jnp.float32)}
    _L0_attn_all = _L0_attn_setup()
    _L0_attn_in = {k: v for k, v in _L0_attn_all.items() if k in ('qkv_w', 'qkv_b', 'w1_write', 'w2_write', 'w1_read', 'w2_read', 'kv_geo_w', 'out_w', 'out_b', 'kv_gate', 'mem_scale', 'decay_logits')}
    del _L0_attn_all

    def _L0_xattn_setup():
        import jax, jax.numpy as jnp
        import numpy as np
        DIM = 256
        NUM_HEADS = 16
        HEAD_DIM = DIM // NUM_HEADS
        MAX_LEN = 512
        ROPE_BASE = 10000.0

        def _rope_tables(n, d, base=ROPE_BASE):
            inv_freq = 1.0 / base ** (np.arange(0, d, 2, dtype=np.float32) / d)
            t = np.arange(n, dtype=np.float32)
            freqs = np.outer(t, inv_freq)
            return (jnp.asarray(np.cos(freqs)), jnp.asarray(np.sin(freqs)))

        def _apply_rotary(x, cos, sin):
            xe = x[..., 0::2]
            xo = x[..., 1::2]
            oe = xe * cos - xo * sin
            oo = xe * sin + xo * cos
            return jnp.stack([oe, oo], axis=-1).reshape(x.shape)
        key = jax.random.key(seed)
        ks = jax.random.split(key, 11)
        B, T, S = (4, 512, 512)
        sc = 1.0 / np.sqrt(DIM)
        inp = {'query': jax.random.normal(ks[0], (B, T, DIM), jnp.float32), 'key': jax.random.normal(ks[1], (B, S, DIM), jnp.float32), 'value': jax.random.normal(ks[2], (B, S, DIM), jnp.float32), 'Wq': jax.random.normal(ks[3], (DIM, DIM), jnp.float32) * sc, 'bq': jnp.zeros((DIM,), jnp.float32), 'Wk': jax.random.normal(ks[4], (DIM, DIM), jnp.float32) * sc, 'bk': jnp.zeros((DIM,), jnp.float32), 'Wv': jax.random.normal(ks[5], (DIM, DIM), jnp.float32) * sc, 'bv': jnp.zeros((DIM,), jnp.float32), 'Wo': jax.random.normal(ks[6], (DIM, DIM), jnp.float32) * sc, 'bo': jnp.zeros((DIM,), jnp.float32)}
        return inp
    _L0_xattn_all = _L0_xattn_setup()
    _L0_xattn_in = {k: v for k, v in _L0_xattn_all.items() if k in ('Wq', 'bq', 'Wk', 'bk', 'Wv', 'bv', 'Wo', 'bo')}
    del _L0_xattn_all

    def _L0_ffn_setup():
        import jax, jax.numpy as jnp
        import numpy as np
        B, S, D_MODEL, D_HIDDEN = (4, 512, 256, 1024)

        def act_quant(x):
            scale = 127.0 / jnp.clip(jnp.max(jnp.abs(x), axis=-1, keepdims=True), 1e-05)
            return jnp.clip(jnp.round(x * scale), -128, 127) / scale

        def weight_quant(w):
            scale = 1.0 / jnp.clip(jnp.mean(jnp.abs(w)), 1e-05)
            return jnp.clip(jnp.round(w * scale), -1, 1) / scale

        def bit_linear(x, w):
            xq = x + jax.lax.stop_gradient(act_quant(x) - x)
            wq = w + jax.lax.stop_gradient(weight_quant(w) - w)
            return jnp.einsum('bsd,hd->bsh', xq, wq)

        def depthwise_conv1d(x_bcl, w, b):
            y = jax.lax.conv_general_dilated(x_bcl, w, window_strides=(1,), padding=[(1, 1)], dimension_numbers=('NCH', 'OIH', 'NCH'), feature_group_count=x_bcl.shape[1])
            return y + b[None, :, None]
        key = jax.random.key(seed)
        ks = jax.random.split(key, 5)
        lim1 = 1.0 / np.sqrt(D_MODEL)
        lim2 = 1.0 / np.sqrt(D_HIDDEN)
        limc = 1.0 / np.sqrt(3.0)
        return {'x': jax.random.normal(ks[0], (B, S, D_MODEL), dtype=jnp.float32), 'w1': jax.random.uniform(ks[1], (D_HIDDEN, D_MODEL), jnp.float32, -lim1, lim1), 'conv_w': jax.random.uniform(ks[2], (D_HIDDEN, 1, 3), jnp.float32, -limc, limc), 'conv_b': jax.random.uniform(ks[3], (D_HIDDEN,), jnp.float32, -limc, limc), 'w2': jax.random.uniform(ks[4], (D_MODEL, D_HIDDEN), jnp.float32, -lim2, lim2)}
    _L0_ffn_all = _L0_ffn_setup()
    _L0_ffn_in = {k: v for k, v in _L0_ffn_all.items() if k in ('w1', 'conv_w', 'conv_b', 'w2')}
    del _L0_ffn_all

    def _L1_attn_setup():
        import jax, jax.numpy as jnp
        import numpy as np
        import math
        N_HEADS = 16
        key = jax.random.key(seed)
        ks = jax.random.split(key, 5)
        B, S, E = (2, 512, 256)
        scale = 1.0 / math.sqrt(E)
        return {'x': jax.random.normal(ks[0], (B, S, E), dtype=jnp.float32), 'w_in': jax.random.normal(ks[1], (3 * E, E), dtype=jnp.float32) * scale, 'b_in': jax.random.normal(ks[2], (3 * E,), dtype=jnp.float32) * 0.01, 'w_out': jax.random.normal(ks[3], (E, E), dtype=jnp.float32) * scale, 'b_out': jax.random.normal(ks[4], (E,), dtype=jnp.float32) * 0.01}
    _L1_attn_all = _L1_attn_setup()
    _L1_attn_in = {k: v for k, v in _L1_attn_all.items() if k in ('w_in', 'b_in', 'w_out', 'b_out')}
    del _L1_attn_all

    def _L1_xattn_setup():
        import jax, jax.numpy as jnp
        import numpy as np
        EMBED = 256
        B, S = (4, 1024)
        INV_SCALE = float(EMBED ** 0.5)
        key = jax.random.key(seed)
        ks = jax.random.split(key, 6)
        std = 1.0 / np.sqrt(EMBED)
        return {'query': jax.random.normal(ks[0], (B, S, EMBED), jnp.float32), 'key': jax.random.normal(ks[1], (B, S, EMBED), jnp.float32), 'value': jax.random.normal(ks[2], (B, S, EMBED), jnp.float32), 'Wq': jax.random.normal(ks[3], (EMBED, EMBED), jnp.float32) * std, 'bq': jnp.zeros((EMBED,), jnp.float32), 'Wk': jax.random.normal(ks[4], (EMBED, EMBED), jnp.float32) * std, 'bk': jnp.zeros((EMBED,), jnp.float32), 'Wv': jax.random.normal(ks[5], (EMBED, EMBED), jnp.float32) * std, 'bv': jnp.zeros((EMBED,), jnp.float32)}
    _L1_xattn_all = _L1_xattn_setup()
    _L1_xattn_in = {k: v for k, v in _L1_xattn_all.items() if k in ('Wq', 'bq', 'Wk', 'bk', 'Wv', 'bv')}
    del _L1_xattn_all

    def _L1_ffn_setup():
        import jax, jax.numpy as jnp
        import numpy as np
        DIM = 256
        EXPERT_DIM = 128
        N_EXPERTS = 16
        TOPK = 2
        SHARED_HIDDEN = EXPERT_DIM * TOPK
        B, T = (4, 256)

        def _moe_forward(x, router_w, router_bias, up_proj, gate_proj, down_proj, sh_gate, sh_up, sh_down):
            Bb, Tt, D = x.shape
            flat = x.reshape(Bb * Tt, D)
            N = flat.shape[0]
            logits = flat @ router_w.T
            topk_scores, topk_idx = jax.lax.top_k(logits + router_bias, TOPK)
            topk_scores = jax.nn.softmax(topk_scores, axis=-1)
            combine = jnp.zeros((N, N_EXPERTS), flat.dtype)
            combine = combine.at[jnp.arange(N)[:, None], topk_idx].add(topk_scores)
            up_all = jnp.einsum('nd,kde->nke', flat, up_proj)
            gate_all = jnp.einsum('nd,kde->nke', flat, gate_proj)
            hidden = jax.nn.silu(gate_all) * up_all
            down_all = jnp.einsum('nke,ked->nkd', hidden, down_proj)
            out = jnp.einsum('nk,nkd->nd', combine, down_all)
            sh_hidden = jax.nn.silu(flat @ sh_gate.T) * (flat @ sh_up.T)
            out = out + sh_hidden @ sh_down.T
            return out.reshape(Bb, Tt, D)
        key = jax.random.key(seed)
        ks = jax.random.split(key, 9)
        std = 0.02
        return {'x': jax.random.normal(ks[0], (B, T, DIM), jnp.float32), 'router_w': jax.random.normal(ks[1], (N_EXPERTS, DIM), jnp.float32) * std, 'router_bias': jnp.zeros((N_EXPERTS,), jnp.float32), 'up_proj': jax.random.normal(ks[2], (N_EXPERTS, DIM, EXPERT_DIM), jnp.float32) * std, 'gate_proj': jax.random.normal(ks[3], (N_EXPERTS, DIM, EXPERT_DIM), jnp.float32) * std, 'down_proj': jax.random.normal(ks[4], (N_EXPERTS, EXPERT_DIM, DIM), jnp.float32) * std, 'sh_gate': jax.random.normal(ks[5], (SHARED_HIDDEN, DIM), jnp.float32) * std, 'sh_up': jax.random.normal(ks[6], (SHARED_HIDDEN, DIM), jnp.float32) * std, 'sh_down': jax.random.normal(ks[7], (DIM, SHARED_HIDDEN), jnp.float32) * std}
    _L1_ffn_all = _L1_ffn_setup()
    _L1_ffn_in = {k: v for k, v in _L1_ffn_all.items() if k in ('router_w', 'router_bias', 'up_proj', 'gate_proj', 'down_proj', 'sh_gate', 'sh_up', 'sh_down')}
    del _L1_ffn_all
    return {'x': x, 'ctx_1024': ctx_1024, 'L0_attn_qkv_w': _L0_attn_in['qkv_w'], 'L0_attn_qkv_b': _L0_attn_in['qkv_b'], 'L0_attn_w1_write': _L0_attn_in['w1_write'], 'L0_attn_w2_write': _L0_attn_in['w2_write'], 'L0_attn_w1_read': _L0_attn_in['w1_read'], 'L0_attn_w2_read': _L0_attn_in['w2_read'], 'L0_attn_kv_geo_w': _L0_attn_in['kv_geo_w'], 'L0_attn_out_w': _L0_attn_in['out_w'], 'L0_attn_out_b': _L0_attn_in['out_b'], 'L0_attn_kv_gate': _L0_attn_in['kv_gate'], 'L0_attn_mem_scale': _L0_attn_in['mem_scale'], 'L0_attn_decay_logits': _L0_attn_in['decay_logits'], 'L0_xattn_Wq': _L0_xattn_in['Wq'], 'L0_xattn_bq': _L0_xattn_in['bq'], 'L0_xattn_Wk': _L0_xattn_in['Wk'], 'L0_xattn_bk': _L0_xattn_in['bk'], 'L0_xattn_Wv': _L0_xattn_in['Wv'], 'L0_xattn_bv': _L0_xattn_in['bv'], 'L0_xattn_Wo': _L0_xattn_in['Wo'], 'L0_xattn_bo': _L0_xattn_in['bo'], 'L0_ffn_w1': _L0_ffn_in['w1'], 'L0_ffn_conv_w': _L0_ffn_in['conv_w'], 'L0_ffn_conv_b': _L0_ffn_in['conv_b'], 'L0_ffn_w2': _L0_ffn_in['w2'], 'L1_attn_w_in': _L1_attn_in['w_in'], 'L1_attn_b_in': _L1_attn_in['b_in'], 'L1_attn_w_out': _L1_attn_in['w_out'], 'L1_attn_b_out': _L1_attn_in['b_out'], 'L1_xattn_Wq': _L1_xattn_in['Wq'], 'L1_xattn_bq': _L1_xattn_in['bq'], 'L1_xattn_Wk': _L1_xattn_in['Wk'], 'L1_xattn_bk': _L1_xattn_in['bk'], 'L1_xattn_Wv': _L1_xattn_in['Wv'], 'L1_xattn_bv': _L1_xattn_in['bv'], 'L1_ffn_router_w': _L1_ffn_in['router_w'], 'L1_ffn_router_bias': _L1_ffn_in['router_bias'], 'L1_ffn_up_proj': _L1_ffn_in['up_proj'], 'L1_ffn_gate_proj': _L1_ffn_in['gate_proj'], 'L1_ffn_down_proj': _L1_ffn_in['down_proj'], 'L1_ffn_sh_gate': _L1_ffn_in['sh_gate'], 'L1_ffn_sh_up': _L1_ffn_in['sh_up'], 'L1_ffn_sh_down': _L1_ffn_in['sh_down']}

def reference(x, ctx_1024, L0_attn_qkv_w, L0_attn_qkv_b, L0_attn_w1_write, L0_attn_w2_write, L0_attn_w1_read, L0_attn_w2_read, L0_attn_kv_geo_w, L0_attn_out_w, L0_attn_out_b, L0_attn_kv_gate, L0_attn_mem_scale, L0_attn_decay_logits, L0_xattn_Wq, L0_xattn_bq, L0_xattn_Wk, L0_xattn_bk, L0_xattn_Wv, L0_xattn_bv, L0_xattn_Wo, L0_xattn_bo, L0_ffn_w1, L0_ffn_conv_w, L0_ffn_conv_b, L0_ffn_w2, L1_attn_w_in, L1_attn_b_in, L1_attn_w_out, L1_attn_b_out, L1_xattn_Wq, L1_xattn_bq, L1_xattn_Wk, L1_xattn_bk, L1_xattn_Wv, L1_xattn_bv, L1_ffn_router_w, L1_ffn_router_bias, L1_ffn_up_proj, L1_ffn_gate_proj, L1_ffn_down_proj, L1_ffn_sh_gate, L1_ffn_sh_up, L1_ffn_sh_down):
    import jax
    import jax.numpy as jnp

    def _L0_attn_ref(x, qkv_w, qkv_b, w1_write, w2_write, w1_read, w2_read, kv_geo_w, out_w, out_b, kv_gate, mem_scale, decay_logits):
        import jax, jax.numpy as jnp
        import numpy as np
        B, T, D, H, PD = (1, 512, 256, 16, 4)
        DH = D // H
        SCALE = DH ** (-0.5)
        _PI = jnp.array([0, 0, 0, 1, 1, 2])
        _PJ = jnp.array([1, 2, 3, 2, 3, 3])
        J6 = jnp.array([[0, 0, 0, 0, 0, 1], [0, 0, 0, 0, -1, 0], [0, 0, 0, 1, 0, 0], [0, 0, 1, 0, 0, 0], [0, -1, 0, 0, 0, 0], [1, 0, 0, 0, 0, 0]], dtype=jnp.float32)

        def exterior(p1, p2):
            L = p1[..., _PI] * p2[..., _PJ] - p1[..., _PJ] * p2[..., _PI]
            n = jnp.clip(jnp.linalg.norm(L, axis=-1, keepdims=True), 1e-12)
            return L / n
        b, t, d = x.shape
        qkv = (x @ qkv_w + qkv_b).reshape(b, t, 3, H, DH)
        q = qkv[:, :, 0].transpose(0, 2, 1, 3)
        k = qkv[:, :, 1].transpose(0, 2, 1, 3)
        v = qkv[:, :, 2].transpose(0, 2, 1, 3)
        x_prev = jnp.concatenate([jnp.zeros((b, 1, d), x.dtype), x[:, :-1]], axis=1)
        w1 = (x_prev @ w1_write).reshape(b, t, H, PD)
        w2 = (x @ w2_write).reshape(b, t, H, PD)
        write_lines = exterior(w1, w2)
        r1 = (x @ w1_read).reshape(b, t, H, PD)
        r2 = (x @ w2_read).reshape(b, t, H, PD)
        read_lines = exterior(r1, r2)
        j_write = jnp.einsum('bthi,ij->bthj', write_lines, J6)
        incidence = jnp.einsum('bthp,bshp->bhts', read_lines, j_write)
        pos = jnp.arange(t)
        diffs = pos[:, None] - pos[None, :]
        causal = diffs > 0
        decays = jax.nn.sigmoid(decay_logits)
        expn = jnp.maximum(diffs, 0).astype(x.dtype)
        weights = jnp.where(causal[None], decays[:, None, None] ** expn[None], 0.0)
        mem_score = jnp.einsum('bhts,hts->bht', incidence ** 2, weights)
        gram_gate = jax.nn.sigmoid(mem_score * mem_scale[None, :, None])[..., None]
        kv_geo = (x @ kv_geo_w).reshape(b, t, 2, H, DH)
        k_geo = kv_geo[:, :, 0].transpose(0, 2, 1, 3)
        v_geo = kv_geo[:, :, 1].transpose(0, 2, 1, 3)
        k_enh = k + kv_gate * gram_gate * k_geo
        v_enh = v + kv_gate * gram_gate * v_geo
        scores = jnp.einsum('bhtd,bhsd->bhts', q, k_enh) * SCALE
        scores = jnp.where((diffs >= 0)[None, None], scores, -jnp.inf)
        attn = jax.nn.softmax(scores, axis=-1)
        out = jnp.einsum('bhts,bhsd->bhtd', attn, v_enh)
        out = out.transpose(0, 2, 1, 3).reshape(b, t, d)
        return out @ out_w + out_b

    def _L0_xattn_ref(query, key, value, Wq, bq, Wk, bk, Wv, bv, Wo, bo):
        import jax, jax.numpy as jnp
        import numpy as np
        DIM = 256
        NUM_HEADS = 16
        HEAD_DIM = DIM // NUM_HEADS
        MAX_LEN = 512
        ROPE_BASE = 10000.0

        def _rope_tables(n, d, base=ROPE_BASE):
            inv_freq = 1.0 / base ** (np.arange(0, d, 2, dtype=np.float32) / d)
            t = np.arange(n, dtype=np.float32)
            freqs = np.outer(t, inv_freq)
            return (jnp.asarray(np.cos(freqs)), jnp.asarray(np.sin(freqs)))

        def _apply_rotary(x, cos, sin):
            xe = x[..., 0::2]
            xo = x[..., 1::2]
            oe = xe * cos - xo * sin
            oo = xe * sin + xo * cos
            return jnp.stack([oe, oo], axis=-1).reshape(x.shape)
        B, T, C = query.shape
        S = key.shape[1]
        H, D = (NUM_HEADS, HEAD_DIM)
        scale = D ** (-0.5)
        q = (query @ Wq + bq).reshape(B, T, H, D).transpose(0, 2, 1, 3)
        k = (key @ Wk + bk).reshape(B, S, H, D).transpose(0, 2, 1, 3)
        v = (value @ Wv + bv).reshape(B, S, H, D).transpose(0, 2, 1, 3)
        cos, sin = _rope_tables(max(T, S), D)
        q = _apply_rotary(q, cos[:T], sin[:T])
        k = _apply_rotary(k, cos[:S], sin[:S])
        scores = jnp.einsum('bhtd,bhsd->bhts', q, k) * scale
        causal = jnp.tril(jnp.ones((T, S), bool))
        scores = jnp.where(causal[None, None], scores, -jnp.inf)
        att = jax.nn.softmax(scores, axis=-1)
        out = jnp.einsum('bhts,bhsd->bhtd', att, v)
        out = out.transpose(0, 2, 1, 3).reshape(B, T, C)
        return out @ Wo + bo

    def _L0_ffn_ref(x, w1, conv_w, conv_b, w2):
        import jax, jax.numpy as jnp
        import numpy as np
        B, S, D_MODEL, D_HIDDEN = (4, 512, 256, 1024)

        def act_quant(x):
            scale = 127.0 / jnp.clip(jnp.max(jnp.abs(x), axis=-1, keepdims=True), 1e-05)
            return jnp.clip(jnp.round(x * scale), -128, 127) / scale

        def weight_quant(w):
            scale = 1.0 / jnp.clip(jnp.mean(jnp.abs(w)), 1e-05)
            return jnp.clip(jnp.round(w * scale), -1, 1) / scale

        def bit_linear(x, w):
            xq = x + jax.lax.stop_gradient(act_quant(x) - x)
            wq = w + jax.lax.stop_gradient(weight_quant(w) - w)
            return jnp.einsum('bsd,hd->bsh', xq, wq)

        def depthwise_conv1d(x_bcl, w, b):
            y = jax.lax.conv_general_dilated(x_bcl, w, window_strides=(1,), padding=[(1, 1)], dimension_numbers=('NCH', 'OIH', 'NCH'), feature_group_count=x_bcl.shape[1])
            return y + b[None, :, None]
        h = bit_linear(x, w1)
        h = depthwise_conv1d(h.transpose(0, 2, 1), conv_w, conv_b)
        h = h.transpose(0, 2, 1)
        h = jax.nn.silu(h)
        return bit_linear(h, w2)

    def _L1_attn_ref(x, w_in, b_in, w_out, b_out):
        import jax, jax.numpy as jnp
        import numpy as np
        import math
        N_HEADS = 16
        B, S, E = x.shape
        H = N_HEADS
        d = E // H
        qkv = x @ w_in.T + b_in
        q, k, v = jnp.split(qkv, 3, axis=-1)
        q = q.reshape(B, S, H, d).transpose(0, 2, 1, 3)
        k = k.reshape(B, S, H, d).transpose(0, 2, 1, 3)
        v = v.reshape(B, S, H, d).transpose(0, 2, 1, 3)
        scores = jnp.einsum('bhqd,bhkd->bhqk', q, k) / jnp.sqrt(jnp.float32(d)).astype(x.dtype)
        w = jax.nn.softmax(scores, axis=-1)
        out = jnp.einsum('bhqk,bhkd->bhqd', w, v)
        out = out.transpose(0, 2, 1, 3).reshape(B, S, E)
        return out @ w_out.T + b_out

    def _L1_xattn_ref(query, key, value, Wq, bq, Wk, bk, Wv, bv):
        import jax, jax.numpy as jnp
        import numpy as np
        EMBED = 256
        B, S = (4, 1024)
        INV_SCALE = float(EMBED ** 0.5)
        q = jnp.einsum('bsd,ed->bse', query, Wq) + bq
        k = jnp.einsum('bsd,ed->bse', key, Wk) + bk
        v = jnp.einsum('bsd,ed->bse', value, Wv) + bv
        scores = jnp.einsum('bqe,bke->bqk', q, k) / INV_SCALE
        probs = jax.nn.softmax(scores, axis=-1)
        return jnp.einsum('bqk,bke->bqe', probs, v)

    def _L1_ffn_ref(x, router_w, router_bias, up_proj, gate_proj, down_proj, sh_gate, sh_up, sh_down):
        import jax, jax.numpy as jnp
        import numpy as np
        DIM = 256
        EXPERT_DIM = 128
        N_EXPERTS = 16
        TOPK = 2
        SHARED_HIDDEN = EXPERT_DIM * TOPK
        B, T = (4, 256)

        def _moe_forward(x, router_w, router_bias, up_proj, gate_proj, down_proj, sh_gate, sh_up, sh_down):
            Bb, Tt, D = x.shape
            flat = x.reshape(Bb * Tt, D)
            N = flat.shape[0]
            logits = flat @ router_w.T
            topk_scores, topk_idx = jax.lax.top_k(logits + router_bias, TOPK)
            topk_scores = jax.nn.softmax(topk_scores, axis=-1)
            combine = jnp.zeros((N, N_EXPERTS), flat.dtype)
            combine = combine.at[jnp.arange(N)[:, None], topk_idx].add(topk_scores)
            up_all = jnp.einsum('nd,kde->nke', flat, up_proj)
            gate_all = jnp.einsum('nd,kde->nke', flat, gate_proj)
            hidden = jax.nn.silu(gate_all) * up_all
            down_all = jnp.einsum('nke,ked->nkd', hidden, down_proj)
            out = jnp.einsum('nk,nkd->nd', combine, down_all)
            sh_hidden = jax.nn.silu(flat @ sh_gate.T) * (flat @ sh_up.T)
            out = out + sh_hidden @ sh_down.T
            return out.reshape(Bb, Tt, D)
        return _moe_forward(x, router_w, router_bias, up_proj, gate_proj, down_proj, sh_gate, sh_up, sh_down)
    x = x + _L0_attn_ref(_layernorm(x, axis=-1), L0_attn_qkv_w, L0_attn_qkv_b, L0_attn_w1_write, L0_attn_w2_write, L0_attn_w1_read, L0_attn_w2_read, L0_attn_kv_geo_w, L0_attn_out_w, L0_attn_out_b, L0_attn_kv_gate, L0_attn_mem_scale, L0_attn_decay_logits)
    x = x + _L0_xattn_ref(_layernorm(x, axis=-1), ctx_1024, ctx_1024, L0_xattn_Wq, L0_xattn_bq, L0_xattn_Wk, L0_xattn_bk, L0_xattn_Wv, L0_xattn_bv, L0_xattn_Wo, L0_xattn_bo)
    x = x + _L0_ffn_ref(_layernorm(x, axis=-1), L0_ffn_w1, L0_ffn_conv_w, L0_ffn_conv_b, L0_ffn_w2)
    x = x + _L1_attn_ref(_layernorm(x, axis=-1), L1_attn_w_in, L1_attn_b_in, L1_attn_w_out, L1_attn_b_out)
    x = x + _L1_xattn_ref(_layernorm(x, axis=-1), ctx_1024, ctx_1024, L1_xattn_Wq, L1_xattn_bq, L1_xattn_Wk, L1_xattn_bk, L1_xattn_Wv, L1_xattn_bv)
    x = x + _L1_ffn_ref(_layernorm(x, axis=-1), L1_ffn_router_w, L1_ffn_router_bias, L1_ffn_up_proj, L1_ffn_gate_proj, L1_ffn_down_proj, L1_ffn_sh_gate, L1_ffn_sh_up, L1_ffn_sh_down)
    return x

_drawn_inputs = setup_inputs


def setup_inputs(seed=0):
    import zlib

    import numpy as np

    out = dict(_drawn_inputs(seed))
    spreads = {'L0_attn_qkv_b': (0.0, 0.1),
     'L0_attn_out_b': (0.0, 0.1),
     'L0_attn_mem_scale': (0.10000000149011612, 0.6),
     'L0_attn_decay_logits': (4.599999904632568, 0.6),
     'L0_xattn_bq': (0.0, 0.439),
     'L0_xattn_bk': (0.0, 0.8),
     'L0_xattn_bv': (0.0, 0.1),
     'L0_xattn_bo': (0.0, 0.1),
     'L1_xattn_bq': (0.0, 0.398),
     'L1_xattn_bk': (0.0, 0.8),
     'L1_xattn_bv': (0.0, 0.1),
     'L1_ffn_router_bias': (0.0, 0.8)}
    factors = {'L0_attn_qkv_w': 7.334,
     'L0_attn_w1_write': 8.0,
     'L0_attn_w2_write': 8.0,
     'L0_attn_w1_read': 8.0,
     'L0_attn_w2_read': 8.0,
     'L0_attn_kv_geo_w': 8.0,
     'L1_attn_b_in': 6.234,
     'L1_attn_b_out': 7.852,
     'L1_ffn_router_w': 8.0,
     'L1_ffn_up_proj': 8.0,
     'L1_ffn_gate_proj': 8.0,
     'L1_ffn_down_proj': 8.0,
     'L1_ffn_sh_gate': 4.34,
     'L1_ffn_sh_up': 4.385,
     'L1_ffn_sh_down': 4.247}
    for name, (base, spread) in spreads.items():
        noise = np.random.default_rng([zlib.crc32(name.encode()), seed]).standard_normal(out[name].shape)
        drawn = base * np.exp(spread * noise) if base else spread * noise
        out[name] = jnp.asarray(drawn.astype(out[name].dtype))
    for name, factor in factors.items():
        out[name] = (out[name] * factor).astype(out[name].dtype)
    return out
```

```python
import math
from contextlib import ExitStack, contextmanager

import numpy as np

import concourse.bass as bass
import concourse.mybir as mybir

F32 = mybir.dt.float32
BF16 = mybir.dt.bfloat16
U32 = mybir.dt.uint32
ALU = mybir.AluOpType
ACT = mybir.ActivationFunctionType
AX = mybir.AxisListType

P = 128
B, T, D, S = 4, 1024, 256, 154
NT = T // P
KD = D // P
H, DH = 16, 16
HG = 4
NG = H // HG
GW = HG * DH
HP = P // HG
HALF = 512
PARTS = 6
NR = PARTS * DH
NM = 3
HID = 1024
NH = HID // P
NE, ED = 16, 128
PAIRS = 21
CR = 7 * H
CTX = (128, S - 128)
FULL = (128,) * NT
ROUND = 12582912.0
LN_EPS = 1e-5
NEG = -1e30
J_SIGN = (1.0, -1.0, 1.0, 1.0, -1.0, 1.0)


class Token:

    def __init__(self, sem, count, loops):
        self.sem, self.count, self.loops = sem, count, loops


class Counts:

    def __init__(self, nc, per_trip):
        self.nc, self.per_trip = nc, per_trip
        self.count, self.loops, self.made, self.waited = {}, (), 0, {}

    def add(self, sem, n):
        self.count[sem] = self.count.get(sem, 0) + n
        return Token(sem, self.count[sem], self.loops)

    @contextmanager
    def loop(self, trips):
        number, self.made = self.made, self.made + 1
        before = dict(self.count)
        with self.nc.Fori(0, trips) as i:
            self.loops += ((i, number),)
            self.waited = {}
            yield i
            self.loops = self.loops[:-1]
        self.waited = {}
        each = {s: c - before.get(s, 0) for s, c in self.count.items() if c != before.get(s, 0)}
        each = {s.name: n for s, n in each.items()}
        self.per_trip[number] = each
        for s in self.count:
            self.count[s] = before.get(s, 0) + trips * each.get(s.name, 0)

    def wait(self, engine, who, token):
        assert self.loops[:len(token.loops)] == token.loops, "a token of a loop that has ended"
        key = (who, token.sem.name)
        if key in self.waited and self.waited[key] >= (len(token.loops), token.count):
            return
        self.waited[key] = (len(token.loops), token.count)
        value = token.count
        for i, number in token.loops:
            n = self.per_trip.get(number, {}).get(token.sem.name, 0)
            if n:
                value = i * n + value
        engine.wait_ge(token.sem, value)
        if value is not token.count:
            engine.sem_inc(self.carrier, 1)

    @contextmanager
    def fresh_loop(self, trips, engines):
        def restart():
            self.nc.all_engine_barrier()
            for e, sems in engines:
                for s in sems:
                    e.sem_clear(s)
            self.nc.all_engine_barrier()
            self.count, self.waited = {}, {}
            for e, sems in engines[:-1]:
                e.sem_inc(sems[0], 1)
                self.add(sems[0], 1)

        restart()
        with self.nc.Fori(0, trips) as i:
            yield i
            restart()


class Engine:

    def __init__(self, counts, engine, sem):
        self.counts, self.engine, self.sem = counts, engine, sem
        engine.sem_inc(sem, 1)
        counts.add(sem, 1)

    def after(self, *tokens):
        for t in tokens:
            if t is not None:
                self.counts.wait(self.engine, self.sem.name, t)

    def done(self, instruction):
        instruction.then_inc(self.sem, 1)
        return self.counts.add(self.sem, 1)

    def now(self):
        return self.counts.add(self.sem, 0)

    def own(self, instruction):
        t = self.done(instruction)
        self.after(t)
        return t


class Ring:

    def __init__(self, n, width=1, first=0):
        self.n, self.width, self.first, self.at, self.free = n, width, first, 0, [None] * n

    def take(self, engine):
        slot = self.at % self.n
        self.at += 1
        if self.free[slot] is not None:
            engine.after(self.free[slot])
        self.free[slot] = None
        return slot

    def release(self, slot, token):
        self.free[slot] = token

    def place(self, slot):
        return self.first + slot * self.width


class Area:

    def __init__(self, whole, words):
        self.whole, self.words, self.at = whole, words, 0

    def reset(self):
        self.at = 0

    def take(self, *shape, dtype=F32):
        n = math.prod(shape)
        words = n if dtype == F32 else n // 2
        assert self.at + words <= self.words, (self.at + words, self.words)
        v = self.whole[:, self.at:self.at + words]
        self.at += words
        if dtype != F32:
            v = v.bitcast(dtype)
        if len(shape) == 1:
            return v
        names = "abcde"[:len(shape)]
        sizes = dict(zip(names[1:], shape[1:]))
        return v.rearrange(f"p ({' '.join(names)}) -> p {' '.join(names)}", **sizes)


def spread(ap, axis, n):
    v = ap.unsqueeze(axis)
    shape = list(v.shape)
    shape[axis] = n
    return v.broadcast_to(shape)


def widen(ap, n):
    shape = list(ap.shape)
    shape[-1] = n
    return ap.broadcast_to(shape)


def build_program(nc, io, per_trip):
    c = Counts(nc, per_trip)
    ctx = ExitStack()
    with ctx:
        sem = lambda name: ctx.enter_context(nc.semaphore(name))
        sb = lambda name, *shape, dtype=F32: ctx.enter_context(nc.sbuf_tensor(name, [P, *shape], dtype))
        pe = Engine(c, nc.tensor, sem("pe_done"))
        act = Engine(c, nc.scalar, sem("act_done"))
        dve = Engine(c, nc.vector, sem("dve_done"))
        pool = Engine(c, nc.gpsimd, sem("pool_done"))
        sem_const, sem_x, sem_row = sem("constants_loaded"), sem("x_loaded"), sem("row_loaded")
        sem_expert = [sem("expert_even_loaded"), sem("expert_odd_loaded")]
        sem_comb, sem_out = sem("combine_stored"), sem("out_stored")
        c.carrier = sem("register_waits")
        sp = nc.sync
        owned = [(e.engine, (e.sem,)) for e in (pe, act, dve, pool)] + \
            [(sp, (sem_x, sem_row, *sem_expert, sem_comb, sem_out))]

        def load(dst, src, s):
            sp.dma_start(dst, src).then_inc(s, 16)
            return c.add(s, 16)

        def sp_after(*tokens):
            for t in tokens:
                c.wait(sp, "sp", t)

        psum = ctx.enter_context(nc.psum_tensor("psum", [P, 8, HALF], F32))
        bank = lambda k: psum[:, k, :]
        banks = lambda k, n: psum[:, k:k + n, :]

        resident = {}
        for name, ap in io.items():
            if name.startswith("r_"):
                resident[name[2:]] = sb(name[2:], *ap.shape[1:])
        ident = resident["ident"]
        ident_bf = sb("ident_bf", P, dtype=BF16)
        ones = sb("ones", P)
        w1q = sb("w1q", KD, HID, dtype=BF16)
        w2q = sb("w2q", NH, D, dtype=BF16)
        wscale = sb("wscale", 8)
        decay = sb("decay", 1)
        mem_decay = sb("mem_decay", H)
        x = sb("x", NT, D)
        xn = sb("xn", NT, D)
        xT = sb("xT", KD, 1 + T)
        ctxT = sb("ctxT", KD, S)
        gate = sb("gate", NT, H)
        small = sb("small", 512)
        words = (nc.sbuf_bytes_remaining - 2048) // 4
        area = Area(sb("work", words), words)

        def phase():
            nc.all_engine_barrier()
            area.reset()

        for name, t in resident.items():
            last = load(t[tuple(slice(None) for _ in t.shape)], io["r_" + name], sem_const)
        w1f = area.take(KD, HID)
        w2f = area.take(NH, D)
        load(w1f, io["w1T"], sem_const)
        last = load(w2f, io["w2T"], sem_const)
        dve.after(last)
        dve.done(nc.vector.tensor_copy(ident_bf[:, :], ident[:, :]))
        dve.own(nc.vector.memset(ones[:, :], 1.0))
        dve.done(nc.vector.memset(xT[:, :, 0:1], 0.0))
        for k, (w, wq) in enumerate(((w1f, w1q), (w2f, w2q))):
            flat = w.rearrange("p a b -> p (a b)")
            out = wq[:, :, :].rearrange("p a b -> p (a b)")
            summed = dve.done(nc.vector.tensor_reduce(small[:, k:k + 1], flat, AX.X, ALU.add,
                                                      apply_absolute_value=True))
            pe.after(summed)
            total = pe.done(nc.tensor.matmul(bank(k)[:, 0:1], ones[:, :], small[:, k:k + 1],
                                             start=True, stop=True))
            dve.after(total)
            mean = wscale[:, k:k + 1]
            dve.own(nc.vector.tensor_scalar(mean, bank(k)[:, 0:1], 1.0 / (D * HID), 1e-5,
                                            ALU.mult, ALU.max))
            dve.own(nc.vector.reciprocal(small[:, 2 + k:3 + k], mean))
            dve.own(nc.vector.tensor_scalar(flat, flat, small[:, 2 + k:3 + k], ROUND, ALU.mult, ALU.add))
            dve.own(nc.vector.tensor_scalar(flat, flat, ROUND, -1.0, ALU.subtract, ALU.max))
            dve.own(nc.vector.tensor_scalar(out, flat, 1.0, None, ALU.min))
        act.after(last)
        a = act.done(nc.scalar.activation(decay[0:CR, :], resident["logit_rows"][0:CR, :], ACT.Sigmoid))
        a = act.done(nc.scalar.activation(small[:, 16:32], resident["logits"][:, :], ACT.Sigmoid))
        dve.after(a)
        dve.own(nc.vector.tensor_tensor(mem_decay[:, :], small[:, 16:32], resident["mem_scale"][:, :], ALU.mult))

        def square_root(v, n, eps, at):
            s0, s1, s2 = (small[:, at + j * n:at + (j + 1) * n] for j in range(3))
            t = dve.own(nc.vector.tensor_scalar(s2, v, eps, None, ALU.add))
            act.after(t)
            t = act.done(nc.scalar.activation(s0, s2, ACT.Sqrt))
            dve.after(t)
            dve.own(nc.vector.tensor_scalar(s0, s0, 1e-18, None, ALU.max))
            dve.own(nc.vector.reciprocal(s1, s0))
            dve.own(nc.vector.tensor_tensor(s1, s1, s2, ALU.mult))
            dve.own(nc.vector.tensor_tensor(s0, s0, s1, ALU.add))
            dve.own(nc.vector.tensor_scalar(s0, s0, 0.5, None, ALU.mult))
            return s0

        def layer_norm():
            stats, mv = small[:, 128:128 + 6 * NT], small[:, 192:192 + 2 * NT]
            for i in range(NT):
                t = dve.done(nc.vector.bn_stats(stats[:, 6 * i:6 * i + 6], x[:, i, :]))
            dve.after(t)
            for i in range(NT):
                t = dve.done(nc.vector.bn_aggr(mv[:, 2 * i:2 * i + 2], stats[:, 6 * i:6 * i + 6]))
            dve.after(t)
            mv2 = mv.rearrange("p (i two) -> p two i", two=2)
            root = square_root(mv2[:, 1, :], NT, LN_EPS, 256)
            rstd = small[:, 320:320 + NT]
            dve.own(nc.vector.reciprocal(rstd, root))
            return [dve.done(nc.vector.tensor_scalar(xn[:, i, :], x[:, i, :], mv[:, 2 * i:2 * i + 1],
                                                     rstd[:, i:i + 1], ALU.subtract, ALU.mult))
                    for i in range(NT)]

        def turn_xn(ready):
            for j in range(NT // 2):
                pe.after(ready[2 * j + 1])
                for a in range(2):
                    for k in range(KD):
                        ins = nc.tensor.transpose(bank(j)[:, (2 * a + k) * P:(2 * a + k + 1) * P],
                                                  xn[:, 2 * j + a, k * P:(k + 1) * P], ident[:, :])
                turned = pe.done(ins)
                act.after(turned)
                dst = xT[:, :, 1 + 2 * P * j:1 + 2 * P * (j + 1)].rearrange("p k (a c) -> p a k c", a=2)
                for a in range(2):
                    act.done(nc.scalar.copy(dst[:, a], bank(j)[:, 2 * a * P:2 * (a + 1) * P]
                                            .rearrange("p (k c) -> p k c", k=KD)))

        def norm_phase():
            turn_xn(layer_norm())
            phase()

        def x_tile(i, k):
            return xT[:, k, 1 + P * i:1 + P * (i + 1)]

        def ctx_tile(i, k):
            return ctxT[:, k, P * i:P * i + CTX[i]]

        def project(out, tile, rows, w, ready=None):
            for k in range(KD):
                ins = nc.tensor.matmul(out, tile(k), w[:, k, :], start=(k == 0), stop=(k == KD - 1))
            return pe.done(ins)

        def add_bias(dst, src, bias, token, ring, slot):
            dve.after(token)
            t = dve.done(nc.vector.tensor_tensor(dst, src, bias, ALU.add))
            ring.release(slot, t)
            return t

        def attention(q_all, k_all, v_all, keys, causal, oT):
            ns = len(keys)
            nk = sum(keys)
            compact = [area.take(NT, GW) for _ in range(2)]
            rest = area.take(NT, GW)
            parts = [area.take(NT * HG, PARTS, DH, dtype=BF16) for _ in range(2)]
            turned = [area.take(HG, T, dtype=BF16) for _ in range(2)]
            qT, kT = turned
            V = area.take(ns, HG, HP)
            probs = area.take(4, 2, HALF)
            lows = area.take(2, HALF)
            top = small[:, 0:HG * NT].rearrange("p (h i) -> p h i", h=HG)
            top_rest = small[:, 32:64]
            top_bf = small[:, 64:64 + 48].bitcast(BF16).rearrange("p (a b) -> p a b", b=NM)

            ones_k = pool.own(nc.gpsimd.memset(kT[NR:NR + NM, :, :], 1.0))
            ones_v = pool.own(nc.gpsimd.memset(V, 1.0))
            with c.loop(NG) as g:
                everyone = (pe.now(), act.now(), dve.now(), pool.now())

                made = []
                for e, (src, n, comp, part) in enumerate(((q_all, NT, compact[0], parts[0]),
                                                          (k_all, ns, compact[1], parts[1]))):
                    dve.after(*everyone)
                    dve.own(nc.vector.tensor_copy(comp[:, 0:n, :], src[:, :, bass.ds(g * GW, GW)]))
                    flat = comp[:, 0:n, :].rearrange("p i (h d) -> p (i h) d", d=DH)
                    r = rest[:, 0:n, :].rearrange("p i (h d) -> p (i h) d", d=DH)
                    pt = part[:, 0:n * HG]
                    first, mid, lo = (slice(0, 3), slice(3, 5), slice(5, 6)) if e == 0 else \
                        (slice(0, 4, 3), slice(1, 5, 3), slice(2, 3))
                    copies = lambda s: len(range(s.start, s.stop, s.step or 1))
                    dve.own(nc.vector.tensor_copy(pt[:, :, first, :], spread(flat, 2, copies(first))))
                    if e == 1:
                        dve.done(nc.vector.tensor_copy(pt[:, :, 5, :], flat))
                    dve.own(nc.vector.tensor_tensor(r, flat, pt[:, :, 0, :], ALU.subtract))
                    dve.own(nc.vector.tensor_copy(pt[:, :, mid, :], spread(r, 2, copies(mid))))
                    m_at = mid.start
                    made.append(dve.own(nc.vector.tensor_tensor(pt[:, :, lo.start, :], r,
                                                                pt[:, :, m_at, :], ALU.subtract)))
                pool.after(*everyone)
                v_ready = pool.done(nc.gpsimd.tensor_copy(
                    V[:, :, :, 0:DH], v_all[:, :, bass.ds(g * GW, GW)].rearrange("p i (h d) -> p i h d", d=DH)))

                pe.after(*everyone)
                ring = Ring(8)
                split = []
                for e, n in ((0, NT), (1, ns)):
                    sizes = FULL if e == 0 else keys
                    pe.after(made[e])
                    for h in range(HG):
                        slot = ring.take(pe)
                        dst = bank(slot).bitcast(BF16)
                        for i in range(n):
                            src = parts[e][0:sizes[i], i * HG + h].rearrange("p a b -> p (a b)")
                            ins = nc.tensor.transpose(dst[0:NR, i * P:i * P + sizes[i]], src,
                                                      ident_bf[0:sizes[i], 0:sizes[i]])
                        t = pe.done(ins)
                        w = sum(sizes)
                        if h % 2:
                            dve.after(t, *everyone)
                            t = dve.done(nc.vector.tensor_copy(turned[e][0:NR, h, 0:w], dst[0:NR, 0:w]))
                        else:
                            act.after(t, *everyone)
                            t = act.done(nc.scalar.copy(turned[e][0:NR, h, 0:w], dst[0:NR, 0:w]))
                        ring.release(slot, t)
                        split.append(t)

                pair = Ring(4, 2)
                pe.after(*split)
                for i in range(NT):
                    n = min(P * (i + 1), nk) if causal else nk
                    for h in range(HG):
                        slot = pair.take(pe)
                        at = pair.place(slot)
                        for s0 in range(0, n, HALF):
                            w = min(HALF, n - s0)
                            ins = nc.tensor.matmul(bank(at + s0 // HALF)[:, 0:w], qT[0:NR, h, i * P:(i + 1) * P],
                                                   kT[0:NR, h, s0:s0 + w], start=True, stop=True)
                        scored = pe.done(ins)
                        dve.after(scored)
                        row = banks(at, 2).rearrange("p a b -> p (a b)")
                        if causal and P * i < nk:
                            diag = row[:, P * i:n]
                            dve.own(nc.vector.tensor_tensor(diag, diag, resident["tri"][:, 0:n - P * i], ALU.add))
                        t = dve.done(nc.vector.tensor_reduce(top[:, h, i:i + 1], row[:, 0:n], AX.X, ALU.max))
                        pair.release(slot, t)
                dve.after(t)
                flat = small[:, 0:HG * NT]
                dve.own(nc.vector.tensor_scalar(flat, flat, -1.0, None, ALU.mult))
                dve.own(nc.vector.tensor_copy(top_bf[:, :, 0], flat))
                dve.own(nc.vector.tensor_tensor(top_rest, flat, top_bf[:, :, 0], ALU.subtract))
                dve.own(nc.vector.tensor_copy(top_bf[:, :, 1], top_rest))
                top_cut = dve.own(nc.vector.tensor_tensor(top_bf[:, :, 2], top_rest, top_bf[:, :, 1], ALU.subtract))
                pe.after(top_cut)
                for h in range(HG):
                    dst = bank(h).bitcast(BF16)
                    for i in range(NT):
                        ins = nc.tensor.transpose(dst[NR:NR + NM, i * P:(i + 1) * P],
                                                  top_bf[:, h * NT + i, :], ident_bf[:, :])
                    t = pe.done(ins)
                    act.after(t)
                    max_in = act.done(nc.scalar.copy(qT[NR:NR + NM, h, :], dst[NR:NR + NM, 0:T]))

                pe.after(max_in, ones_k, v_ready)
                scores = Ring(3, 2)
                prob = Ring(4)
                rows = NR + NM
                for half in range(2):
                    end = HALF * (half + 1)
                    steps = [s for s in range(ns) if not causal or P * s < end]
                    acc = bank(6 + half)

                    def score(s):
                        t0 = max(HALF * half, P * s) if causal else HALF * half
                        n, size = end - t0, keys[s]
                        out = []
                        for hp in range(2):
                            slot = scores.take(pe)
                            at = scores.place(slot)
                            for a in range(2):
                                h = 2 * hp + a
                                ins = nc.tensor.matmul(bank(at + a)[0:size, 0:n], kT[0:rows, h, P * s:P * s + size],
                                                       qT[0:rows, h, t0:end], start=True, stop=True)
                            t = pe.done(ins)
                            ps = prob.take(act)
                            act.after(t)
                            t = act.done(nc.scalar.activation(probs[0:size, ps, :, 0:n], banks(at, 2)[0:size, :, 0:n],
                                                              ACT.Exp, scale=DH ** -0.5))
                            scores.release(slot, t)
                            if causal and t0 == P * s:
                                pool.after(t)
                                w = min(P, n)
                                blk = probs[0:size, ps, :, 0:w]
                                t = pool.done(nc.gpsimd.affine_select(
                                    out=blk, in_=blk, pattern=[[0, 2], [1, w]], compare_op=ALU.is_ge,
                                    fill=0.0, base=0, channel_multiplier=-1))
                            out.append((ps, t))
                        return t0, n, size, out

                    def values(s, t0, n, size, out):
                        for hp in range(2):
                            pe.after(out[hp][1])
                        for hp in range(2):
                            ps, _ = out[hp]
                            for a in range(2):
                                h = 2 * hp + a
                                ins = nc.tensor.matmul(
                                    acc[HP * h:HP * (h + 1), t0 - HALF * half:t0 - HALF * half + n],
                                    V[0:size, s, h, :], probs[0:size, ps, a, 0:n],
                                    start=(s == 0), stop=(s == steps[-1]), skip_group_check=True)
                        t = pe.done(ins)
                        for hp in range(2):
                            prob.release(out[hp][0], t)
                        return t

                    waiting = score(steps[0])
                    for j, s in enumerate(steps):
                        ahead = score(steps[j + 1]) if j + 1 < len(steps) else None
                        summed = values(s, *waiting)
                        waiting = ahead
                    dve.after(summed)
                    low = lows[:, half, :]
                    dve.own(nc.vector.stream_shuffle(low, acc, [DH] * 32))
                    dve.own(nc.vector.reciprocal(low, low))
                    dve.done(nc.vector.tensor_tensor(oT[:, bass.ds(g, 1), HALF * half:end].rearrange("p a t -> p (a t)"),
                                                     acc, low, ALU.mult))
            phase()

        def out_project(oT, w, bias):
            ring = Ring(8)
            for i in range(NT):
                slot = ring.take(pe)
                for g in range(NG):
                    ins = nc.tensor.matmul(bank(slot)[:, 0:D], oT[:, g, P * i:P * (i + 1)], w[:, g, :],
                                           start=(g == 0), stop=(g == NG - 1))
                dve.after(pe.done(ins))
                dve.own(nc.vector.tensor_tensor(x[:, i, :], x[:, i, :], bank(slot)[:, 0:D], ALU.add))
                t = dve.done(nc.vector.tensor_tensor(x[:, i, :], x[:, i, :], bias[:, :], ALU.add))
                ring.release(slot, t)
            phase()

        def geometry():
            lines = area.take(NT, 2 * 2 * 4 * H)
            for i in range(NT):
                for k in range(KD):
                    nc.tensor.matmul(bank(i)[:, 0:64], xT[:, k, P * i:P * (i + 1)], resident["geo"][:, k, 0:64],
                                     start=(k == 0), stop=(k == KD - 1))
                for k in range(KD):
                    ins = nc.tensor.matmul(bank(i)[:, 64:256], x_tile(i, k), resident["geo"][:, k, 64:256],
                                           start=(k == 0), stop=(k == KD - 1))
                t = pe.done(ins)
                act.after(t)
                copied = act.done(nc.scalar.copy(lines[:, i, :], bank(i)[:, 0:256]))
            dve.after(copied)
            pts = lines.rearrange("p i (w r) -> p (i w) r", w=2).rearrange("p n (two c h) -> p n two c h", two=2, c=4)
            one, two = pts[:, :, 0], pts[:, :, 1]
            L, N, LN = (area.take(2 * NT, 6, H) for _ in range(3))
            for i, (k0, n) in enumerate(((0, 3), (3, 2), (5, 1))):
                dve.done(nc.vector.tensor_tensor(L[:, :, k0:k0 + n, :], spread(one[:, :, i, :], 2, n),
                                                 two[:, :, i + 1:4, :], ALU.mult))
                t = dve.done(nc.vector.tensor_tensor(N[:, :, k0:k0 + n, :], one[:, :, i + 1:4, :],
                                                     spread(two[:, :, i, :], 2, n), ALU.mult))
            dve.after(t)
            flat = lambda v: v.rearrange("p a b c -> p (a b c)")
            dve.own(nc.vector.tensor_tensor(flat(L), flat(L), flat(N), ALU.subtract))
            dve.own(nc.vector.tensor_tensor(flat(N), flat(L), flat(L), ALU.mult))
            n2, s0, s1, rn = (area.take(2 * NT * H) for _ in range(4))
            dve.own(nc.vector.tensor_reduce(n2.rearrange("p (a h) -> p a h", h=H), N.rearrange("p a k h -> p a h k"),
                                            AX.X, ALU.add))
            act.after(dve.now())
            dve.after(act.done(nc.scalar.activation(s0, n2, ACT.Sqrt)))
            dve.own(nc.vector.tensor_scalar(s0, s0, 1e-18, None, ALU.max))
            dve.own(nc.vector.reciprocal(s1, s0))
            dve.own(nc.vector.tensor_tensor(s1, s1, n2, ALU.mult))
            dve.own(nc.vector.tensor_tensor(s0, s0, s1, ALU.add))
            dve.own(nc.vector.tensor_scalar(s0, s0, 0.5, 1e-12, ALU.mult, ALU.max))
            dve.own(nc.vector.reciprocal(rn, s0))
            by = lambda v, w: v.rearrange("p (i w) k h -> p i w k h", w=2)[:, :, w]
            rnv = rn.rearrange("p (i w h) -> p i w h", w=2, h=H)
            for k in range(6):
                dve.done(nc.vector.tensor_tensor(by(LN, 0)[:, :, k, :], by(L, 0)[:, :, 5 - k, :], rnv[:, :, 0, :], ALU.mult))
                t = dve.done(nc.vector.scalar_tensor_tensor(out=by(LN, 1)[:, :, k, :], in0=by(L, 1)[:, :, k, :],
                                                            scalar=J_SIGN[k], in1=rnv[:, :, 1, :],
                                                            op0=ALU.mult, op1=ALU.mult))
            dve.after(t)
            prods = area.take(2 * NT, PAIRS, H)
            s = 0
            for p in range(6):
                n = 6 - p
                t = dve.done(nc.vector.tensor_tensor(prods[:, :, s:s + n, :], spread(LN[:, :, p, :], 2, n),
                                                     LN[:, :, p:6, :], ALU.mult))
                s += n
            pe.after(t)
            turned = area.take(2, 3, T)
            ring = Ring(4, 2)
            flat_prods = prods.rearrange("p a s h -> p a (s h)")
            got = {}
            for w in range(2):
                for q in range(3):
                    slot = ring.take(pe)
                    dst = banks(ring.place(slot), 2).rearrange("p a b -> p (a b)")
                    for i in range(NT):
                        ins = nc.tensor.transpose(dst[0:CR, P * i:P * (i + 1)],
                                                  flat_prods[:, 2 * i + w, q * CR:(q + 1) * CR], ident[:, :])
                    act.after(pe.done(ins))
                    got[w, q] = act.done(nc.scalar.copy(turned[0:CR, w, q, :], dst[0:CR, :]))
                    ring.release(slot, got[w, q])
            state = area.take(3, 1 + T)
            dve.done(nc.vector.memset(state[:, :, 0:1], 0.0))
            for q in range(3):
                dve.after(got[0, q])
                t = dve.done(nc.vector.tensor_tensor_scan(state[0:CR, q, 1:1 + T], widen(decay[0:CR, :], T),
                                                          turned[0:CR, 0, q, :], 0.0, ALU.mult, ALU.add))
            dve.after(t, got[1, 2])
            read = turned[0:CR, 1]
            t = dve.done(nc.vector.tensor_tensor(read, read, state[0:CR, :, 0:T], ALU.mult))
            pe.after(t, act.now())
            for i in range(NT):
                for q in range(3):
                    ins = nc.tensor.matmul(bank(0)[:, H * i:H * (i + 1)], turned[0:CR, 1, q, P * i:P * (i + 1)],
                                           resident["pair_sum"][0:CR, q, :], start=(q == 0), stop=(q == 2))
            dve.after(pe.done(ins))
            t = dve.own(nc.vector.tensor_tensor(gate[:, :, :], bank(0)[:, 0:H * NT].rearrange("p (i h) -> p i h", h=H),
                                                spread(mem_decay[:, :], 1, NT), ALU.mult))
            act.after(t)
            dve.after(act.done(nc.scalar.activation(gate[:, :, :], gate[:, :, :], ACT.Sigmoid)))
            dve.done(nc.vector.tensor_scalar(gate[:, :, :], gate[:, :, :], resident["kv_gate"][:, 0:1], None, ALU.mult))
            phase()

        def column_to_rows(columns, dst):
            diag = area.take(NT, P)
            for i in range(NT):
                t = dve.done(nc.vector.tensor_scalar(diag[:, i, :], ident[:, :], columns[:, i:i + 1], None, ALU.mult))
            pe.after(t)
            for i in range(NT):
                ins = nc.tensor.matmul(banks(6, 2).rearrange("p a b -> p (a b)")[:, P * i:P * (i + 1)], ones[:, :],
                                       diag[:, i, :], start=True, stop=True)
            t = pe.done(ins)
            act.after(t)
            return act.done(nc.scalar.copy(dst, banks(6, 2).rearrange("p a b -> p (a b)")))

        def quantiser(top, inverse, scale, w_inverse):
            dve.own(nc.vector.tensor_scalar(top, top, 1e-5, None, ALU.max))
            dve.own(nc.vector.reciprocal(scale, top))
            dve.own(nc.vector.tensor_scalar(scale, scale, 127.0, None, ALU.mult))
            dve.own(nc.vector.tensor_scalar(inverse, top, 1.0 / 127.0, w_inverse, ALU.mult, ALU.mult))

        def bit_ffn():
            hid_flat = area.take(NH * (T + 2))
            hid = hid_flat.rearrange("p (m t) -> p m t", m=NH)
            conv = area.take(NH, T)
            whole = area.take(T)
            xqT = area.take(KD, T, dtype=BF16)
            xqb = hid_flat[:, 0:NT * D // 2].bitcast(BF16).rearrange("p (i d) -> p i d", i=NT)
            hq = hid_flat[:, 2 * (T + 2):2 * (T + 2) + NH * T // 2].bitcast(BF16).rearrange("p (m t) -> p m t", m=NH)
            top, inv, scale = (small[:, 400 + NT * j:400 + NT * (j + 1)] for j in range(3))
            t = layer_norm()[-1]
            dve.after(t)
            dve.own(nc.vector.tensor_reduce(top, xn[:, :, :], AX.X, ALU.max, apply_absolute_value=True))
            quantiser(top, inv, scale, wscale[:, 0:1])
            for i in range(NT):
                t = dve.done(nc.vector.tensor_scalar(xn[:, i, :], xn[:, i, :], scale[:, i:i + 1], ROUND, ALU.mult, ALU.add))
            dve.after(t)
            t = dve.done(nc.vector.tensor_scalar(xqb, xn[:, :, :], ROUND, None, ALU.subtract))
            pe.after(t)
            for k in range(KD):
                dst = bank(k).bitcast(BF16)
                for i in range(NT):
                    ins = nc.tensor.transpose(dst[:, P * i:P * (i + 1)], xqb[:, i, P * k:P * (k + 1)], ident_bf[:, :])
                act.after(pe.done(ins))
                turned = act.done(nc.scalar.copy(xqT[:, k, :], dst))
            spread_done = column_to_rows(inv, whole)
            dve.after(turned, spread_done)
            for col in (0, T + 1):
                dve.done(nc.vector.memset(hid[:, :, col:col + 1], 0.0))
            ring = Ring(6)
            pe.after(turned)
            filled = []
            for m in range(NH):
                for half in range(2):
                    slot = ring.take(pe)
                    for k in range(KD):
                        ins = nc.tensor.matmul(bank(slot), w1q[:, k, P * m:P * (m + 1)],
                                               xqT[:, k, HALF * half:HALF * (half + 1)], start=(k == 0), stop=(k == KD - 1))
                    dve.after(pe.done(ins))
                    t = dve.done(nc.vector.tensor_tensor(hid[:, m, 1 + HALF * half:1 + HALF * (half + 1)], bank(slot),
                                                         whole[:, HALF * half:HALF * (half + 1)], ALU.mult))
                    ring.release(slot, t)
                act.after(t)
                w = resident["conv_w"]
                mid = act.done(nc.scalar.activation(conv[:, m, :], hid[:, m, 1:1 + T], ACT.Identity,
                                                    bias=resident["conv_b"][:, m:m + 1], scale=w[:, m, 1:2]))
                dve.after(mid)
                dve.own(nc.vector.scalar_tensor_tensor(out=conv[:, m, :], in0=hid[:, m, 0:T], scalar=w[:, m, 0:1],
                                                       in1=conv[:, m, :], op0=ALU.mult, op1=ALU.add))
                t = dve.own(nc.vector.scalar_tensor_tensor(out=conv[:, m, :], in0=hid[:, m, 2:2 + T], scalar=w[:, m, 2:3],
                                                           in1=conv[:, m, :], op0=ALU.mult, op1=ALU.add))
                act.after(t)
                act.own(nc.scalar.activation(conv[:, m, :], conv[:, m, :], ACT.Silu))
                filled.append(act.done(nc.scalar.activation(hid[:, m, 0:T], conv[:, m, :], ACT.Abs)))
            hi = hid[:, 0, 0:T]
            for m in range(1, NH):
                dve.after(filled[m])
                t = dve.own(nc.vector.tensor_tensor(hi, hi, hid[:, m, 0:T], ALU.max))
            pe.after(t)
            for i in range(NT):
                ins = nc.tensor.transpose(banks(0, 2).rearrange("p a b -> p (a b)")[:, P * i:P * (i + 1)],
                                          hi[:, P * i:P * (i + 1)], ident[:, :])
            dve.after(pe.done(ins))
            dve.own(nc.vector.tensor_reduce(top, banks(0, 2).rearrange("p a b -> p (a b)")
                                            .rearrange("p (i b) -> p i b", i=NT), AX.X, ALU.max))
            quantiser(top, inv, scale, wscale[:, 1:2])
            t = column_to_rows(scale, whole)
            dve.after(t)
            done = []
            for m in range(NH):
                dve.own(nc.vector.tensor_tensor(conv[:, m, :], conv[:, m, :], whole, ALU.mult))
                done.append(dve.done(nc.vector.tensor_scalar(hq[:, m, :], conv[:, m, :],
                                                             ROUND, ROUND, ALU.add, ALU.subtract)))
            pe.after(done[-1])
            for i in range(NT):
                for m in range(NH):
                    ins = nc.tensor.matmul(bank(i)[:, 0:D], hq[:, m, P * i:P * (i + 1)], w2q[:, m, :],
                                           start=(m == 0), stop=(m == NH - 1))
                dve.after(pe.done(ins))
                dve.done(nc.vector.scalar_tensor_tensor(out=x[:, i, :], in0=bank(i)[:, 0:D], scalar=inv[:, i:i + 1],
                                                        in1=x[:, i, :], op0=ALU.mult, op1=ALU.add))
            phase()

        def wide_attention():
            qT, kT = area.take(KD, T), area.take(KD, S)
            v = area.take(2, D)
            ring = Ring(8)
            for m in range(KD):
                for half in range(2):
                    slot = ring.take(pe)
                    for k in range(KD):
                        ins = nc.tensor.matmul(bank(slot), resident["wide_q"][:, k, P * m:P * (m + 1)],
                                               xT[:, k, 1 + HALF * half:1 + HALF * (half + 1)],
                                               start=(k == 0), stop=(k == KD - 1))
                    act.after(pe.done(ins))
                    t = act.done(nc.scalar.activation(qT[:, m, HALF * half:HALF * (half + 1)], bank(slot), ACT.Identity,
                                                      bias=resident["wide_qb"][:, m:m + 1]))
                    ring.release(slot, t)
                slot = ring.take(pe)
                for k in range(KD):
                    ins = nc.tensor.matmul(bank(slot)[:, 0:S], resident["wide_k"][:, k, P * m:P * (m + 1)], ctxT[:, k, :],
                                           start=(k == 0), stop=(k == KD - 1))
                act.after(pe.done(ins))
                t = act.done(nc.scalar.activation(kT[:, m, :], bank(slot)[:, 0:S], ACT.Identity,
                                                  bias=resident["wide_kb"][:, m:m + 1]))
                ring.release(slot, t)
            for i, n in enumerate(CTX):
                slot = ring.take(pe)
                t = project(bank(slot)[0:n, 0:D], lambda k: ctx_tile(i, k), n, resident["wide_v"])
                add_bias(v[0:n, i, :], bank(slot)[0:n, 0:D], resident["wide_vb"][0:n, :], t, ring, slot)
            pe.after(act.now(), dve.now())
            E = area.take(2, S)
            ET = area.take(2, 2, P)
            top, rsum = small[:, 400:408], small[:, 408:416]
            scale = D ** -0.5
            taken = [None, None]
            for i in range(NT):
                e = i % 2
                s_bank, t_bank, o_bank = bank(e), bank(2 + e), bank(4 + e)
                pe.after(taken[e])
                for k in range(KD):
                    ins = nc.tensor.matmul(s_bank[:, 0:S], qT[:, k, P * i:P * (i + 1)], kT[:, k, :],
                                           start=(k == 0), stop=(k == KD - 1))
                dve.after(pe.done(ins))
                dve.own(nc.vector.tensor_reduce(top[:, i:i + 1], s_bank[:, 0:S], AX.X, ALU.max))
                t = dve.own(nc.vector.tensor_scalar(top[:, i:i + 1], top[:, i:i + 1], -scale, None, ALU.mult))
                act.after(t)
                t = act.done(nc.scalar.activation(E[:, e, :], s_bank[:, 0:S], ACT.Exp, bias=top[:, i:i + 1],
                                                  scale=scale, accum_out=rsum[:, i:i + 1]))
                pe.after(t)
                nc.tensor.transpose(t_bank[:, 0:P], E[:, e, 0:P], ident[:, :])
                ins = nc.tensor.transpose(t_bank[0:CTX[1], P:2 * P], E[:, e, P:S], ident[:, :])
                act.after(pe.done(ins))
                act.done(nc.scalar.copy(ET[:, e, 0, :], t_bank[:, 0:P]))
                t = act.done(nc.scalar.copy(ET[0:CTX[1], e, 1, :], t_bank[0:CTX[1], P:2 * P]))
                pe.after(t)
                for j, n in enumerate(CTX):
                    ins = nc.tensor.matmul(o_bank[:, 0:D], ET[0:n, e, j, :], v[0:n, j, :], start=(j == 0), stop=(j == 1))
                dve.after(pe.done(ins))
                dve.own(nc.vector.reciprocal(rsum[:, i:i + 1], rsum[:, i:i + 1]))
                taken[e] = dve.done(nc.vector.scalar_tensor_tensor(out=x[:, i, :], in0=o_bank[:, 0:D], scalar=rsum[:, i:i + 1],
                                                                   in1=x[:, i, :], op0=ALU.mult, op1=ALU.add))
            phase()

        def experts(b):
            logits, onehot, comb = area.take(NT, NE), area.take(NT, NE), area.take(NT, NE)
            best = area.take(NT, 8)
            index = area.take(NT, 8).bitcast(U32)
            p = area.take(4, NT)
            combT = area.take(T)
            sets = [[area.take(KD, ED), area.take(KD, ED), area.take(D), area.take(T)] for _ in range(2)]
            act_buf, hid = area.take(2, HALF), area.take(2, HALF)
            for i in range(NT):
                for k in range(KD):
                    ins = nc.tensor.matmul(bank(0)[:, NE * i:NE * (i + 1)], x_tile(i, k), resident["router"][:, k, :],
                                           start=(k == 0), stop=(k == KD - 1))
            dve.after(pe.done(ins))
            dve.own(nc.vector.tensor_tensor(logits, bank(0)[:, 0:NT * NE].rearrange("p (i e) -> p i e", e=NE),
                                            spread(resident["router_b"][:, :], 1, NT), ALU.add))
            for i in range(NT):
                t = dve.done(nc.vector.max(best[:, i, :], logits[:, i, :]))
            dve.after(t)
            for i in range(NT):
                t = dve.done(nc.vector.max_index(index[:, i, :], best[:, i, :], logits[:, i, :]))
            dve.after(t)
            t = dve.own(nc.vector.tensor_tensor(p[:, 0, :], best[:, :, 1], best[:, :, 0], ALU.subtract))
            act.after(t)
            dve.after(act.done(nc.scalar.activation(p[:, 1, :], p[:, 0, :], ACT.Exp)))
            dve.own(nc.vector.tensor_scalar(p[:, 0, :], p[:, 1, :], 1.0, None, ALU.add))
            dve.own(nc.vector.reciprocal(p[:, 2, :], p[:, 0, :]))
            dve.own(nc.vector.tensor_tensor(p[:, 3, :], p[:, 1, :], p[:, 2, :], ALU.mult))
            chosen = area.take(2, NT)
            dve.own(nc.vector.tensor_copy(chosen, index[:, :, 0:2].rearrange("p i two -> p two i")))
            for i in range(NT):
                for j, o in ((0, comb), (1, onehot)):
                    t = dve.done(nc.vector.tensor_scalar(o[:, i, :], resident["iota"][:, :], chosen[:, j, i:i + 1],
                                                         p[:, 2 + j, i:i + 1], ALU.is_equal, ALU.mult))
            dve.after(t)
            t = dve.own(nc.vector.tensor_tensor(comb, comb, onehot, ALU.add))
            pe.after(t)
            for i in range(NT):
                ins = nc.tensor.transpose(banks(2, 2).rearrange("p a b -> p (a b)")[0:NE, P * i:P * (i + 1)],
                                          comb[:, i, :], ident[:, :])
            act.after(pe.done(ins))
            t = act.done(nc.scalar.copy(combT[0:NE, :], banks(2, 2).rearrange("p a b -> p (a b)")[0:NE, :]))
            sp_after(t)
            stored = load(io["combine"], combT[0:NE, :], sem_comb)
            sp_after(stored)

            out = banks(4, 4).rearrange("p k (two d) -> p (k two) d", two=2)
            pair = Ring(2, 2)
            turn = [0]

            def expert(wg, wu, wd, weight, ready, first=False, last=False):
                made = []
                for half in range(2):
                    slot = pair.take(pe)
                    at = pair.place(slot)
                    pe.after(ready)
                    for j, w in ((0, wg), (1, wu)):
                        for k in range(KD):
                            ins = nc.tensor.matmul(bank(at + j), w[:, k, :], xT[:, k, 1 + HALF * half:1 + HALF * (half + 1)],
                                                   start=(k == 0), stop=(k == KD - 1))
                    t = pe.done(ins)
                    act.after(t, hid_free[half])
                    t = act.done(nc.scalar.activation(act_buf[:, half, :], bank(at), ACT.Silu))
                    dve.after(t)
                    t = dve.own(nc.vector.tensor_tensor(hid[:, half, :], act_buf[:, half, :], bank(at + 1), ALU.mult))
                    pair.release(slot, t)
                    if weight is not None:
                        dve.after(ready)
                        t = dve.done(nc.vector.tensor_tensor(hid[:, half, :], hid[:, half, :],
                                                             weight[:, HALF * half:HALF * (half + 1)], ALU.mult))
                    made.append(t)
                for half in range(2):
                    pe.after(made[half])
                    for i in range(4):
                        tile = 4 * half + i
                        ins = nc.tensor.matmul(out[:, tile, :], hid[:, half, P * i:P * (i + 1)], wd,
                                               start=(first and tile % 2 == 0), stop=last, skip_group_check=True)
                    hid_free[half] = pe.done(ins)
                return hid_free[1]

            hid_free = [None, None]
            shared = [(resident["sh_gate"][:, :, ED * j:ED * (j + 1)], resident["sh_up"][:, :, ED * j:ED * (j + 1)],
                       resident["sh_down"][:, j, :]) for j in range(2)]
            pe.after(act.now(), dve.now())
            expert(*shared[0], None, None, first=True)
            pe_before = pe.now()
            with c.loop(NE // 2) as j:
                loaded = []
                hid_free[:] = [pe.now(), pe.now()]
                pair.free = [dve.now(), dve.now()]
                for odd in range(2):
                    sp_after(pe.now())
                    s = sem_expert[odd]
                    e = j * 2 + odd
                    wg, wu, wd, wt = sets[odd]
                    load(wg, io["w_gate"][bass.ds(e, 1)].rearrange("a k p e -> p (a k) e"), s)
                    load(wu, io["w_up"][bass.ds(e, 1)].rearrange("a k p e -> p (a k) e"), s)
                    load(wd, io["w_down"][bass.ds(e, 1)].rearrange("a p d -> p (a d)"), s)
                    loaded.append(load(wt, io["combine"][bass.ds(e, 1), :].broadcast_to([P, T]), s))
                for odd in range(2):
                    wg, wu, wd, wt = sets[odd]
                    expert(wg, wu, wd, wt, loaded[odd])
            pair.free = [dve.now(), dve.now()]
            hid_free[:] = [pe.now(), pe.now()]
            done = expert(*shared[1], None, None, last=True)
            dve.after(done)
            for i in range(NT):
                t = dve.done(nc.vector.tensor_tensor(x[:, i, :], x[:, i, :], out[:, i, :], ALU.add))
            sp_after(t)
            load(io["out"][bass.ds(b, 1)].rearrange("b (i p) d -> p (b i) d", p=P), x[:, :, :], sem_out)
            sp_after(c.add(sem_out, 0))
            phase()

        with c.fresh_loop(B, owned) as b:
            area.reset()
            ctx_rows = area.take(2, D)
            load(x[:, :, :], io["x"][bass.ds(b, 1)].rearrange("b (i p) d -> p (b i) d", p=P), sem_x)
            for i, n in enumerate(CTX):
                t = load(ctx_rows[0:n, i:i + 1, :], io["ctx"][bass.ds(b, 1), P * i:P * i + n, :].rearrange("b p d -> p b d"), sem_x)
            pe.after(t)
            for k in range(KD):
                for i, n in enumerate(CTX):
                    ins = nc.tensor.transpose(bank(7)[:, k * 256 + P * i:k * 256 + P * i + n],
                                              ctx_rows[0:n, i, P * k:P * (k + 1)], ident[0:n, 0:n])
            act.after(pe.done(ins))
            act.done(nc.scalar.copy(ctxT[:, :, :], bank(7).rearrange("p (k s) -> p k s", k=KD)[:, :, 0:S]))
            dve.after(t)

            norm_phase()
            geometry()
            qkv = area.take(NT, 3 * D)
            oT = area.take(NG, T)
            mark = area.at
            ring = Ring(8)
            fresh = area.take(2, 2 * D)
            for i in range(NT):
                tile = lambda k: x_tile(i, k)
                sq, sk, sg = ring.take(pe), None, None
                t = project(bank(sq)[:, 0:D], tile, P, resident["qkv"][:, :, 0:D])
                add_bias(qkv[:, i, 0:D], bank(sq)[:, 0:D], resident["qkv_b"][:, 0:D], t, ring, sq)
                sk = ring.take(pe)
                t = project(bank(sk), tile, P, resident["qkv"][:, :, D:3 * D])
                t = add_bias(qkv[:, i, D:3 * D], bank(sk), resident["qkv_b"][:, D:3 * D], t, ring, sk)
                sg = ring.take(pe)
                g = project(bank(sg), tile, P, resident["kv_geo"])
                dve.after(g)
                v4 = lambda v: v.rearrange("p (a h d) -> p a h d", a=2, h=H)
                for a in range(2):
                    g = dve.own(nc.vector.tensor_tensor(
                        fresh[:, a, 0:D].rearrange("p (h d) -> p h d", h=H),
                        bank(sg)[:, a * D:(a + 1) * D].rearrange("p (h d) -> p h d", h=H),
                        spread(gate[:, i, :], 2, DH), ALU.mult))
                ring.release(sg, g)
                dve.own(nc.vector.tensor_tensor(qkv[:, i, D:3 * D].rearrange("p (a d) -> p a d", a=2),
                                                qkv[:, i, D:3 * D].rearrange("p (a d) -> p a d", a=2),
                                                fresh[:, :, 0:D], ALU.add))
            nc.all_engine_barrier()
            area.at = mark
            attention(qkv[:, :, 0:D], qkv[:, :, D:2 * D], qkv[:, :, 2 * D:3 * D], FULL, True, oT)
            out_project(oT, resident["out0"], resident["out0_b"])

            norm_phase()
            oT = area.take(NG, T)
            q = area.take(NT, D)
            kv = area.take(2, 2 * D)
            mark = area.at
            ring = Ring(8)
            kraw, qraw, t1, t2 = area.take(2, D), area.take(NT, D), area.take(NT * H, 8), area.take(NT * H, 8)
            for i in range(NT):
                slot = ring.take(pe)
                t = project(bank(slot)[:, 0:D], lambda k: x_tile(i, k), P, resident["cross_q"])
                add_bias(qraw[:, i, :], bank(slot)[:, 0:D], resident["cross_qb"][:, :], t, ring, slot)
            for i, n in enumerate(CTX):
                slot = ring.take(pe)
                t = project(bank(slot)[0:n, :], lambda k: ctx_tile(i, k), n, resident["cross_kv"])
                add_bias(kraw[0:n, i, :], bank(slot)[0:n, 0:D], resident["cross_kvb"][0:n, 0:D], t, ring, slot)
                dve.after(add_bias(kv[0:n, i, D:2 * D], bank(slot)[0:n, D:2 * D], resident["cross_kvb"][0:n, D:2 * D], t, ring, slot))

            def rotate(dst, src, i, n):
                even = lambda v, o: v.rearrange("p (h f two) -> p two h f", f=8, two=2)[:, o]
                xe, xo = even(src[0:n, i, :], 0), even(src[0:n, i, :], 1)
                cos = spread(resident["cos"][0:n, i, :], 1, H)
                sin = spread(resident["sin"][0:n, i, :], 1, H)
                a1, a2 = t1[0:n, 0:H, :], t2[0:n, 0:H, :]
                for o, (u, v, op) in enumerate(((cos, sin, ALU.subtract), (sin, cos, ALU.add))):
                    dve.done(nc.vector.tensor_tensor(a1, xe, u, ALU.mult))
                    dve.own(nc.vector.tensor_tensor(a2, xo, v, ALU.mult))
                    dve.own(nc.vector.tensor_tensor(even(dst, o), a1, a2, op))

            for i in range(NT):
                rotate(q[:, i, :], qraw, i, P)
            for i, n in enumerate(CTX):
                rotate(kv[0:n, i, 0:D], kraw, i, n)
            nc.all_engine_barrier()
            area.at = mark
            attention(q, kv[:, :, 0:D], kv[:, :, D:2 * D], CTX, True, oT)
            out_project(oT, resident["cross_o"], resident["cross_ob"])

            bit_ffn()

            norm_phase()
            qkv = area.take(NT, 3 * D)
            oT = area.take(NG, T)
            mark = area.at
            ring = Ring(8)
            for i in range(NT):
                for a, w in ((0, D), (D, 2 * D)):
                    slot = ring.take(pe)
                    t = project(bank(slot)[:, 0:w], lambda k: x_tile(i, k), P, resident["qkv1"][:, :, a:a + w])
                    add_bias(qkv[:, i, a:a + w], bank(slot)[:, 0:w], resident["qkv1_b"][:, a:a + w], t, ring, slot)
            nc.all_engine_barrier()
            area.at = mark
            attention(qkv[:, :, 0:D], qkv[:, :, D:2 * D], qkv[:, :, 2 * D:3 * D], FULL, False, oT)
            out_project(oT, resident["out1"], resident["out1_b"])

            norm_phase()
            wide_attention()
            norm_phase()
            experts(b)


def tiles(w):
    return np.ascontiguousarray(w.reshape(w.shape[0] // P, P, -1).transpose(1, 0, 2))


def rows(v, n=P):
    return np.ascontiguousarray(np.tile(v.reshape(1, -1), (n, 1)))


def head_rows(w):
    n = w.shape[1]
    out = np.zeros((HG, HP, NG, n), np.float32)
    out[:, :DH] = w.reshape(NG, HG, DH, n).transpose(1, 2, 0, 3)
    return out.reshape(P, NG, n)


def constants():
    f = 1.0 / 10000.0 ** (np.arange(0, DH, 2, dtype=np.float32) / DH)
    angle = np.outer(np.arange(T, dtype=np.float32), f)
    pair_sum = np.zeros((P, 3, H), np.float32)
    slot = 0
    for p in range(6):
        for q in range(p, 6):
            for h in range(H):
                pair_sum[(slot % 7) * H + h, slot // 7, h] = 1.0 if p == q else 2.0
            slot += 1
    tri = np.where(np.arange(P)[None, :] <= np.arange(P)[:, None], 0.0, NEG).astype(np.float32)
    return {"ident": np.eye(P, dtype=np.float32), "tri": tri, "pair_sum": pair_sum,
            "iota": rows(np.arange(NE, dtype=np.float32)),
            "cos": tiles(np.cos(angle)), "sin": tiles(np.sin(angle))}


def kernel(**i):
    import concourse.bacc as bacc
    from concourse.bass_utils import run_bass_kernel_spmd

    i = {k: np.asarray(v) for k, v in i.items()}
    L0, X0, F0, L1, X1, E1 = ("L0_attn_", "L0_xattn_", "L0_ffn_", "L1_attn_", "L1_xattn_", "L1_ffn_")
    points = lambda w: w.reshape(D, H, 4).transpose(0, 2, 1).reshape(D, 4 * H)
    scalar = lambda v: rows(v.reshape(1, 1))
    logit = i[L0 + "decay_logits"]
    resident = {
        **constants(),
        "geo": tiles(np.concatenate([points(i[L0 + n]) for n in ("w1_write", "w2_write", "w1_read", "w2_read")], 1)),
        "qkv": tiles(i[L0 + "qkv_w"]), "qkv_b": rows(i[L0 + "qkv_b"]), "kv_geo": tiles(i[L0 + "kv_geo_w"]),
        "out0": head_rows(i[L0 + "out_w"]), "out0_b": rows(i[L0 + "out_b"]),
        "kv_gate": scalar(i[L0 + "kv_gate"]), "mem_scale": rows(i[L0 + "mem_scale"]), "logits": rows(logit),
        "logit_rows": np.ascontiguousarray(np.tile(logit, P // H).reshape(P, 1)),
        "cross_q": tiles(i[X0 + "Wq"]), "cross_qb": rows(i[X0 + "bq"]),
        "cross_kv": tiles(np.concatenate([i[X0 + "Wk"], i[X0 + "Wv"]], 1)),
        "cross_kvb": rows(np.concatenate([i[X0 + "bk"], i[X0 + "bv"]])),
        "cross_o": head_rows(i[X0 + "Wo"]), "cross_ob": rows(i[X0 + "bo"]),
        "conv_w": tiles(i[F0 + "conv_w"].reshape(HID, 3)), "conv_b": tiles(i[F0 + "conv_b"].reshape(HID, 1)).reshape(P, NH),
        "qkv1": tiles(i[L1 + "w_in"].T), "qkv1_b": rows(i[L1 + "b_in"]),
        "out1": head_rows(i[L1 + "w_out"].T), "out1_b": rows(i[L1 + "b_out"]),
        "wide_q": tiles(i[X1 + "Wq"].T), "wide_k": tiles(i[X1 + "Wk"].T), "wide_v": tiles(i[X1 + "Wv"].T),
        "wide_qb": tiles(i[X1 + "bq"].reshape(D, 1)).reshape(P, KD),
        "wide_kb": tiles(i[X1 + "bk"].reshape(D, 1)).reshape(P, KD), "wide_vb": rows(i[X1 + "bv"]),
        "router": tiles(i[E1 + "router_w"].T), "router_b": rows(i[E1 + "router_bias"]),
        "sh_gate": tiles(i[E1 + "sh_gate"].T), "sh_up": tiles(i[E1 + "sh_up"].T), "sh_down": tiles(i[E1 + "sh_down"].T),
    }
    arrays = {"r_" + k: v for k, v in resident.items()}
    arrays.update({
        "x": i["x"], "ctx": i["ctx_1024"], "w1T": tiles(i[F0 + "w1"].T), "w2T": tiles(i[F0 + "w2"].T),
        "w_gate": i[E1 + "gate_proj"].reshape(NE, KD, P, ED), "w_up": i[E1 + "up_proj"].reshape(NE, KD, P, ED),
        "w_down": i[E1 + "down_proj"],
    })
    arrays = {k: np.ascontiguousarray(v) for k, v in arrays.items()}

    def write(per_trip):
        nc = bacc.Bacc("TRN2", target_bir_lowering=False, num_devices=1)
        io = {k: nc.dram_tensor("in_" + k, v.shape, F32, kind="ExternalInput").ap() for k, v in arrays.items()}
        io["combine"] = nc.dram_tensor("combine", (NE, T), F32, kind="Internal").ap()
        io["out"] = nc.dram_tensor("out", (B, T, D), F32, kind="ExternalOutput").ap()
        build_program(nc, io, per_trip)
        return nc

    per_trip = {}
    write(per_trip)
    nc = write(per_trip)
    return run_bass_kernel_spmd(nc, [{"in_" + k: v for k, v in arrays.items()}], core_ids=[0]).results[0]["out"]
```

```python
import math
from contextlib import ExitStack, contextmanager
from itertools import zip_longest

import numpy as np

import concourse.bass as bass
import concourse.mybir as mybir

F32 = mybir.dt.float32
BF16 = mybir.dt.bfloat16
U32 = mybir.dt.uint32
ALU = mybir.AluOpType
ACT = mybir.ActivationFunctionType
AX = mybir.AxisListType

P = 128
B, T, D, S = 4, 1024, 256, 154
NT = T // P
KD = D // P
H, DH = 16, 16
HG = 4
NG = H // HG
GW = HG * DH
HP = P // HG
HALF = 512
PARTS = 6
NR = PARTS * DH
NM = 3
HID = 1024
NH = HID // P
NE, ED = 16, 128
PAIRS = 21
CR = 7 * H
CTX = (128, S - 128)
FULL = (128,) * NT
ROUND = 12582912.0
LN_EPS = 1e-5
NEG = -1e30
J_SIGN = (1.0, -1.0, 1.0, 1.0, -1.0, 1.0)


class Token:

    def __init__(self, sem, count, loops):
        self.sem, self.count, self.loops = sem, count, loops


class Counts:

    def __init__(self, nc, per_trip):
        self.nc, self.per_trip = nc, per_trip
        self.count, self.loops, self.made, self.waited = {}, (), 0, {}

    def add(self, sem, n):
        self.count[sem] = self.count.get(sem, 0) + n
        return Token(sem, self.count[sem], self.loops)

    @contextmanager
    def loop(self, trips):
        number, self.made = self.made, self.made + 1
        before = dict(self.count)
        with self.nc.Fori(0, trips) as i:
            self.loops += ((i, number),)
            self.waited = {}
            yield i
            self.loops = self.loops[:-1]
        self.waited = {}
        each = {s: c - before.get(s, 0) for s, c in self.count.items() if c != before.get(s, 0)}
        each = {s.name: n for s, n in each.items()}
        self.per_trip[number] = each
        for s in self.count:
            self.count[s] = before.get(s, 0) + trips * each.get(s.name, 0)

    def wait(self, engine, who, token):
        assert self.loops[:len(token.loops)] == token.loops, "a token of a loop that has ended"
        key = (who, token.sem.name)
        if key in self.waited and self.waited[key] >= (len(token.loops), token.count):
            return
        self.waited[key] = (len(token.loops), token.count)
        value = token.count
        for i, number in token.loops:
            n = self.per_trip.get(number, {}).get(token.sem.name, 0)
            if n:
                value = i * n + value
        engine.wait_ge(token.sem, value)
        if value is not token.count:
            engine.sem_inc(self.carrier, 1)

    @contextmanager
    def fresh_loop(self, trips, engines):
        def restart():
            self.nc.all_engine_barrier()
            for e, sems in engines:
                for s in sems:
                    e.sem_clear(s)
            self.nc.all_engine_barrier()
            self.count, self.waited = {}, {}
            for e, sems in engines[:-1]:
                e.sem_inc(sems[0], 1)
                self.add(sems[0], 1)

        restart()
        with self.nc.Fori(0, trips) as i:
            yield i
            restart()


class Engine:

    def __init__(self, counts, engine, sem):
        self.counts, self.engine, self.sem = counts, engine, sem
        engine.sem_inc(sem, 1)
        counts.add(sem, 1)

    def after(self, *tokens):
        for t in tokens:
            if t is not None:
                self.counts.wait(self.engine, self.sem.name, t)

    def done(self, instruction):
        instruction.then_inc(self.sem, 1)
        return self.counts.add(self.sem, 1)

    def now(self):
        return self.counts.add(self.sem, 0)

    def own(self, instruction):
        t = self.done(instruction)
        self.after(t)
        return t


class Ring:

    def __init__(self, n, width=1, first=0):
        self.n, self.width, self.first, self.at, self.free = n, width, first, 0, [None] * n

    def take(self, engine):
        slot = self.at % self.n
        self.at += 1
        if self.free[slot] is not None:
            engine.after(self.free[slot])
        self.free[slot] = None
        return slot

    def release(self, slot, token):
        self.free[slot] = token

    def place(self, slot):
        return self.first + slot * self.width


class Area:

    def __init__(self, whole, words):
        self.whole, self.words, self.at = whole, words, 0

    def reset(self):
        self.at = 0

    def take(self, *shape, dtype=F32):
        n = math.prod(shape)
        words = n if dtype == F32 else n // 2
        assert self.at + words <= self.words, (self.at + words, self.words)
        v = self.whole[:, self.at:self.at + words]
        self.at += words
        if dtype != F32:
            v = v.bitcast(dtype)
        if len(shape) == 1:
            return v
        names = "abcde"[:len(shape)]
        sizes = dict(zip(names[1:], shape[1:]))
        return v.rearrange(f"p ({' '.join(names)}) -> p {' '.join(names)}", **sizes)


def spread(ap, axis, n):
    v = ap.unsqueeze(axis)
    shape = list(v.shape)
    shape[axis] = n
    return v.broadcast_to(shape)


def widen(ap, n):
    shape = list(ap.shape)
    shape[-1] = n
    return ap.broadcast_to(shape)


def build_program(nc, io, per_trip):
    c = Counts(nc, per_trip)
    ctx = ExitStack()
    with ctx:
        sem = lambda name: ctx.enter_context(nc.semaphore(name))
        sb = lambda name, *shape, dtype=F32: ctx.enter_context(nc.sbuf_tensor(name, [P, *shape], dtype))
        pe = Engine(c, nc.tensor, sem("pe_done"))
        act = Engine(c, nc.scalar, sem("act_done"))
        dve = Engine(c, nc.vector, sem("dve_done"))
        pool = Engine(c, nc.gpsimd, sem("pool_done"))
        sem_const, sem_x, sem_row = sem("constants_loaded"), sem("x_loaded"), sem("row_loaded")
        sem_expert = [sem("expert_even_loaded"), sem("expert_odd_loaded")]
        sem_comb, sem_out = sem("combine_stored"), sem("out_stored")
        c.carrier = sem("register_waits")
        ready = Engine(c, nc.vector, sem("group_ready"))
        sp = nc.sync
        owned = [(e.engine, (e.sem,)) for e in (pe, act, dve, pool, ready)] + \
            [(sp, (sem_x, sem_row, *sem_expert, sem_comb, sem_out))]

        def load(dst, src, s):
            sp.dma_start(dst, src).then_inc(s, 16)
            return c.add(s, 16)

        def sp_after(*tokens):
            for t in tokens:
                c.wait(sp, "sp", t)

        psum = ctx.enter_context(nc.psum_tensor("psum", [P, 8, HALF], F32))
        bank = lambda k: psum[:, k, :]
        banks = lambda k, n: psum[:, k:k + n, :]

        resident = {}
        for name, ap in io.items():
            if name.startswith("r_"):
                resident[name[2:]] = sb(name[2:], *ap.shape[1:])
        ident = resident["ident"]
        ident_bf = sb("ident_bf", P, dtype=BF16)
        tri_bf = sb("tri_bf", P, dtype=BF16)
        ones = sb("ones", P)
        w1q = sb("w1q", KD, HID, dtype=BF16)
        w2q = sb("w2q", NH, D, dtype=BF16)
        wscale = sb("wscale", 8)
        decay = sb("decay", 1)
        mem_decay = sb("mem_decay", H)
        x = sb("x", NT, D)
        xn = sb("xn", NT, D)
        xT = sb("xT", KD, 1 + T)
        ctxT = sb("ctxT", KD, S)
        gate = sb("gate", NT, H)
        small = sb("small", 512)
        words = (nc.sbuf_bytes_remaining - 256) // 4
        area = Area(sb("work", words), words)

        def phase():
            nc.all_engine_barrier()
            area.reset()

        for name, t in resident.items():
            last = load(t[tuple(slice(None) for _ in t.shape)], io["r_" + name], sem_const)
        w1f = area.take(KD, HID)
        w2f = area.take(NH, D)
        load(w1f, io["w1T"], sem_const)
        last = load(w2f, io["w2T"], sem_const)
        dve.after(last)
        dve.done(nc.vector.tensor_copy(ident_bf[:, :], ident[:, :]))
        dve.done(nc.vector.tensor_copy(tri_bf[:, :], resident["tri"][:, :]))
        dve.own(nc.vector.memset(ones[:, :], 1.0))
        dve.done(nc.vector.memset(xT[:, :, 0:1], 0.0))
        for k, (w, wq) in enumerate(((w1f, w1q), (w2f, w2q))):
            flat = w.rearrange("p a b -> p (a b)")
            out = wq[:, :, :].rearrange("p a b -> p (a b)")
            summed = dve.done(nc.vector.tensor_reduce(small[:, k:k + 1], flat, AX.X, ALU.add,
                                                      apply_absolute_value=True))
            pe.after(summed)
            total = pe.done(nc.tensor.matmul(bank(k)[:, 0:1], ones[:, :], small[:, k:k + 1],
                                             start=True, stop=True))
            dve.after(total)
            mean = wscale[:, k:k + 1]
            dve.own(nc.vector.tensor_scalar(mean, bank(k)[:, 0:1], 1.0 / (D * HID), 1e-5,
                                            ALU.mult, ALU.max))
            dve.own(nc.vector.reciprocal(small[:, 2 + k:3 + k], mean))
            dve.own(nc.vector.tensor_scalar(flat, flat, small[:, 2 + k:3 + k], ROUND, ALU.mult, ALU.add))
            dve.own(nc.vector.tensor_scalar(flat, flat, ROUND, -1.0, ALU.subtract, ALU.max))
            dve.own(nc.vector.tensor_scalar(out, flat, 1.0, None, ALU.min))
        act.after(last)
        a = act.done(nc.scalar.activation(decay[0:CR, :], resident["logit_rows"][0:CR, :], ACT.Sigmoid))
        a = act.done(nc.scalar.activation(small[:, 16:32], resident["logits"][:, :], ACT.Sigmoid))
        dve.after(a)
        dve.own(nc.vector.tensor_tensor(mem_decay[:, :], small[:, 16:32], resident["mem_scale"][:, :], ALU.mult))

        def square_root(v, n, eps, at):
            s0, s1, s2 = (small[:, at + j * n:at + (j + 1) * n] for j in range(3))
            t = dve.own(nc.vector.tensor_scalar(s2, v, eps, None, ALU.add))
            act.after(t)
            t = act.done(nc.scalar.activation(s0, s2, ACT.Sqrt))
            dve.after(t)
            dve.own(nc.vector.tensor_scalar(s0, s0, 1e-18, None, ALU.max))
            dve.own(nc.vector.reciprocal(s1, s0))
            dve.own(nc.vector.tensor_tensor(s1, s1, s2, ALU.mult))
            dve.own(nc.vector.tensor_tensor(s0, s0, s1, ALU.add))
            dve.own(nc.vector.tensor_scalar(s0, s0, 0.5, None, ALU.mult))
            return s0

        def layer_norm():
            stats, mv = small[:, 128:128 + 6 * NT], small[:, 192:192 + 2 * NT]
            for i in range(NT):
                t = dve.done(nc.vector.bn_stats(stats[:, 6 * i:6 * i + 6], x[:, i, :]))
            dve.after(t)
            for i in range(NT):
                t = dve.done(nc.vector.bn_aggr(mv[:, 2 * i:2 * i + 2], stats[:, 6 * i:6 * i + 6]))
            dve.after(t)
            mv2 = mv.rearrange("p (i two) -> p two i", two=2)
            root = square_root(mv2[:, 1, :], NT, LN_EPS, 256)
            rstd = small[:, 320:320 + NT]
            dve.own(nc.vector.reciprocal(rstd, root))
            return [dve.done(nc.vector.tensor_scalar(xn[:, i, :], x[:, i, :], mv[:, 2 * i:2 * i + 1],
                                                     rstd[:, i:i + 1], ALU.subtract, ALU.mult))
                    for i in range(NT)]

        def turn_xn(ready):
            for j in range(NT // 2):
                pe.after(ready[2 * j + 1])
                for a in range(2):
                    for k in range(KD):
                        ins = nc.tensor.transpose(bank(j)[:, (2 * a + k) * P:(2 * a + k + 1) * P],
                                                  xn[:, 2 * j + a, k * P:(k + 1) * P], ident[:, :])
                turned = pe.done(ins)
                act.after(turned)
                dst = xT[:, :, 1 + 2 * P * j:1 + 2 * P * (j + 1)].rearrange("p k (a c) -> p a k c", a=2)
                for a in range(2):
                    act.done(nc.scalar.copy(dst[:, a], bank(j)[:, 2 * a * P:2 * (a + 1) * P]
                                            .rearrange("p (k c) -> p k c", k=KD)))

        def norm_phase():
            turn_xn(layer_norm())
            phase()

        def x_tile(i, k):
            return xT[:, k, 1 + P * i:1 + P * (i + 1)]

        def ctx_tile(i, k):
            return ctxT[:, k, P * i:P * i + CTX[i]]

        def project(out, tile, rows, w, ready=None):
            for k in range(KD):
                ins = nc.tensor.matmul(out, tile(k), w[:, k, :], start=(k == 0), stop=(k == KD - 1))
            return pe.done(ins)

        def add_bias(dst, src, bias, token, ring, slot):
            dve.after(token)
            t = dve.done(nc.vector.tensor_tensor(dst, src, bias, ALU.add))
            ring.release(slot, t)
            return t

        def attention(q_all, k_all, v_all, keys, causal, oT):
            ns = len(keys)
            nk = sum(keys)
            first_rows, rows = NR, NR + NM
            parts = [area.take(NT * HG, PARTS, DH, dtype=BF16) for _ in range(2)]
            ahead = [area.take(HG, T, dtype=BF16) for _ in range(2)]
            qT, kT = (area.take(HG, T, dtype=BF16) for _ in range(2))
            V = area.take(ns, HG, HP)
            probs = area.take(4, 2, HALF)
            low = area.take(HALF)
            kept, low_turned = xT[:, 0, 1:1 + T].rearrange("p (half t) -> p half t", half=2), xT[:, 1, 1:1 + HALF]
            idle = xn[:, :, :].rearrange("p i d -> p (i d)").rearrange("p (four i d) -> p four i d", four=4, i=NT)
            tops = small[:, 0:2 * HG * NT].rearrange("p (h i two) -> p h i two", h=HG, two=2)
            top, top_rest = small[:, 64:96], small[:, 96:128]
            top_bf = small[:, 128:128 + 48].bitcast(BF16).rearrange("p (a b) -> p a b", b=NM)
            pool.own(nc.gpsimd.memset(kT[NR:rows, :, :], 1.0))
            pool.own(nc.gpsimd.memset(V, 1.0))
            dve.own(nc.vector.memset(small[:, 0:2 * HG * NT], -3e38))

            def split(e, g, by=None):
                eng, ops = (dve, nc.vector) if (by or (dve, pool)[e]) is dve else (pool, nc.gpsimd)
                src, n = ((q_all, NT), (k_all, ns))[e]
                flat, r = (idle[:, 2 * e + j, 0:n, :].rearrange("p i (h d) -> p (i h) d", d=DH) for j in range(2))
                part = parts[e][:, 0:n * HG]
                high, mid, last = ((0, 1, 2), (3, 4), 5) if e == 0 else ((0, 3, 5), (1, 4), 2)
                turned = pe.now()

                def step(op, *args):
                    def run():
                        eng.after(eng.now(), turned)
                        eng.done(op(*args))
                    return run

                at = lambda j: part[:, :, j, :]
                copy, minus = ops.tensor_copy, ops.tensor_tensor
                return [step(copy, idle[:, 2 * e, 0:n, :], src[:, :, bass.ds(g * GW, GW)]),
                        step(copy, at(high[0]), flat),
                        step(minus, r, flat, at(high[0]), ALU.subtract),
                        step(copy, at(mid[0]), r),
                        step(minus, at(last), r, at(mid[0]), ALU.subtract),
                        step(copy, at(high[1]), at(high[0])),
                        step(copy, at(high[2]), at(high[0])),
                        step(copy, at(mid[1]), at(mid[0]))]

            def first_pass(following, cut_keys=None):
                ring = Ring(3, first=4)
                turned, last = {}, {}
                cut, copied = (dve.now(), cut_keys or pool.now()), ready.now()

                def turn(e, h):
                    sizes = FULL if e == 0 else keys
                    pe.after(cut[e])
                    slot = ring.take(pe)
                    dst = bank(ring.place(slot)).bitcast(BF16)
                    for i, size in enumerate(sizes):
                        src = parts[e][0:size, i * HG + h].rearrange("p a b -> p (a b)")
                        ins = nc.tensor.transpose(dst[0:NR, i * P:i * P + size], src, ident_bf[0:size, 0:size])
                    act.after(pe.done(ins), copied)
                    turned[h] = act.done(nc.scalar.copy(ahead[e][0:NR, h, 0:sum(sizes)], dst[0:NR, 0:sum(sizes)]))
                    ring.release(slot, turned[h])

                def largest(h, tiles, part, s0, n):
                    slot = ring.take(pe)
                    pe.after(turned[h])
                    whole = bank(ring.place(slot))[:, 0:len(tiles) * n].rearrange("p (a n) -> p a n", n=n)
                    for a, i in enumerate(tiles):
                        dst = whole[:, a]
                        masked = causal and P * i < nk and s0 <= P * i < s0 + n
                        ins = nc.tensor.matmul(dst, ahead[0][0:NR, h, i * P:(i + 1) * P],
                                               ahead[1][0:NR, h, s0:s0 + n],
                                               start=True, stop=not masked, skip_group_check=True)
                        if masked:
                            ins = nc.tensor.matmul(dst[:, P * i - s0:n], ident_bf[:, :], tri_bf[:, 0:s0 + n - P * i],
                                                   start=False, stop=True, skip_group_check=True)
                    dve.after(pe.done(ins))
                    t = dve.done(nc.vector.tensor_reduce(tops[:, h, tiles[0]:tiles[-1] + 1, part], whole, AX.X, ALU.max))
                    ring.release(slot, t)
                    last[h] = t

                def negate(h, stage):
                    at = slice(h * NT, (h + 1) * NT)
                    m, rest, cut_m = top[:, at], top_rest[:, at], lambda j: top_bf[:, at, j]
                    dve.after(last[h])
                    if stage == 0:
                        ins = nc.vector.tensor_reduce(m, tops[:, h], AX.X, ALU.max, negate=True)
                    elif stage == 2:
                        ins = nc.vector.tensor_tensor(rest, m, cut_m(0), ALU.subtract)
                    elif stage == 4:
                        ins = nc.vector.tensor_tensor(cut_m(2), rest, cut_m(1), ALU.subtract)
                    else:
                        ins = nc.vector.tensor_copy(cut_m(stage // 2), (m, rest)[stage // 2])
                    last[h] = dve.done(ins)

                def turn_top(h):
                    pe.after(last[h])
                    slot = ring.take(pe)
                    dst = bank(ring.place(slot)).bitcast(BF16)
                    for i in range(NT):
                        ins = nc.tensor.transpose(dst[NR:rows, i * P:(i + 1) * P], top_bf[:, h * NT + i, :], ident_bf[:, :])
                    act.after(pe.done(ins))
                    ring.release(slot, act.done(nc.scalar.copy(ahead[0][NR:rows, h, :], dst[NR:rows, 0:T])))

                def split_keys():
                    for run in split(1, following):
                        run()

                pieces = [(turn, 0, 0), (turn, 1, 0)]
                for h in range(HG):
                    units, i = [], 0
                    while i < NT:
                        n = min(P * (i + 1), nk) if causal else nk
                        tiles = [i + a for a in range(max(1, HALF // n) if n == nk else 1) if i + a < NT]
                        units += [(largest, h, tiles, part, s0, min(HALF, n - s0)) for part, s0 in enumerate(range(0, n, HALF))]
                        i += len(tiles)
                    extra = []
                    if h:
                        extra = [(negate, h - 1, stage) for stage in range(5)] + [None, (turn_top, h - 1)]
                    if h < HG - 1:
                        extra += [(turn, 0, h + 1), (turn, 1, h + 1)]
                    elif following is not None:
                        queries = [(run,) for run in split(0, following)]
                        extra = [(split_keys,)] + [p for pair in zip_longest(extra, queries) for p in pair]
                    for j, unit in enumerate(units):
                        pieces.append(unit)
                        if j < len(extra) and extra[j]:
                            pieces.append(extra[j])
                    pieces += [p for p in extra[len(units):] if p]
                return pieces + [(negate, HG - 1, stage) for stage in range(5)] + [(turn_top, HG - 1)]

            def bring():
                for hp in range(0, HG, 2):
                    for e, r in ((0, rows), (1, NR)):
                        t = ready.done(nc.vector.tensor_copy((qT, kT)[e][0:r, hp:hp + 2, :], ahead[e][0:r, hp:hp + 2, :]))
                return t

            def group(g, more):
                valued, divided = pe.now(), dve.now()
                act.after(divided)
                pool.after(valued)
                v_ready = pool.own(nc.gpsimd.tensor_copy(
                    V[:, :, :, 0:DH], v_all[:, :, bass.ds(g * GW, GW)].rearrange("p i (h d) -> p i h d", d=DH)))
                act.after(valued)
                pe.after(ready.now(), act.now())
                side = first_pass((g + 2) % NG) if more else []
                pending = []
                acc, acc_free = bank(7), [act.now()]
                scores, prob = Ring(2, 2), Ring(4)
                steps = [(half, s) for half in range(2) for s in range(ns) if not causal or P * s < HALF * (half + 1)]

                def score(half, s, between):
                    end = HALF * (half + 1)
                    t0 = max(HALF * half, P * s) if causal else HALF * half
                    n, size, out = end - t0, keys[s], []
                    for hp in range(2):
                        slot = scores.take(pe)
                        at = scores.place(slot)
                        for a in range(2):
                            h = 2 * hp + a
                            masked = causal and t0 == P * s
                            ins = nc.tensor.matmul(bank(at + a)[0:size, 0:n], kT[0:rows, h, P * s:P * s + size],
                                                   qT[0:rows, h, t0:end], start=True, stop=not masked,
                                                   skip_group_check=True)
                            if masked:
                                w = min(P, n)
                                ins = nc.tensor.matmul(bank(at + a)[0:size, 0:w], tri_bf[:, 0:size], ident_bf[:, 0:w],
                                                       start=False, stop=True, skip_group_check=True)
                        t = pe.done(ins)
                        ps = prob.take(act)
                        act.after(t)
                        t = act.done(nc.scalar.activation(probs[0:size, ps, :, 0:n], banks(at, 2)[0:size, :, 0:n],
                                                          ACT.Exp, scale=DH ** -0.5))
                        scores.release(slot, t)
                        out.append((ps, t))
                        between()
                    return t0 - HALF * half, n, size, out

                def values(half, s, t0, n, size, out):
                    last = steps[-1] == (half, s) or steps[steps.index((half, s)) + 1][0] != half
                    pe.after(*(t for _, t in out), v_ready)
                    if s == 0:
                        pe.after(acc_free[0])
                    for h in range(HG):
                        ps = out[h // 2][0]
                        ins = nc.tensor.matmul(acc[HP * h:HP * (h + 1), t0:t0 + n], V[0:size, s, h, :],
                                               probs[0:size, ps, h % 2, 0:n], start=(s == 0), stop=last,
                                               skip_group_check=True)
                    t = pe.done(ins)
                    for ps, _ in out:
                        prob.release(ps, t)
                    if last:
                        act.after(t)
                        acc_free[0] = t = act.done(nc.scalar.copy(kept[:, half], acc))
                        sums = low_turned.rearrange("p (n c) -> p n c", c=32)[:, :, DH]
                        inverse = small[:, 192:192 + HALF // 32]
                        dst = oT[:, bass.ds(g, 1), HALF * half:HALF * (half + 1)].rearrange("p a t -> p (a t)")
                        stages = [(nc.vector.transpose, low_turned, kept[:, half]), (nc.vector.reciprocal, inverse, sums),
                                  (nc.vector.transpose, low.rearrange("p (n c) -> p n c", c=32), spread(inverse, 2, 32)),
                                  (nc.vector.tensor_tensor, dst, kept[:, half], low, ALU.mult)]

                        def run(stage, t=t, stages=stages):
                            op, *args = stages[stage]
                            dve.after(t, dve.now())
                            dve.done(op(*args))

                        pending.extend((run, k) for k in range(4))

                places = 4 * len(steps) - 3
                run = [0, 0]

                def some_side():
                    run[0] += 1
                    upto = min(len(side), -(-len(side) * run[0] // places))
                    for piece, *args in side[run[1]:upto]:
                        piece(*args)
                    run[1] = upto
                    if pending:
                        piece, arg = pending.pop(0)
                        piece(arg)

                waiting = score(*steps[0], lambda: None)
                for j, step in enumerate(steps):
                    if j + 1 < len(steps):
                        following = score(*steps[j + 1], some_side)
                    some_side()
                    if j == len(steps) - 1:
                        assert run[1] == len(side)
                        scored = pe.now()
                        values(*step, *waiting)
                        if more:
                            dve.after(scored, act.now())
                            bring()
                    else:
                        values(*step, *waiting)
                        some_side()
                    waiting = following
                for piece, arg in pending:
                    piece(arg)

            for e in (1, 0):
                for run in split(e, 0, by=dve):
                    run()
            for piece, *args in first_pass(1, dve.now()):
                piece(*args)
            dve.after(act.now())
            bring()
            pe.after(pool.now())
            with c.loop(NG - 1) as g:
                group(g, True)
            group(NG - 1, False)
            phase()

        def out_project(oT, w, bias):
            ring = Ring(8)
            for i in range(NT):
                slot = ring.take(pe)
                for g in range(NG):
                    ins = nc.tensor.matmul(bank(slot)[:, 0:D], oT[:, g, P * i:P * (i + 1)], w[:, g, :],
                                           start=(g == 0), stop=(g == NG - 1))
                dve.after(pe.done(ins))
                dve.own(nc.vector.tensor_tensor(x[:, i, :], x[:, i, :], bank(slot)[:, 0:D], ALU.add))
                t = dve.done(nc.vector.tensor_tensor(x[:, i, :], x[:, i, :], bias[:, :], ALU.add))
                ring.release(slot, t)
            phase()

        def geometry():
            lines = area.take(NT, 2 * 2 * 4 * H)
            for i in range(NT):
                for k in range(KD):
                    nc.tensor.matmul(bank(i)[:, 0:64], xT[:, k, P * i:P * (i + 1)], resident["geo"][:, k, 0:64],
                                     start=(k == 0), stop=(k == KD - 1))
                for k in range(KD):
                    ins = nc.tensor.matmul(bank(i)[:, 64:256], x_tile(i, k), resident["geo"][:, k, 64:256],
                                           start=(k == 0), stop=(k == KD - 1))
                t = pe.done(ins)
                act.after(t)
                copied = act.done(nc.scalar.copy(lines[:, i, :], bank(i)[:, 0:256]))
            dve.after(copied)
            pts = lines.rearrange("p i (w r) -> p (i w) r", w=2).rearrange("p n (two c h) -> p n two c h", two=2, c=4)
            one, two = pts[:, :, 0], pts[:, :, 1]
            L, N, LN = (area.take(2 * NT, 6, H) for _ in range(3))
            for i, (k0, n) in enumerate(((0, 3), (3, 2), (5, 1))):
                dve.done(nc.vector.tensor_tensor(L[:, :, k0:k0 + n, :], spread(one[:, :, i, :], 2, n),
                                                 two[:, :, i + 1:4, :], ALU.mult))
                t = dve.done(nc.vector.tensor_tensor(N[:, :, k0:k0 + n, :], one[:, :, i + 1:4, :],
                                                     spread(two[:, :, i, :], 2, n), ALU.mult))
            dve.after(t)
            flat = lambda v: v.rearrange("p a b c -> p (a b c)")
            dve.own(nc.vector.tensor_tensor(flat(L), flat(L), flat(N), ALU.subtract))
            dve.own(nc.vector.tensor_tensor(flat(N), flat(L), flat(L), ALU.mult))
            n2, s0, s1, rn = (area.take(2 * NT * H) for _ in range(4))
            dve.own(nc.vector.tensor_reduce(n2.rearrange("p (a h) -> p a h", h=H), N.rearrange("p a k h -> p a h k"),
                                            AX.X, ALU.add))
            act.after(dve.now())
            dve.after(act.done(nc.scalar.activation(s0, n2, ACT.Sqrt)))
            dve.own(nc.vector.tensor_scalar(s0, s0, 1e-18, None, ALU.max))
            dve.own(nc.vector.reciprocal(s1, s0))
            dve.own(nc.vector.tensor_tensor(s1, s1, n2, ALU.mult))
            dve.own(nc.vector.tensor_tensor(s0, s0, s1, ALU.add))
            dve.own(nc.vector.tensor_scalar(s0, s0, 0.5, 1e-12, ALU.mult, ALU.max))
            dve.own(nc.vector.reciprocal(rn, s0))
            by = lambda v, w: v.rearrange("p (i w) k h -> p i w k h", w=2)[:, :, w]
            rnv = rn.rearrange("p (i w h) -> p i w h", w=2, h=H)
            for k in range(6):
                dve.done(nc.vector.tensor_tensor(by(LN, 0)[:, :, k, :], by(L, 0)[:, :, 5 - k, :], rnv[:, :, 0, :], ALU.mult))
                t = dve.done(nc.vector.scalar_tensor_tensor(out=by(LN, 1)[:, :, k, :], in0=by(L, 1)[:, :, k, :],
                                                            scalar=J_SIGN[k], in1=rnv[:, :, 1, :],
                                                            op0=ALU.mult, op1=ALU.mult))
            dve.after(t)
            prods = area.take(2 * NT, PAIRS, H)
            s = 0
            for p in range(6):
                n = 6 - p
                t = dve.done(nc.vector.tensor_tensor(prods[:, :, s:s + n, :], spread(LN[:, :, p, :], 2, n),
                                                     LN[:, :, p:6, :], ALU.mult))
                s += n
            pe.after(t)
            turned = area.take(2, 3, T)
            ring = Ring(4, 2)
            flat_prods = prods.rearrange("p a s h -> p a (s h)")
            got = {}
            for w in range(2):
                for q in range(3):
                    slot = ring.take(pe)
                    dst = banks(ring.place(slot), 2).rearrange("p a b -> p (a b)")
                    for i in range(NT):
                        ins = nc.tensor.transpose(dst[0:CR, P * i:P * (i + 1)],
                                                  flat_prods[:, 2 * i + w, q * CR:(q + 1) * CR], ident[:, :])
                    act.after(pe.done(ins))
                    got[w, q] = act.done(nc.scalar.copy(turned[0:CR, w, q, :], dst[0:CR, :]))
                    ring.release(slot, got[w, q])
            state = area.take(3, 1 + T)
            dve.done(nc.vector.memset(state[:, :, 0:1], 0.0))
            for q in range(3):
                dve.after(got[0, q])
                t = dve.done(nc.vector.tensor_tensor_scan(state[0:CR, q, 1:1 + T], widen(decay[0:CR, :], T),
                                                          turned[0:CR, 0, q, :], 0.0, ALU.mult, ALU.add))
            dve.after(t, got[1, 2])
            read = turned[0:CR, 1]
            t = dve.done(nc.vector.tensor_tensor(read, read, state[0:CR, :, 0:T], ALU.mult))
            pe.after(t, act.now())
            for i in range(NT):
                for q in range(3):
                    ins = nc.tensor.matmul(bank(0)[:, H * i:H * (i + 1)], turned[0:CR, 1, q, P * i:P * (i + 1)],
                                           resident["pair_sum"][0:CR, q, :], start=(q == 0), stop=(q == 2))
            dve.after(pe.done(ins))
            t = dve.own(nc.vector.tensor_tensor(gate[:, :, :], bank(0)[:, 0:H * NT].rearrange("p (i h) -> p i h", h=H),
                                                spread(mem_decay[:, :], 1, NT), ALU.mult))
            act.after(t)
            dve.after(act.done(nc.scalar.activation(gate[:, :, :], gate[:, :, :], ACT.Sigmoid)))
            dve.done(nc.vector.tensor_scalar(gate[:, :, :], gate[:, :, :], resident["kv_gate"][:, 0:1], None, ALU.mult))
            phase()

        def column_to_rows(columns, dst):
            diag = area.take(NT, P)
            for i in range(NT):
                t = dve.done(nc.vector.tensor_scalar(diag[:, i, :], ident[:, :], columns[:, i:i + 1], None, ALU.mult))
            pe.after(t)
            for i in range(NT):
                ins = nc.tensor.matmul(banks(6, 2).rearrange("p a b -> p (a b)")[:, P * i:P * (i + 1)], ones[:, :],
                                       diag[:, i, :], start=True, stop=True)
            t = pe.done(ins)
            act.after(t)
            return act.done(nc.scalar.copy(dst, banks(6, 2).rearrange("p a b -> p (a b)")))

        def quantiser(top, inverse, scale, w_inverse):
            dve.own(nc.vector.tensor_scalar(top, top, 1e-5, None, ALU.max))
            dve.own(nc.vector.reciprocal(scale, top))
            dve.own(nc.vector.tensor_scalar(scale, scale, 127.0, None, ALU.mult))
            dve.own(nc.vector.tensor_scalar(inverse, top, 1.0 / 127.0, w_inverse, ALU.mult, ALU.mult))

        def bit_ffn():
            hid_flat = area.take(NH * (T + 2))
            hid = hid_flat.rearrange("p (m t) -> p m t", m=NH)
            conv = area.take(NH, T)
            whole = area.take(T)
            xqT = area.take(KD, T, dtype=BF16)
            xqb = hid_flat[:, 0:NT * D // 2].bitcast(BF16).rearrange("p (i d) -> p i d", i=NT)
            hq = hid_flat[:, 2 * (T + 2):2 * (T + 2) + NH * T // 2].bitcast(BF16).rearrange("p (m t) -> p m t", m=NH)
            top, inv, scale = (small[:, 400 + NT * j:400 + NT * (j + 1)] for j in range(3))
            t = layer_norm()[-1]
            dve.after(t)
            dve.own(nc.vector.tensor_reduce(top, xn[:, :, :], AX.X, ALU.max, apply_absolute_value=True))
            quantiser(top, inv, scale, wscale[:, 0:1])
            for i in range(NT):
                t = dve.done(nc.vector.tensor_scalar(xn[:, i, :], xn[:, i, :], scale[:, i:i + 1], ROUND, ALU.mult, ALU.add))
            dve.after(t)
            t = dve.done(nc.vector.tensor_scalar(xqb, xn[:, :, :], ROUND, None, ALU.subtract))
            pe.after(t)
            for k in range(KD):
                dst = bank(k).bitcast(BF16)
                for i in range(NT):
                    ins = nc.tensor.transpose(dst[:, P * i:P * (i + 1)], xqb[:, i, P * k:P * (k + 1)], ident_bf[:, :])
                act.after(pe.done(ins))
                turned = act.done(nc.scalar.copy(xqT[:, k, :], dst))
            spread_done = column_to_rows(inv, whole)
            dve.after(turned, spread_done)
            for col in (0, T + 1):
                dve.done(nc.vector.memset(hid[:, :, col:col + 1], 0.0))
            ring = Ring(6)
            pe.after(turned)
            filled = []
            for m in range(NH):
                for half in range(2):
                    slot = ring.take(pe)
                    for k in range(KD):
                        ins = nc.tensor.matmul(bank(slot), w1q[:, k, P * m:P * (m + 1)],
                                               xqT[:, k, HALF * half:HALF * (half + 1)], start=(k == 0), stop=(k == KD - 1))
                    dve.after(pe.done(ins))
                    t = dve.done(nc.vector.tensor_tensor(hid[:, m, 1 + HALF * half:1 + HALF * (half + 1)], bank(slot),
                                                         whole[:, HALF * half:HALF * (half + 1)], ALU.mult))
                    ring.release(slot, t)
                act.after(t)
                w = resident["conv_w"]
                mid = act.done(nc.scalar.activation(conv[:, m, :], hid[:, m, 1:1 + T], ACT.Identity,
                                                    bias=resident["conv_b"][:, m:m + 1], scale=w[:, m, 1:2]))
                dve.after(mid)
                dve.own(nc.vector.scalar_tensor_tensor(out=conv[:, m, :], in0=hid[:, m, 0:T], scalar=w[:, m, 0:1],
                                                       in1=conv[:, m, :], op0=ALU.mult, op1=ALU.add))
                t = dve.own(nc.vector.scalar_tensor_tensor(out=conv[:, m, :], in0=hid[:, m, 2:2 + T], scalar=w[:, m, 2:3],
                                                           in1=conv[:, m, :], op0=ALU.mult, op1=ALU.add))
                act.after(t)
                act.own(nc.scalar.activation(conv[:, m, :], conv[:, m, :], ACT.Silu))
                filled.append(act.done(nc.scalar.activation(hid[:, m, 0:T], conv[:, m, :], ACT.Abs)))
            hi = hid[:, 0, 0:T]
            for m in range(1, NH):
                dve.after(filled[m])
                t = dve.own(nc.vector.tensor_tensor(hi, hi, hid[:, m, 0:T], ALU.max))
            pe.after(t)
            for i in range(NT):
                ins = nc.tensor.transpose(banks(0, 2).rearrange("p a b -> p (a b)")[:, P * i:P * (i + 1)],
                                          hi[:, P * i:P * (i + 1)], ident[:, :])
            dve.after(pe.done(ins))
            dve.own(nc.vector.tensor_reduce(top, banks(0, 2).rearrange("p a b -> p (a b)")
                                            .rearrange("p (i b) -> p i b", i=NT), AX.X, ALU.max))
            quantiser(top, inv, scale, wscale[:, 1:2])
            t = column_to_rows(scale, whole)
            dve.after(t)
            done = []
            for m in range(NH):
                dve.own(nc.vector.tensor_tensor(conv[:, m, :], conv[:, m, :], whole, ALU.mult))
                done.append(dve.done(nc.vector.tensor_scalar(hq[:, m, :], conv[:, m, :],
                                                             ROUND, ROUND, ALU.add, ALU.subtract)))
            pe.after(done[-1])
            for i in range(NT):
                for m in range(NH):
                    ins = nc.tensor.matmul(bank(i)[:, 0:D], hq[:, m, P * i:P * (i + 1)], w2q[:, m, :],
                                           start=(m == 0), stop=(m == NH - 1))
                dve.after(pe.done(ins))
                dve.done(nc.vector.scalar_tensor_tensor(out=x[:, i, :], in0=bank(i)[:, 0:D], scalar=inv[:, i:i + 1],
                                                        in1=x[:, i, :], op0=ALU.mult, op1=ALU.add))
            phase()

        def wide_attention():
            qT, kT = area.take(KD, T), area.take(KD, S)
            v = area.take(2, D)
            ring = Ring(8)
            for m in range(KD):
                for half in range(2):
                    slot = ring.take(pe)
                    for k in range(KD):
                        ins = nc.tensor.matmul(bank(slot), resident["wide_q"][:, k, P * m:P * (m + 1)],
                                               xT[:, k, 1 + HALF * half:1 + HALF * (half + 1)],
                                               start=(k == 0), stop=(k == KD - 1))
                    act.after(pe.done(ins))
                    t = act.done(nc.scalar.activation(qT[:, m, HALF * half:HALF * (half + 1)], bank(slot), ACT.Identity,
                                                      bias=resident["wide_qb"][:, m:m + 1]))
                    ring.release(slot, t)
                slot = ring.take(pe)
                for k in range(KD):
                    ins = nc.tensor.matmul(bank(slot)[:, 0:S], resident["wide_k"][:, k, P * m:P * (m + 1)], ctxT[:, k, :],
                                           start=(k == 0), stop=(k == KD - 1))
                act.after(pe.done(ins))
                t = act.done(nc.scalar.activation(kT[:, m, :], bank(slot)[:, 0:S], ACT.Identity,
                                                  bias=resident["wide_kb"][:, m:m + 1]))
                ring.release(slot, t)
            for i, n in enumerate(CTX):
                slot = ring.take(pe)
                t = project(bank(slot)[0:n, 0:D], lambda k: ctx_tile(i, k), n, resident["wide_v"])
                add_bias(v[0:n, i, :], bank(slot)[0:n, 0:D], resident["wide_vb"][0:n, :], t, ring, slot)
            pe.after(act.now(), dve.now())
            E = area.take(2, S)
            ET = area.take(2, 2, P)
            top, rsum = small[:, 400:408], small[:, 408:416]
            scale = D ** -0.5
            taken = [None, None]
            for i in range(NT):
                e = i % 2
                s_bank, t_bank, o_bank = bank(e), bank(2 + e), bank(4 + e)
                pe.after(taken[e])
                for k in range(KD):
                    ins = nc.tensor.matmul(s_bank[:, 0:S], qT[:, k, P * i:P * (i + 1)], kT[:, k, :],
                                           start=(k == 0), stop=(k == KD - 1))
                dve.after(pe.done(ins))
                dve.own(nc.vector.tensor_reduce(top[:, i:i + 1], s_bank[:, 0:S], AX.X, ALU.max))
                t = dve.own(nc.vector.tensor_scalar(top[:, i:i + 1], top[:, i:i + 1], -scale, None, ALU.mult))
                act.after(t)
                t = act.done(nc.scalar.activation(E[:, e, :], s_bank[:, 0:S], ACT.Exp, bias=top[:, i:i + 1],
                                                  scale=scale, accum_out=rsum[:, i:i + 1]))
                pe.after(t)
                nc.tensor.transpose(t_bank[:, 0:P], E[:, e, 0:P], ident[:, :])
                ins = nc.tensor.transpose(t_bank[0:CTX[1], P:2 * P], E[:, e, P:S], ident[:, :])
                act.after(pe.done(ins))
                act.done(nc.scalar.copy(ET[:, e, 0, :], t_bank[:, 0:P]))
                t = act.done(nc.scalar.copy(ET[0:CTX[1], e, 1, :], t_bank[0:CTX[1], P:2 * P]))
                pe.after(t)
                for j, n in enumerate(CTX):
                    ins = nc.tensor.matmul(o_bank[:, 0:D], ET[0:n, e, j, :], v[0:n, j, :], start=(j == 0), stop=(j == 1))
                dve.after(pe.done(ins))
                dve.own(nc.vector.reciprocal(rsum[:, i:i + 1], rsum[:, i:i + 1]))
                taken[e] = dve.done(nc.vector.scalar_tensor_tensor(out=x[:, i, :], in0=o_bank[:, 0:D], scalar=rsum[:, i:i + 1],
                                                                   in1=x[:, i, :], op0=ALU.mult, op1=ALU.add))
            phase()

        def experts(b):
            logits, onehot, comb = area.take(NT, NE), area.take(NT, NE), area.take(NT, NE)
            best = area.take(NT, 8)
            index = area.take(NT, 8).bitcast(U32)
            p = area.take(4, NT)
            combT = area.take(T)
            sets = [[area.take(KD, ED), area.take(KD, ED), area.take(D), area.take(T)] for _ in range(2)]
            act_buf, hid = area.take(2, HALF), area.take(2, HALF)
            for i in range(NT):
                for k in range(KD):
                    ins = nc.tensor.matmul(bank(0)[:, NE * i:NE * (i + 1)], x_tile(i, k), resident["router"][:, k, :],
                                           start=(k == 0), stop=(k == KD - 1))
            dve.after(pe.done(ins))
            dve.own(nc.vector.tensor_tensor(logits, bank(0)[:, 0:NT * NE].rearrange("p (i e) -> p i e", e=NE),
                                            spread(resident["router_b"][:, :], 1, NT), ALU.add))
            for i in range(NT):
                t = dve.done(nc.vector.max(best[:, i, :], logits[:, i, :]))
            dve.after(t)
            for i in range(NT):
                t = dve.done(nc.vector.max_index(index[:, i, :], best[:, i, :], logits[:, i, :]))
            dve.after(t)
            t = dve.own(nc.vector.tensor_tensor(p[:, 0, :], best[:, :, 1], best[:, :, 0], ALU.subtract))
            act.after(t)
            dve.after(act.done(nc.scalar.activation(p[:, 1, :], p[:, 0, :], ACT.Exp)))
            dve.own(nc.vector.tensor_scalar(p[:, 0, :], p[:, 1, :], 1.0, None, ALU.add))
            dve.own(nc.vector.reciprocal(p[:, 2, :], p[:, 0, :]))
            dve.own(nc.vector.tensor_tensor(p[:, 3, :], p[:, 1, :], p[:, 2, :], ALU.mult))
            chosen = area.take(2, NT)
            dve.own(nc.vector.tensor_copy(chosen, index[:, :, 0:2].rearrange("p i two -> p two i")))
            for i in range(NT):
                for j, o in ((0, comb), (1, onehot)):
                    t = dve.done(nc.vector.tensor_scalar(o[:, i, :], resident["iota"][:, :], chosen[:, j, i:i + 1],
                                                         p[:, 2 + j, i:i + 1], ALU.is_equal, ALU.mult))
            dve.after(t)
            t = dve.own(nc.vector.tensor_tensor(comb, comb, onehot, ALU.add))
            pe.after(t)
            for i in range(NT):
                ins = nc.tensor.transpose(banks(2, 2).rearrange("p a b -> p (a b)")[0:NE, P * i:P * (i + 1)],
                                          comb[:, i, :], ident[:, :])
            act.after(pe.done(ins))
            t = act.done(nc.scalar.copy(combT[0:NE, :], banks(2, 2).rearrange("p a b -> p (a b)")[0:NE, :]))
            sp_after(t)
            stored = load(io["combine"], combT[0:NE, :], sem_comb)
            sp_after(stored)

            out = banks(4, 4).rearrange("p k (two d) -> p (k two) d", two=2)
            pair = Ring(2, 2)
            turn = [0]

            def expert(wg, wu, wd, weight, ready, first=False, last=False):
                made = []
                for half in range(2):
                    slot = pair.take(pe)
                    at = pair.place(slot)
                    pe.after(ready)
                    for j, w in ((0, wg), (1, wu)):
                        for k in range(KD):
                            ins = nc.tensor.matmul(bank(at + j), w[:, k, :], xT[:, k, 1 + HALF * half:1 + HALF * (half + 1)],
                                                   start=(k == 0), stop=(k == KD - 1))
                    t = pe.done(ins)
                    act.after(t, hid_free[half])
                    t = act.done(nc.scalar.activation(act_buf[:, half, :], bank(at), ACT.Silu))
                    dve.after(t)
                    t = dve.own(nc.vector.tensor_tensor(hid[:, half, :], act_buf[:, half, :], bank(at + 1), ALU.mult))
                    pair.release(slot, t)
                    if weight is not None:
                        dve.after(ready)
                        t = dve.done(nc.vector.tensor_tensor(hid[:, half, :], hid[:, half, :],
                                                             weight[:, HALF * half:HALF * (half + 1)], ALU.mult))
                    made.append(t)
                for half in range(2):
                    pe.after(made[half])
                    for i in range(4):
                        tile = 4 * half + i
                        ins = nc.tensor.matmul(out[:, tile, :], hid[:, half, P * i:P * (i + 1)], wd,
                                               start=(first and tile % 2 == 0), stop=last, skip_group_check=True)
                    hid_free[half] = pe.done(ins)
                return hid_free[1]

            hid_free = [None, None]
            shared = [(resident["sh_gate"][:, :, ED * j:ED * (j + 1)], resident["sh_up"][:, :, ED * j:ED * (j + 1)],
                       resident["sh_down"][:, j, :]) for j in range(2)]
            pe.after(act.now(), dve.now())
            expert(*shared[0], None, None, first=True)
            pe_before = pe.now()
            with c.loop(NE // 2) as j:
                loaded = []
                hid_free[:] = [pe.now(), pe.now()]
                pair.free = [dve.now(), dve.now()]
                for odd in range(2):
                    sp_after(pe.now())
                    s = sem_expert[odd]
                    e = j * 2 + odd
                    wg, wu, wd, wt = sets[odd]
                    load(wg, io["w_gate"][bass.ds(e, 1)].rearrange("a k p e -> p (a k) e"), s)
                    load(wu, io["w_up"][bass.ds(e, 1)].rearrange("a k p e -> p (a k) e"), s)
                    load(wd, io["w_down"][bass.ds(e, 1)].rearrange("a p d -> p (a d)"), s)
                    loaded.append(load(wt, io["combine"][bass.ds(e, 1), :].broadcast_to([P, T]), s))
                for odd in range(2):
                    wg, wu, wd, wt = sets[odd]
                    expert(wg, wu, wd, wt, loaded[odd])
            pair.free = [dve.now(), dve.now()]
            hid_free[:] = [pe.now(), pe.now()]
            done = expert(*shared[1], None, None, last=True)
            dve.after(done)
            for i in range(NT):
                t = dve.done(nc.vector.tensor_tensor(x[:, i, :], x[:, i, :], out[:, i, :], ALU.add))
            sp_after(t)
            load(io["out"][bass.ds(b, 1)].rearrange("b (i p) d -> p (b i) d", p=P), x[:, :, :], sem_out)
            sp_after(c.add(sem_out, 0))
            phase()

        with c.fresh_loop(B, owned) as b:
            area.reset()
            ctx_rows = area.take(2, D)
            load(x[:, :, :], io["x"][bass.ds(b, 1)].rearrange("b (i p) d -> p (b i) d", p=P), sem_x)
            for i, n in enumerate(CTX):
                t = load(ctx_rows[0:n, i:i + 1, :], io["ctx"][bass.ds(b, 1), P * i:P * i + n, :].rearrange("b p d -> p b d"), sem_x)
            pe.after(t)
            for k in range(KD):
                for i, n in enumerate(CTX):
                    ins = nc.tensor.transpose(bank(7)[:, k * 256 + P * i:k * 256 + P * i + n],
                                              ctx_rows[0:n, i, P * k:P * (k + 1)], ident[0:n, 0:n])
            act.after(pe.done(ins))
            act.done(nc.scalar.copy(ctxT[:, :, :], bank(7).rearrange("p (k s) -> p k s", k=KD)[:, :, 0:S]))
            dve.after(t)

            norm_phase()
            geometry()
            qkv = area.take(NT, 3 * D)
            oT = area.take(NG, T)
            mark = area.at
            ring = Ring(8)
            fresh = area.take(2, 2 * D)
            for i in range(NT):
                tile = lambda k: x_tile(i, k)
                sq, sk, sg = ring.take(pe), None, None
                t = project(bank(sq)[:, 0:D], tile, P, resident["qkv"][:, :, 0:D])
                add_bias(qkv[:, i, 0:D], bank(sq)[:, 0:D], resident["qkv_b"][:, 0:D], t, ring, sq)
                sk = ring.take(pe)
                t = project(bank(sk), tile, P, resident["qkv"][:, :, D:3 * D])
                t = add_bias(qkv[:, i, D:3 * D], bank(sk), resident["qkv_b"][:, D:3 * D], t, ring, sk)
                sg = ring.take(pe)
                g = project(bank(sg), tile, P, resident["kv_geo"])
                dve.after(g)
                v4 = lambda v: v.rearrange("p (a h d) -> p a h d", a=2, h=H)
                for a in range(2):
                    g = dve.own(nc.vector.tensor_tensor(
                        fresh[:, a, 0:D].rearrange("p (h d) -> p h d", h=H),
                        bank(sg)[:, a * D:(a + 1) * D].rearrange("p (h d) -> p h d", h=H),
                        spread(gate[:, i, :], 2, DH), ALU.mult))
                ring.release(sg, g)
                dve.own(nc.vector.tensor_tensor(qkv[:, i, D:3 * D].rearrange("p (a d) -> p a d", a=2),
                                                qkv[:, i, D:3 * D].rearrange("p (a d) -> p a d", a=2),
                                                fresh[:, :, 0:D], ALU.add))
            nc.all_engine_barrier()
            area.at = mark
            attention(qkv[:, :, 0:D], qkv[:, :, D:2 * D], qkv[:, :, 2 * D:3 * D], FULL, True, oT)
            out_project(oT, resident["out0"], resident["out0_b"])

            norm_phase()
            oT = area.take(NG, T)
            q = area.take(NT, D)
            kv = area.take(2, 2 * D)
            mark = area.at
            ring = Ring(8)
            kraw, qraw, t1, t2 = area.take(2, D), area.take(NT, D), area.take(NT * H, 8), area.take(NT * H, 8)
            for i in range(NT):
                slot = ring.take(pe)
                t = project(bank(slot)[:, 0:D], lambda k: x_tile(i, k), P, resident["cross_q"])
                add_bias(qraw[:, i, :], bank(slot)[:, 0:D], resident["cross_qb"][:, :], t, ring, slot)
            for i, n in enumerate(CTX):
                slot = ring.take(pe)
                t = project(bank(slot)[0:n, :], lambda k: ctx_tile(i, k), n, resident["cross_kv"])
                add_bias(kraw[0:n, i, :], bank(slot)[0:n, 0:D], resident["cross_kvb"][0:n, 0:D], t, ring, slot)
                dve.after(add_bias(kv[0:n, i, D:2 * D], bank(slot)[0:n, D:2 * D], resident["cross_kvb"][0:n, D:2 * D], t, ring, slot))

            def rotate(dst, src, i, n):
                even = lambda v, o: v.rearrange("p (h f two) -> p two h f", f=8, two=2)[:, o]
                xe, xo = even(src[0:n, i, :], 0), even(src[0:n, i, :], 1)
                cos = spread(resident["cos"][0:n, i, :], 1, H)
                sin = spread(resident["sin"][0:n, i, :], 1, H)
                a1, a2 = t1[0:n, 0:H, :], t2[0:n, 0:H, :]
                for o, (u, v, op) in enumerate(((cos, sin, ALU.subtract), (sin, cos, ALU.add))):
                    dve.done(nc.vector.tensor_tensor(a1, xe, u, ALU.mult))
                    dve.own(nc.vector.tensor_tensor(a2, xo, v, ALU.mult))
                    dve.own(nc.vector.tensor_tensor(even(dst, o), a1, a2, op))

            for i in range(NT):
                rotate(q[:, i, :], qraw, i, P)
            for i, n in enumerate(CTX):
                rotate(kv[0:n, i, 0:D], kraw, i, n)
            nc.all_engine_barrier()
            area.at = mark
            attention(q, kv[:, :, 0:D], kv[:, :, D:2 * D], CTX, True, oT)
            out_project(oT, resident["cross_o"], resident["cross_ob"])

            bit_ffn()

            norm_phase()
            qkv = area.take(NT, 3 * D)
            oT = area.take(NG, T)
            mark = area.at
            ring = Ring(8)
            for i in range(NT):
                for a, w in ((0, D), (D, 2 * D)):
                    slot = ring.take(pe)
                    t = project(bank(slot)[:, 0:w], lambda k: x_tile(i, k), P, resident["qkv1"][:, :, a:a + w])
                    add_bias(qkv[:, i, a:a + w], bank(slot)[:, 0:w], resident["qkv1_b"][:, a:a + w], t, ring, slot)
            nc.all_engine_barrier()
            area.at = mark
            attention(qkv[:, :, 0:D], qkv[:, :, D:2 * D], qkv[:, :, 2 * D:3 * D], FULL, False, oT)
            out_project(oT, resident["out1"], resident["out1_b"])

            norm_phase()
            wide_attention()
            norm_phase()
            experts(b)


def tiles(w):
    return np.ascontiguousarray(w.reshape(w.shape[0] // P, P, -1).transpose(1, 0, 2))


def rows(v, n=P):
    return np.ascontiguousarray(np.tile(v.reshape(1, -1), (n, 1)))


def head_rows(w):
    n = w.shape[1]
    out = np.zeros((HG, HP, NG, n), np.float32)
    out[:, :DH] = w.reshape(NG, HG, DH, n).transpose(1, 2, 0, 3)
    return out.reshape(P, NG, n)


def constants():
    f = 1.0 / 10000.0 ** (np.arange(0, DH, 2, dtype=np.float32) / DH)
    angle = np.outer(np.arange(T, dtype=np.float32), f)
    pair_sum = np.zeros((P, 3, H), np.float32)
    slot = 0
    for p in range(6):
        for q in range(p, 6):
            for h in range(H):
                pair_sum[(slot % 7) * H + h, slot // 7, h] = 1.0 if p == q else 2.0
            slot += 1
    tri = np.where(np.arange(P)[None, :] <= np.arange(P)[:, None], 0.0, NEG).astype(np.float32)
    return {"ident": np.eye(P, dtype=np.float32), "tri": tri, "pair_sum": pair_sum,
            "iota": rows(np.arange(NE, dtype=np.float32)),
            "cos": tiles(np.cos(angle)), "sin": tiles(np.sin(angle))}


def kernel(**i):
    import concourse.bacc as bacc
    from concourse.bass_utils import run_bass_kernel_spmd

    i = {k: np.asarray(v) for k, v in i.items()}
    L0, X0, F0, L1, X1, E1 = ("L0_attn_", "L0_xattn_", "L0_ffn_", "L1_attn_", "L1_xattn_", "L1_ffn_")
    points = lambda w: w.reshape(D, H, 4).transpose(0, 2, 1).reshape(D, 4 * H)
    scalar = lambda v: rows(v.reshape(1, 1))
    logit = i[L0 + "decay_logits"]
    resident = {
        **constants(),
        "geo": tiles(np.concatenate([points(i[L0 + n]) for n in ("w1_write", "w2_write", "w1_read", "w2_read")], 1)),
        "qkv": tiles(i[L0 + "qkv_w"]), "qkv_b": rows(i[L0 + "qkv_b"]), "kv_geo": tiles(i[L0 + "kv_geo_w"]),
        "out0": head_rows(i[L0 + "out_w"]), "out0_b": rows(i[L0 + "out_b"]),
        "kv_gate": scalar(i[L0 + "kv_gate"]), "mem_scale": rows(i[L0 + "mem_scale"]), "logits": rows(logit),
        "logit_rows": np.ascontiguousarray(np.tile(logit, P // H).reshape(P, 1)),
        "cross_q": tiles(i[X0 + "Wq"]), "cross_qb": rows(i[X0 + "bq"]),
        "cross_kv": tiles(np.concatenate([i[X0 + "Wk"], i[X0 + "Wv"]], 1)),
        "cross_kvb": rows(np.concatenate([i[X0 + "bk"], i[X0 + "bv"]])),
        "cross_o": head_rows(i[X0 + "Wo"]), "cross_ob": rows(i[X0 + "bo"]),
        "conv_w": tiles(i[F0 + "conv_w"].reshape(HID, 3)), "conv_b": tiles(i[F0 + "conv_b"].reshape(HID, 1)).reshape(P, NH),
        "qkv1": tiles(i[L1 + "w_in"].T), "qkv1_b": rows(i[L1 + "b_in"]),
        "out1": head_rows(i[L1 + "w_out"].T), "out1_b": rows(i[L1 + "b_out"]),
        "wide_q": tiles(i[X1 + "Wq"].T), "wide_k": tiles(i[X1 + "Wk"].T), "wide_v": tiles(i[X1 + "Wv"].T),
        "wide_qb": tiles(i[X1 + "bq"].reshape(D, 1)).reshape(P, KD),
        "wide_kb": tiles(i[X1 + "bk"].reshape(D, 1)).reshape(P, KD), "wide_vb": rows(i[X1 + "bv"]),
        "router": tiles(i[E1 + "router_w"].T), "router_b": rows(i[E1 + "router_bias"]),
        "sh_gate": tiles(i[E1 + "sh_gate"].T), "sh_up": tiles(i[E1 + "sh_up"].T), "sh_down": tiles(i[E1 + "sh_down"].T),
    }
    arrays = {"r_" + k: v for k, v in resident.items()}
    arrays.update({
        "x": i["x"], "ctx": i["ctx_1024"], "w1T": tiles(i[F0 + "w1"].T), "w2T": tiles(i[F0 + "w2"].T),
        "w_gate": i[E1 + "gate_proj"].reshape(NE, KD, P, ED), "w_up": i[E1 + "up_proj"].reshape(NE, KD, P, ED),
        "w_down": i[E1 + "down_proj"],
    })
    arrays = {k: np.ascontiguousarray(v) for k, v in arrays.items()}

    def write(per_trip):
        nc = bacc.Bacc("TRN2", target_bir_lowering=False, num_devices=1)
        io = {k: nc.dram_tensor("in_" + k, v.shape, F32, kind="ExternalInput").ap() for k, v in arrays.items()}
        io["combine"] = nc.dram_tensor("combine", (NE, T), F32, kind="Internal").ap()
        io["out"] = nc.dram_tensor("out", (B, T, D), F32, kind="ExternalOutput").ap()
        build_program(nc, io, per_trip)
        return nc

    per_trip = {}
    write(per_trip)
    nc = write(per_trip)
    return run_bass_kernel_spmd(nc, [{"in_" + k: v for k, v in arrays.items()}], core_ids=[0]).results[0]["out"]
```

```python
import math
from contextlib import ExitStack, contextmanager
from itertools import zip_longest

import numpy as np

import concourse.bass as bass
import concourse.mybir as mybir

F32 = mybir.dt.float32
BF16 = mybir.dt.bfloat16
U32 = mybir.dt.uint32
F32R = mybir.dt.float32r
ALU = mybir.AluOpType
ACT = mybir.ActivationFunctionType
AX = mybir.AxisListType

P = 128
B, T, D, S = 4, 1024, 256, 154
NT = T // P
KD = D // P
H, DH = 16, 16
HG = 4
NG = H // HG
GW = HG * DH
HP = P // HG
HALF = 512
PARTS = 6
NR = PARTS * DH
SLACK = 4
NM = 3
HID = 1024
NH = HID // P
NE, ED = 16, 128
PAIRS = 21
CR = 7 * H
CTX = (128, S - 128)
FULL = (128,) * NT
ROUND = 12582912.0
LN_EPS = 1e-5
NEG = -1e30
J_SIGN = (1.0, -1.0, 1.0, 1.0, -1.0, 1.0)


class Token:

    def __init__(self, sem, count, loops):
        self.sem, self.count, self.loops = sem, count, loops


class Counts:

    def __init__(self, nc, per_trip):
        self.nc, self.per_trip = nc, per_trip
        self.count, self.loops, self.made, self.waited = {}, (), 0, {}

    def add(self, sem, n):
        self.count[sem] = self.count.get(sem, 0) + n
        return Token(sem, self.count[sem], self.loops)

    @contextmanager
    def loop(self, trips):
        number, self.made = self.made, self.made + 1
        before = dict(self.count)
        with self.nc.Fori(0, trips) as i:
            self.loops += ((i, number),)
            self.waited = {}
            yield i
            self.loops = self.loops[:-1]
        self.waited = {}
        each = {s: c - before.get(s, 0) for s, c in self.count.items() if c != before.get(s, 0)}
        each = {s.name: n for s, n in each.items()}
        self.per_trip[number] = each
        for s in self.count:
            self.count[s] = before.get(s, 0) + trips * each.get(s.name, 0)

    def wait(self, engine, who, token):
        assert self.loops[:len(token.loops)] == token.loops, "a token of a loop that has ended"
        key = (who, token.sem.name)
        if key in self.waited and self.waited[key] >= (len(token.loops), token.count):
            return
        self.waited[key] = (len(token.loops), token.count)
        value = token.count
        for i, number in token.loops:
            n = self.per_trip.get(number, {}).get(token.sem.name, 0)
            if n:
                value = i * n + value
        engine.wait_ge(token.sem, value)
        if value is not token.count:
            engine.sem_inc(self.carrier, 1)

    @contextmanager
    def fresh_loop(self, trips, engines):
        def restart():
            self.nc.all_engine_barrier()
            for e, sems in engines:
                for s in sems:
                    e.sem_clear(s)
            self.nc.all_engine_barrier()
            self.count, self.waited = {}, {}
            for e, sems in engines[:-1]:
                e.sem_inc(sems[0], 1)
                self.add(sems[0], 1)

        restart()
        with self.nc.Fori(0, trips) as i:
            yield i
            restart()


class Engine:

    def __init__(self, counts, engine, sem):
        self.counts, self.engine, self.sem = counts, engine, sem
        engine.sem_inc(sem, 1)
        counts.add(sem, 1)

    def after(self, *tokens):
        for t in tokens:
            if t is not None:
                self.counts.wait(self.engine, self.sem.name, t)

    def done(self, instruction):
        instruction.then_inc(self.sem, 1)
        return self.counts.add(self.sem, 1)

    def now(self):
        return self.counts.add(self.sem, 0)

    def back(self, n):
        t = self.now()
        return Token(t.sem, t.count - n, t.loops)

    def own(self, instruction):
        t = self.done(instruction)
        self.after(t)
        return t


class Ring:

    def __init__(self, n, width=1, first=0):
        self.n, self.width, self.first, self.at, self.free = n, width, first, 0, [None] * n

    def take(self, engine):
        slot = self.at % self.n
        self.at += 1
        if self.free[slot] is not None:
            engine.after(self.free[slot])
        self.free[slot] = None
        return slot

    def release(self, slot, token):
        self.free[slot] = token

    def place(self, slot):
        return self.first + slot * self.width


class Area:

    def __init__(self, whole, words):
        self.whole, self.words, self.at = whole, words, 0

    def reset(self):
        self.at = 0

    def take(self, *shape, dtype=F32):
        n = math.prod(shape)
        words = n if dtype == F32 else n // 2
        assert self.at + words <= self.words, (self.at + words, self.words)
        v = self.whole[:, self.at:self.at + words]
        self.at += words
        if dtype != F32:
            v = v.bitcast(dtype)
        if len(shape) == 1:
            return v
        names = "abcde"[:len(shape)]
        sizes = dict(zip(names[1:], shape[1:]))
        return v.rearrange(f"p ({' '.join(names)}) -> p {' '.join(names)}", **sizes)


def spread(ap, axis, n):
    v = ap.unsqueeze(axis)
    shape = list(v.shape)
    shape[axis] = n
    return v.broadcast_to(shape)


def widen(ap, n):
    shape = list(ap.shape)
    shape[-1] = n
    return ap.broadcast_to(shape)


def build_program(nc, io, per_trip):
    c = Counts(nc, per_trip)
    ctx = ExitStack()
    with ctx:
        sem = lambda name: ctx.enter_context(nc.semaphore(name))
        sb = lambda name, *shape, dtype=F32: ctx.enter_context(nc.sbuf_tensor(name, [P, *shape], dtype))
        pe = Engine(c, nc.tensor, sem("pe_done"))
        act = Engine(c, nc.scalar, sem("act_done"))
        dve = Engine(c, nc.vector, sem("dve_done"))
        pool = Engine(c, nc.gpsimd, sem("pool_done"))
        sem_const, sem_x, sem_row = sem("constants_loaded"), sem("x_loaded"), [sem("row_even_loaded"), sem("row_odd_loaded")]
        sem_expert = [sem("expert_even_loaded"), sem("expert_odd_loaded")]
        sem_comb, sem_out = sem("combine_stored"), sem("out_stored")
        sem_feed = sem("feed_forward_loaded")
        c.carrier = sem("register_waits")
        ready = Engine(c, nc.vector, sem("group_ready"))
        sp = nc.sync
        owned = [(e.engine, (e.sem,)) for e in (pe, act, dve, pool, ready)] + \
            [(sp, (sem_x, *sem_row, *sem_expert, sem_comb, sem_out))]

        def load(dst, src, s):
            sp.dma_start(dst, src).then_inc(s, 16)
            return c.add(s, 16)

        def sp_after(*tokens):
            for t in tokens:
                c.wait(sp, "sp", t)

        psum = ctx.enter_context(nc.psum_tensor("psum", [P, 8, HALF], F32))
        bank = lambda k: psum[:, k, :]
        banks = lambda k, n: psum[:, k:k + n, :]

        resident = {}
        for name, ap in io.items():
            if name.startswith("r_"):
                resident[name[2:]] = sb(name[2:], *ap.shape[1:])
        ident = resident["ident"]
        ident_bf = sb("ident_bf", P, dtype=BF16)
        tri_bf = sb("tri_bf", P, dtype=BF16)
        ones = sb("ones", P)
        w1q = sb("w1q", KD, HID, dtype=BF16)
        w2q = sb("w2q", NH, D, dtype=BF16)
        wscale = sb("wscale", 8)
        decay = sb("decay", 1)
        mem_decay = sb("mem_decay", H)
        x = sb("x", NT, D)
        xn = sb("xn", NT, D)
        xT = sb("xT", KD, 1 + T)
        ctxT = sb("ctxT", KD, S)
        gate = sb("gate", NT, H)
        small = sb("small", 512)
        words = (nc.sbuf_bytes_remaining - 256) // 4
        work_scope = ctx.enter_context(ExitStack())
        area = Area(work_scope.enter_context(nc.sbuf_tensor("work", [P, words], F32)), words)

        def phase():
            nc.all_engine_barrier()
            area.reset()

        ctx_rows = xT[:, :, 1:1 + D]

        def load_x(b, i0, i1):
            return load(x[:, i0:i1, :], io["x"][bass.ds(b, 1), P * i0:P * i1, :].rearrange("b (i p) d -> p (b i) d", p=P), sem_x)

        def load_context(b):
            for i, n in enumerate(CTX):
                t = load(ctx_rows[0:n, i:i + 1, :], io["ctx"][bass.ds(b, 1), P * i:P * i + n, :].rearrange("b p d -> p b d"), sem_x)
            return t

        w1f = area.take(KD, HID)
        w2f = area.take(NH, D)
        load(w1f, io["w1T"], sem_feed)
        feed_loaded = load(w2f, io["w2T"], sem_feed)
        for name, t in resident.items():
            last = load(t[tuple(slice(None) for _ in t.shape)], io["r_" + name], sem_const)
        load_x(0, 0, NT)
        first_loaded = load_context(0)
        dve.own(nc.vector.memset(ones[:, :], 1.0))
        dve.after(feed_loaded)
        dve.done(nc.vector.memset(xT[:, :, 0:1], 0.0))
        for k, (w, wq) in enumerate(((w1f, w1q), (w2f, w2q))):
            flat = w.rearrange("p a b -> p (a b)")
            out = wq[:, :, :].rearrange("p a b -> p (a b)")
            summed = dve.done(nc.vector.tensor_reduce(small[:, k:k + 1], flat, AX.X, ALU.add,
                                                      apply_absolute_value=True))
            pe.after(summed)
            total = pe.done(nc.tensor.matmul(bank(k)[:, 0:1], ones[:, :], small[:, k:k + 1],
                                             start=True, stop=True))
            dve.after(total)
            mean = wscale[:, k:k + 1]
            dve.own(nc.vector.tensor_scalar(mean, bank(k)[:, 0:1], 1.0 / (D * HID), 1e-5,
                                            ALU.mult, ALU.max))
            dve.own(nc.vector.reciprocal(small[:, 2 + k:3 + k], mean))
            dve.own(nc.vector.tensor_scalar(flat, flat, small[:, 2 + k:3 + k], ROUND, ALU.mult, ALU.add))
            dve.own(nc.vector.tensor_scalar(flat, flat, ROUND, -1.0, ALU.subtract, ALU.max))
            dve.own(nc.vector.tensor_scalar(out, flat, 1.0, None, ALU.min))
        dve.after(last)
        dve.done(nc.vector.tensor_copy(ident_bf[:, :], ident[:, :]))
        dve.done(nc.vector.tensor_copy(tri_bf[:, :], resident["tri"][:, :]))
        act.after(last)
        a = act.done(nc.scalar.activation(decay[0:CR, :], resident["logit_rows"][0:CR, :], ACT.Sigmoid))
        a = act.done(nc.scalar.activation(small[:, 16:32], resident["logits"][:, :], ACT.Sigmoid))
        dve.after(a)
        dve.own(nc.vector.tensor_tensor(mem_decay[:, :], small[:, 16:32], resident["mem_scale"][:, :], ALU.mult))

        def square_root(v, n, eps, at):
            s0, s1, s2 = (small[:, at + j * n:at + (j + 1) * n] for j in range(3))
            t = dve.own(nc.vector.tensor_scalar(s2, v, eps, None, ALU.add))
            act.after(t)
            t = act.done(nc.scalar.activation(s0, s2, ACT.Sqrt))
            dve.after(t)
            dve.own(nc.vector.tensor_scalar(s0, s0, 1e-18, None, ALU.max))
            dve.own(nc.vector.reciprocal(s1, s0))
            dve.own(nc.vector.tensor_tensor(s1, s1, s2, ALU.mult))
            dve.own(nc.vector.tensor_tensor(s0, s0, s1, ALU.add))
            dve.own(nc.vector.tensor_scalar(s0, s0, 0.5, None, ALU.mult))
            return s0

        stats, mv, rstd = small[:, 128:128 + 6 * NT], small[:, 192:192 + 2 * NT], small[:, 320:320 + NT]
        normed, turned_x = [None] * NT, [None] * (NT // 2)

        def completed(i):
            dve.after(dve.now())
            t = dve.done(nc.vector.bn_stats(stats[:, 6 * i:6 * i + 6], x[:, i, :]))
            n = NT // 2
            if (i + 1) % n:
                return
            i0 = i + 1 - n
            dve.after(t)
            for j in range(i0, i0 + n):
                t = dve.done(nc.vector.bn_aggr(mv[:, 2 * j:2 * j + 2], stats[:, 6 * j:6 * j + 6]))
            dve.after(t)
            variance = mv[:, 2 * i0:2 * (i0 + n)].rearrange("p (i two) -> p two i", two=2)[:, 1, :]
            root = square_root(variance, n, LN_EPS, 256 + 3 * i0)
            dve.own(nc.vector.reciprocal(rstd[:, i0:i0 + n], root))
            for j in range(i0, i0 + n):
                normed[j] = dve.done(nc.vector.tensor_scalar(xn[:, j, :], x[:, j, :], mv[:, 2 * j:2 * j + 1],
                                                             rstd[:, j:j + 1], ALU.subtract, ALU.mult))

        def turn_xn(j):
            pe.after(normed[2 * j + 1])
            for a in range(2):
                for k in range(KD):
                    ins = nc.tensor.transpose(bank(j)[:, (2 * a + k) * P:(2 * a + k + 1) * P],
                                              xn[:, 2 * j + a, k * P:(k + 1) * P], ident[:, :])
            act.after(pe.done(ins))
            dst = xT[:, :, 1 + 2 * P * j:1 + 2 * P * (j + 1)].rearrange("p k (a c) -> p a k c", a=2)
            turned_x[j] = act.done(nc.scalar.copy(dst, bank(j).rearrange("p (a k c) -> p a k c", a=2, k=KD)))

        def turn_all():
            for j in range(NT // 2):
                turn_xn(j)
            area.reset()

        def ring_after_turns(n):
            ring = Ring(n)
            ring.free[0:NT // 2] = turned_x
            return ring

        def x_tile(i, k):
            pe.after(turned_x[i // 2])
            return xT[:, k, 1 + P * i:1 + P * (i + 1)]

        def ctx_tile(i, k):
            return ctxT[:, k, P * i:P * i + CTX[i]]

        def project(out, tile, rows, w, ready=None):
            for k in range(KD):
                ins = nc.tensor.matmul(out, tile(k), w[:, k, :], start=(k == 0), stop=(k == KD - 1))
            return pe.done(ins)

        def add_bias(dst, src, bias, token, ring, slot):
            dve.after(token)
            t = dve.done(nc.vector.tensor_tensor(dst, src, bias, ALU.add))
            ring.release(slot, t)
            return t

        def attention(q_all, k_all, v_all, keys, causal, oT, out_bias):
            ns = len(keys)
            nk = sum(keys)
            first_rows, rows = NR, NR + NM
            parts = [area.take(NT * HG, PARTS, DH, dtype=BF16) for _ in range(2)]
            ahead = [area.take(HG, T, dtype=BF16) for _ in range(2)]
            qT, kT = (area.take(HG, T, dtype=BF16) for _ in range(2))
            V = area.take(ns, HG, HP)
            probs = area.take(4, 2, HALF)
            low = area.take(HALF)
            kept, low_turned = xT[:, 0, 1:1 + T].rearrange("p (half t) -> p half t", half=2), xT[:, 1, 1:1 + HALF]
            idle = xn[:, :, :].rearrange("p i d -> p (i d)").rearrange("p (four i d) -> p four i d", four=4, i=NT)
            tops = small[:, 0:2 * HG * NT].rearrange("p (h i two) -> p h i two", h=HG, two=2)
            top, top_rest = small[:, 64:96], small[:, 96:128]
            top_bf = small[:, 128:128 + 48].bitcast(BF16).rearrange("p (a b) -> p a b", b=NM)
            written = (act.now(), dve.now(), pool.now())
            for e in (pool, act, dve):
                e.after(*written)
            pool.own(nc.gpsimd.memset(kT[NR:rows, :, :], 1.0))
            pool.own(nc.gpsimd.memset(V, 1.0))
            pool.done(nc.gpsimd.tensor_tensor(x[:, :, :], x[:, :, :], spread(out_bias[:, :], 1, NT), ALU.add))
            dve.own(nc.vector.memset(small[:, 0:2 * HG * NT], -3e38))

            def parts_of(e):
                src, n = ((q_all, NT), (k_all, ns))[e]
                flat, r = (idle[:, 2 * e + j, 0:n, :].rearrange("p i (h d) -> p (i h) d", d=DH) for j in range(2))
                at = lambda j: parts[e][:, 0:n * HG, j, :]
                high, mid, last = ((0, 1, 2), (3, 4), 5) if e == 0 else ((0, 3, 5), (1, 4), 2)
                return src, idle[:, 2 * e, 0:n, :], flat, r, [at(j) for j in high], [at(j) for j in mid], at(last)

            def split(e, g):
                eng, ops = ((dve, nc.vector), (pool, nc.gpsimd))[e]
                src, gathered, flat, r, high, mid, last = parts_of(e)
                turned = pe.now()

                def step(op, *args):
                    def run():
                        eng.after(eng.now(), turned)
                        eng.done(op(*args))
                    return run

                copy, minus = ops.tensor_copy, ops.tensor_tensor
                return [step(copy, gathered, src[:, :, bass.ds(g * GW, GW)]),
                        step(copy, high[0], flat),
                        step(minus, r, flat, high[0], ALU.subtract),
                        step(copy, mid[0], r),
                        step(minus, last, r, mid[0], ALU.subtract),
                        step(copy, high[1], high[0]),
                        step(copy, high[2], high[0]),
                        step(copy, mid[1], mid[0])]

            def split_first():
                gathers, cut = {}, [None, None]
                for e in (1, 0):
                    src, gathered, *_ = parts_of(e)
                    gathers[e] = act.done(nc.scalar.copy(gathered, src[:, :, 0:GW]))
                for e in (1, 0):
                    _, _, flat, r, high, mid, last = parts_of(e)
                    dve.after(gathers[e])
                    h = dve.own(nc.vector.tensor_copy(high[0], flat))
                    dve.own(nc.vector.tensor_tensor(r, flat, high[0], ALU.subtract))
                    m = dve.own(nc.vector.tensor_copy(mid[0], r))
                    lowest = dve.done(nc.vector.tensor_tensor(last, r, mid[0], ALU.subtract))
                    act.after(h)
                    act.done(nc.scalar.copy(high[1], high[0]))
                    act.done(nc.scalar.copy(high[2], high[0]))
                    act.after(m)
                    cut[e] = (lowest, act.done(nc.scalar.copy(mid[1], mid[0])))
                return cut

            def first_pass(following, cut):
                ring = Ring(3, first=4)
                turned, last = {}, {}
                copied = ready.now()

                def turn(e, h):
                    sizes = FULL if e == 0 else keys
                    pe.after(*cut[e])
                    slot = ring.take(pe)
                    dst = bank(ring.place(slot)).bitcast(BF16)
                    for i, size in enumerate(sizes):
                        src = parts[e][0:size, i * HG + h].rearrange("p a b -> p (a b)")
                        ins = nc.tensor.transpose(dst[0:NR, i * P:i * P + size], src, ident_bf[0:size, 0:size])
                    act.after(pe.done(ins), copied)
                    turned[h] = act.done(nc.scalar.copy(ahead[e][0:NR, h, 0:sum(sizes)], dst[0:NR, 0:sum(sizes)]))
                    ring.release(slot, turned[h])

                def largest(h, tiles, part, s0, n):
                    slot = ring.take(pe)
                    pe.after(turned[h])
                    whole = bank(ring.place(slot))[:, 0:len(tiles) * n].rearrange("p (a n) -> p a n", n=n)
                    for a, i in enumerate(tiles):
                        dst = whole[:, a]
                        masked = causal and P * i < nk and s0 <= P * i < s0 + n
                        ins = nc.tensor.matmul(dst, ahead[0][0:NR, h, i * P:(i + 1) * P],
                                               ahead[1][0:NR, h, s0:s0 + n],
                                               start=True, stop=not masked, skip_group_check=True)
                        if masked:
                            ins = nc.tensor.matmul(dst[:, P * i - s0:n], ident_bf[:, :], tri_bf[:, 0:s0 + n - P * i],
                                                   start=False, stop=True, skip_group_check=True)
                    dve.after(pe.done(ins))
                    t = dve.done(nc.vector.tensor_reduce(tops[:, h, tiles[0]:tiles[-1] + 1, part], whole, AX.X, ALU.max))
                    ring.release(slot, t)
                    last[h] = t

                def negate(h, stage):
                    at = slice(h * NT, (h + 1) * NT)
                    m, rest, cut_m = top[:, at], top_rest[:, at], lambda j: top_bf[:, at, j]
                    dve.after(last[h])
                    if stage == 0:
                        ins = nc.vector.tensor_reduce(m, tops[:, h], AX.X, ALU.max, negate=True)
                    elif stage == 2:
                        ins = nc.vector.tensor_tensor(rest, m, cut_m(0), ALU.subtract)
                    elif stage == 4:
                        ins = nc.vector.tensor_tensor(cut_m(2), rest, cut_m(1), ALU.subtract)
                    else:
                        ins = nc.vector.tensor_copy(cut_m(stage // 2), (m, rest)[stage // 2])
                    last[h] = dve.done(ins)

                def turn_top(h):
                    pe.after(last[h])
                    slot = ring.take(pe)
                    dst = bank(ring.place(slot)).bitcast(BF16)
                    for i in range(NT):
                        ins = nc.tensor.transpose(dst[NR:rows, i * P:(i + 1) * P], top_bf[:, h * NT + i, :], ident_bf[:, :])
                    act.after(pe.done(ins))
                    to = qT if h == HG - 1 else ahead[0]
                    ring.release(slot, act.done(nc.scalar.copy(to[NR:rows, h, :], dst[NR:rows, 0:T])))

                def split_keys():
                    for run in split(1, following):
                        run()

                pieces = [(turn, 0, 0), (turn, 1, 0)]
                for h in range(HG):
                    units, i = [], 0
                    while i < NT:
                        n = min(P * (i + 1), nk) if causal else nk
                        tiles = [i + a for a in range(max(1, HALF // n) if n == nk else 1) if i + a < NT]
                        units += [(largest, h, tiles, part, s0, min(HALF, n - s0)) for part, s0 in enumerate(range(0, n, HALF))]
                        i += len(tiles)
                    extra = []
                    if h < HG - 1:
                        extra += [(turn, 0, h + 1), (turn, 1, h + 1)]
                    if h:
                        extra += [(negate, h - 1, stage) for stage in range(5)] + [None, (turn_top, h - 1)]
                    if h == HG - 1 and following is not None:
                        queries = [(run,) for run in split(0, following)]
                        extra = [(split_keys,)] + [p for pair in zip_longest(extra, queries) for p in pair]
                    at = 0
                    for j, unit in enumerate(units):
                        pieces.append(unit)
                        upto = max(-(-len(extra) * (j + 1) // len(units)), min(len(extra), j + 1))
                        pieces += [p for p in extra[at:upto] if p]
                        at = upto
                return pieces, [(negate, HG - 1, stage) for stage in range(5)] + [(turn_top, HG - 1)]

            def finish(tail, scored):
                def bring(e, heads, r):
                    dve.after(scored, filled)
                    ready.done(nc.vector.tensor_copy((qT, kT)[e][0:r, heads, :], ahead[e][0:r, heads, :]))

                filled = act.now()
                act.after(scored)
                brings = [(1, slice(0, 2), NR), (1, slice(2, 4), NR), (0, slice(0, 2), rows), (0, slice(2, 3), rows),
                          (0, slice(3, 4), NR)]
                for (piece, *args), b in zip_longest(tail, brings):
                    piece(*args)
                    if b:
                        bring(*b)

            def group(g, more):
                valued, divided = pe.now(), dve.now()
                act.done(nc.scalar.activation(small[:, 400:401], ident[:, 0:1], ACT.Exp))
                pool.after(valued)
                v_ready = pool.own(nc.gpsimd.tensor_copy(
                    V[:, :, :, 0:DH], v_all[:, :, bass.ds(g * GW, GW)].rearrange("p i (h d) -> p i h d", d=DH)))
                act.after(valued)
                pe.after(ready.now(), act.now())
                side, tail = first_pass((g + 2) % NG, ((dve.back(4),), (pool.now(),))) if more else ([], [])
                pending = []
                acc, acc_free = bank(7), [act.now()]
                scores, prob = Ring(2, 2), Ring(4)
                steps = [(half, s) for half in range(2) for s in range(ns) if not causal or P * s < HALF * (half + 1)]

                def score(half, s, between):
                    end = HALF * (half + 1)
                    t0 = max(HALF * half, P * s) if causal else HALF * half
                    n, size, out = end - t0, keys[s], []
                    for hp in range(2):
                        slot = scores.take(pe)
                        at = scores.place(slot)
                        for a in range(2):
                            h = 2 * hp + a
                            masked = causal and t0 == P * s
                            ins = nc.tensor.matmul(bank(at + a)[0:size, 0:n], kT[0:rows, h, P * s:P * s + size],
                                                   qT[0:rows, h, t0:end], start=True, stop=not masked,
                                                   skip_group_check=True)
                            if masked:
                                w = min(P, n)
                                ins = nc.tensor.matmul(bank(at + a)[0:size, 0:w], tri_bf[:, 0:size], ident_bf[:, 0:w],
                                                       start=False, stop=True, skip_group_check=True)
                        t = pe.done(ins)
                        ps = prob.take(act)
                        act.after(t)
                        t = act.done(nc.scalar.activation(probs[0:size, ps, :, 0:n], banks(at, 2)[0:size, :, 0:n],
                                                          ACT.Exp, scale=DH ** -0.5))
                        scores.release(slot, t)
                        out.append((ps, t))
                        between()
                    return t0 - HALF * half, n, size, out

                def values(half, s, t0, n, size, out):
                    last = steps[-1] == (half, s) or steps[steps.index((half, s)) + 1][0] != half
                    pe.after(*(t for _, t in out), v_ready)
                    if s == 0:
                        pe.after(acc_free[0])
                    for h in range(HG):
                        ps = out[h // 2][0]
                        ins = nc.tensor.matmul(acc[HP * h:HP * (h + 1), t0:t0 + n], V[0:size, s, h, :],
                                               probs[0:size, ps, h % 2, 0:n], start=(s == 0), stop=last,
                                               skip_group_check=True)
                    t = pe.done(ins)
                    for ps, _ in out:
                        prob.release(ps, t)
                    if last:
                        act.after(t, divided)
                        acc_free[0] = t = act.done(nc.scalar.copy(kept[:, half], acc))
                        sums = low_turned.rearrange("p (n c) -> p n c", c=32)[:, :, DH]
                        inverse = small[:, 192:192 + HALF // 32]
                        dst = oT[:, bass.ds(g, 1), HALF * half:HALF * (half + 1)].rearrange("p a t -> p (a t)")
                        stages = [(nc.vector.transpose, low_turned, kept[:, half]), (nc.vector.reciprocal, inverse, sums),
                                  (nc.vector.transpose, low.rearrange("p (n c) -> p n c", c=32), spread(inverse, 2, 32)),
                                  (nc.vector.tensor_tensor, dst, kept[:, half], low, ALU.mult)]

                        def run(stage, t=t, stages=stages):
                            op, *args = stages[stage]
                            dve.after(t, dve.now())
                            dve.done(op(*args))

                        pending.extend((run, k) for k in range(4))

                places = max(4 * len(steps) - 1 - SLACK, 1)
                run = [0, 0]

                for piece, *args in side[:2]:
                    piece(*args)
                run[1] = len(side[:2])

                def some_side():
                    run[0] = min(run[0] + 1, places)
                    upto = min(len(side), -(-len(side) * run[0] // places))
                    for piece, *args in side[min(run[1], upto):upto]:
                        piece(*args)
                    run[1] = max(run[1], upto)
                    if pending:
                        piece, arg = pending.pop(0)
                        piece(arg)

                waiting = score(*steps[0], some_side)
                for j, step in enumerate(steps):
                    if j + 1 < len(steps):
                        following = score(*steps[j + 1], some_side)
                        scored = pe.now()
                    some_side()
                    if j == len(steps) - 1:
                        assert run[1] == len(side)
                        if more:
                            finish(tail[:-1], scored)
                        values(*step, *waiting)
                        if more:
                            act.after(scored)
                            piece, *args = tail[-1]
                            piece(*args)
                    else:
                        values(*step, *waiting)
                        some_side()
                    waiting = following
                for piece, arg in pending:
                    piece(arg)

            side, tail = first_pass(1, split_first())
            for piece, *args in side:
                piece(*args)
            finish(tail, pe.now())
            pe.after(pool.now())
            with c.loop(NG - 1) as g:
                group(g, True)
            group(NG - 1, False)
            phase()

        def out_project(oT, w, turn):
            ring = Ring(4, first=4)
            for i in range(NT):
                slot = ring.take(pe)
                for g in range(NG):
                    ins = nc.tensor.matmul(bank(ring.place(slot))[:, 0:D], oT[:, g, P * i:P * (i + 1)], w[:, g, :],
                                           start=(g == 0), stop=(g == NG - 1))
                dve.after(pe.done(ins))
                ring.release(slot, dve.done(nc.vector.tensor_tensor(x[:, i, :], x[:, i, :], bank(ring.place(slot))[:, 0:D], ALU.add)))
                completed(i)
                if turn and i == NT - 2:
                    turn_xn(0)
                    turn_xn(1)
            if turn:
                turn_xn(2)
                turn_xn(3)
            area.reset()

        def gated_projections(qkv):
            lines = xn[:, :, :]
            fresh = area.take(NT, 2 * D)
            proj, evacuated = ring_after_turns(4), {}

            def project_tile(i):
                for w0, w1, weights, dst in ((0, D, resident["qkv"], qkv), (D, 3 * D, resident["qkv"], qkv),
                                             (0, 2 * D, resident["kv_geo"], fresh)):
                    slot = proj.take(pe)
                    t = project(bank(slot)[:, 0:w1 - w0], lambda k: x_tile(i, k), P, weights[:, :, w0:w1])
                    act.after(t)
                    evacuated[i] = act.done(nc.scalar.copy(dst[:, i, w0:w1], bank(slot)[:, 0:w1 - w0]))
                    proj.release(slot, evacuated[i])
                pool.after(evacuated[i])
                pool.done(nc.gpsimd.tensor_tensor(qkv[:, i, :], qkv[:, i, :], resident["qkv_b"][:, :], ALU.add))

            for i in range(NT):
                at = bank(4 + i // 2)[:, 256 * (i % 2):256 * (i % 2 + 1)]
                x_tile(i, 0)
                for k in range(KD):
                    nc.tensor.matmul(at[:, 0:64], xT[:, k, P * i:P * (i + 1)], resident["geo"][:, k, 0:64],
                                     start=(k == 0), stop=(k == KD - 1))
                for k in range(KD):
                    ins = nc.tensor.matmul(at[:, 64:256], x_tile(i, k), resident["geo"][:, k, 64:256],
                                           start=(k == 0), stop=(k == KD - 1))
                if i % 2:
                    act.after(pe.done(ins))
                    copied = act.done(nc.scalar.copy(lines[:, i - 1:i + 1, :].rearrange("p a c -> p (a c)"), bank(4 + i // 2)))
            dve.after(copied)
            for i in range(0, 2):
                project_tile(i)
            pts = lines.rearrange("p i (w r) -> p (i w) r", w=2).rearrange("p n (two c h) -> p n two c h", two=2, c=4)
            one, two = pts[:, :, 0], pts[:, :, 1]
            LN_pair = area.take(2, 2 * NT, 6 * H)
            L, N = (LN_pair[:, a].rearrange("p n (k h) -> p n k h", k=6) for a in range(2))
            LN = area.take(2 * NT, 6, H)
            for i, (k0, n) in enumerate(((0, 3), (3, 2), (5, 1))):
                dve.done(nc.vector.tensor_tensor(L[:, :, k0:k0 + n, :], spread(one[:, :, i, :], 2, n),
                                                 two[:, :, i + 1:4, :], ALU.mult))
                t = dve.done(nc.vector.tensor_tensor(N[:, :, k0:k0 + n, :], one[:, :, i + 1:4, :],
                                                     spread(two[:, :, i, :], 2, n), ALU.mult))
            dve.after(t)
            flat = lambda v: v.rearrange("p a b c -> p (a b c)")
            dve.own(nc.vector.tensor_tensor(flat(L), flat(L), flat(N), ALU.subtract))
            dve.own(nc.vector.tensor_tensor(flat(N), flat(L), flat(L), ALU.mult))
            n2, s0, s1, rn = (area.take(2 * NT * H) for _ in range(4))
            dve.own(nc.vector.tensor_reduce(n2.rearrange("p (a h) -> p a h", h=H), N.rearrange("p a k h -> p a h k"),
                                            AX.X, ALU.add))
            act.after(dve.now())
            dve.after(act.done(nc.scalar.activation(s0, n2, ACT.Sqrt)))
            for i in range(2, NT - 2):
                project_tile(i)
            dve.own(nc.vector.tensor_scalar(s0, s0, 1e-18, None, ALU.max))
            dve.own(nc.vector.reciprocal(s1, s0))
            dve.own(nc.vector.tensor_tensor(s1, s1, n2, ALU.mult))
            dve.own(nc.vector.tensor_tensor(s0, s0, s1, ALU.add))
            dve.own(nc.vector.tensor_scalar(s0, s0, 0.5, 1e-12, ALU.mult, ALU.max))
            dve.own(nc.vector.reciprocal(rn, s0))
            by = lambda v, w: v.rearrange("p (i w) k h -> p i w k h", w=2)[:, :, w]
            rnv = rn.rearrange("p (i w h) -> p i w h", w=2, h=H)
            for k in range(6):
                dve.done(nc.vector.tensor_tensor(by(LN, 0)[:, :, k, :], by(L, 0)[:, :, 5 - k, :], rnv[:, :, 0, :], ALU.mult))
                t = dve.done(nc.vector.scalar_tensor_tensor(out=by(LN, 1)[:, :, k, :], in0=by(L, 1)[:, :, k, :],
                                                            scalar=J_SIGN[k], in1=rnv[:, :, 1, :],
                                                            op0=ALU.mult, op1=ALU.mult))
            dve.after(t)
            prods = area.take(2 * NT, PAIRS, H)
            s = 0
            for p in range(6):
                n = 6 - p
                t = dve.done(nc.vector.tensor_tensor(prods[:, :, s:s + n, :], spread(LN[:, :, p, :], 2, n),
                                                     LN[:, :, p:6, :], ALU.mult))
                s += n
            pe.after(t)
            turned = area.take(2, 3, T)
            ring = Ring(2, 2, first=4)
            flat_prods = prods.rearrange("p a s h -> p a (s h)")
            got = {}
            for w in range(2):
                for q in range(3):
                    slot = ring.take(pe)
                    dst = banks(ring.place(slot), 2).rearrange("p a b -> p (a b)")
                    for i in range(NT):
                        ins = nc.tensor.transpose(dst[0:CR, P * i:P * (i + 1)],
                                                  flat_prods[:, 2 * i + w, q * CR:(q + 1) * CR], ident[:, :])
                    act.after(pe.done(ins))
                    got[w, q] = act.done(nc.scalar.copy(turned[0:CR, w, q, :], dst[0:CR, :]))
                    ring.release(slot, got[w, q])
            for i in range(NT - 2, NT):
                project_tile(i)
            state = LN_pair.rearrange("p a n k -> p (a n k)")[:, 0:3 * T].rearrange("p (q t) -> p q t", q=3)
            for q in range(3):
                dve.after(got[0, q])
                t = dve.done(nc.vector.tensor_tensor_scan(state[0:CR, q, :], widen(decay[0:CR, :], T),
                                                          turned[0:CR, 0, q, :], 0.0, ALU.mult, ALU.add))
            dve.after(t, got[1, 2])
            read = turned[0:CR, 1]
            dve.done(nc.vector.memset(read[:, :, 0:1], 0.0))
            t = dve.done(nc.vector.tensor_tensor(read[:, :, 1:T], read[:, :, 1:T], state[0:CR, :, 0:T - 1], ALU.mult))
            pe.after(t, act.now())
            for i in range(NT):
                for q in range(3):
                    ins = nc.tensor.matmul(bank(4)[:, H * i:H * (i + 1)], turned[0:CR, 1, q, P * i:P * (i + 1)],
                                           resident["pair_sum"][0:CR, q, :], start=(q == 0), stop=(q == 2))
            dve.after(pe.done(ins))
            t = dve.own(nc.vector.tensor_tensor(gate[:, :, :], bank(4)[:, 0:H * NT].rearrange("p (i h) -> p i h", h=H),
                                                spread(mem_decay[:, :], 1, NT), ALU.mult))
            act.after(t)
            dve.after(act.done(nc.scalar.activation(gate[:, :, :], gate[:, :, :], ACT.Sigmoid)))
            t = dve.own(nc.vector.tensor_scalar(gate[:, :, :], gate[:, :, :], resident["kv_gate"][:, 0:1], None, ALU.mult))
            biased = pool.now()
            for eng, ops, i0, i1 in ((pool, nc.gpsimd, 6, NT), (dve, nc.vector, 0, 3), (dve, nc.vector, 3, 6)):
                eng.after(t, act.now(), biased)
                for a in range(2):
                    part = fresh[:, i0:i1, D * a:D * (a + 1)].rearrange("p i (h d) -> p i h d", h=H)
                    eng.done(ops.tensor_tensor(part, part, spread(gate[:, i0:i1, :], 3, DH), ALU.mult))
                eng.after(eng.now())
                eng.done(ops.tensor_tensor(qkv[:, i0:i1, D:3 * D], qkv[:, i0:i1, D:3 * D], fresh[:, i0:i1, :], ALU.add))

        def column_to_rows(columns, dst):
            diag = area.take(NT, P)
            for i in range(NT):
                t = dve.done(nc.vector.tensor_scalar(diag[:, i, :], ident[:, :], columns[:, i:i + 1], None, ALU.mult))
            pe.after(t)
            for i in range(NT):
                ins = nc.tensor.matmul(banks(6, 2).rearrange("p a b -> p (a b)")[:, P * i:P * (i + 1)], ones[:, :],
                                       diag[:, i, :], start=True, stop=True)
            t = pe.done(ins)
            act.after(t)
            return act.done(nc.scalar.copy(dst, banks(6, 2).rearrange("p a b -> p (a b)")))

        def quantiser(top, inverse, scale, w_inverse):
            dve.own(nc.vector.tensor_scalar(top, top, 1e-5, None, ALU.max))
            dve.own(nc.vector.reciprocal(scale, top))
            dve.own(nc.vector.tensor_scalar(scale, scale, 127.0, None, ALU.mult))
            dve.own(nc.vector.tensor_scalar(inverse, top, 1.0 / 127.0, w_inverse, ALU.mult, ALU.mult))

        def bit_ffn():
            hid_flat = area.take(NH * (T + 2))
            hid = hid_flat.rearrange("p (m t) -> p m t", m=NH)
            conv = area.take(NH, T)
            whole = area.take(T)
            xqT = area.take(KD, T, dtype=BF16)
            xqb = hid_flat[:, 0:NT * D // 2].bitcast(BF16).rearrange("p (i d) -> p i d", i=NT)
            hq = hid_flat[:, 2 * (T + 2):2 * (T + 2) + NH * T // 2].bitcast(BF16).rearrange("p (m t) -> p m t", m=NH)
            top, inv, scale = (small[:, 400 + NT * j:400 + NT * (j + 1)] for j in range(3))
            dve.after(normed[-1])
            dve.own(nc.vector.tensor_reduce(top, xn[:, :, :], AX.X, ALU.max, apply_absolute_value=True))
            quantiser(top, inv, scale, wscale[:, 0:1])
            for i in range(NT):
                t = dve.done(nc.vector.tensor_scalar(xn[:, i, :], xn[:, i, :], scale[:, i:i + 1], ROUND, ALU.mult, ALU.add))
            dve.after(t)
            t = dve.done(nc.vector.tensor_scalar(xqb, xn[:, :, :], ROUND, None, ALU.subtract))
            pe.after(t)
            for k in range(KD):
                dst = bank(k).bitcast(BF16)
                for i in range(NT):
                    ins = nc.tensor.transpose(dst[:, P * i:P * (i + 1)], xqb[:, i, P * k:P * (k + 1)], ident_bf[:, :])
                act.after(pe.done(ins))
                turned = act.done(nc.scalar.copy(xqT[:, k, :], dst))
            spread_done = column_to_rows(inv, whole)
            dve.after(turned, spread_done)
            for col in (0, T + 1):
                dve.done(nc.vector.memset(hid[:, :, col:col + 1], 0.0))
            ring = Ring(6)
            pe.after(turned)
            w, hi = resident["conv_w"], hid[:, 0, 0:T]
            middle, filled = {}, {}

            def hidden(m):
                for half in range(2):
                    slot = ring.take(pe)
                    for k in range(KD):
                        ins = nc.tensor.matmul(bank(slot), w1q[:, k, P * m:P * (m + 1)],
                                               xqT[:, k, HALF * half:HALF * (half + 1)], start=(k == 0), stop=(k == KD - 1))
                    dve.after(pe.done(ins))
                    t = dve.done(nc.vector.tensor_tensor(hid[:, m, 1 + HALF * half:1 + HALF * (half + 1)], bank(slot),
                                                         whole[:, HALF * half:HALF * (half + 1)], ALU.mult))
                    ring.release(slot, t)
                act.after(t)
                middle[m] = act.done(nc.scalar.activation(conv[:, m, :], hid[:, m, 1:1 + T], ACT.Identity,
                                                          bias=resident["conv_b"][:, m:m + 1], scale=w[:, m, 1:2]))

            def convolve(m):
                dve.after(middle[m])
                dve.own(nc.vector.scalar_tensor_tensor(out=conv[:, m, :], in0=hid[:, m, 0:T], scalar=w[:, m, 0:1],
                                                       in1=conv[:, m, :], op0=ALU.mult, op1=ALU.add))
                t = dve.done(nc.vector.scalar_tensor_tensor(out=conv[:, m, :], in0=hid[:, m, 2:2 + T], scalar=w[:, m, 2:3],
                                                            in1=conv[:, m, :], op0=ALU.mult, op1=ALU.add))
                act.after(t)
                act.own(nc.scalar.activation(conv[:, m, :], conv[:, m, :], ACT.Silu))
                filled[m] = act.done(nc.scalar.activation(hid[:, m, 0:T], conv[:, m, :], ACT.Abs))

            def raise_top(m):
                dve.after(filled[m], dve.now())
                return dve.done(nc.vector.tensor_tensor(hi, hi, hid[:, m, 0:T], ALU.max))

            for m in range(NH + 2):
                if m < NH:
                    hidden(m)
                if 1 <= m <= NH:
                    convolve(m - 1)
                if m == 2:
                    dve.after(filled[0])
                if m > 2:
                    t = raise_top(m - 2)
            pe.after(t)
            for i in range(NT):
                ins = nc.tensor.transpose(banks(0, 2).rearrange("p a b -> p (a b)")[:, P * i:P * (i + 1)],
                                          hi[:, P * i:P * (i + 1)], ident[:, :])
            dve.after(pe.done(ins))
            dve.own(nc.vector.tensor_reduce(top, banks(0, 2).rearrange("p a b -> p (a b)")
                                            .rearrange("p (i b) -> p i b", i=NT), AX.X, ALU.max))
            quantiser(top, inv, scale, wscale[:, 1:2])
            t = column_to_rows(scale, whole)
            dve.after(t)
            done = []
            for m in range(NH):
                dve.own(nc.vector.tensor_tensor(conv[:, m, :], conv[:, m, :], whole, ALU.mult))
                done.append(dve.done(nc.vector.tensor_scalar(hq[:, m, :], conv[:, m, :],
                                                             ROUND, ROUND, ALU.add, ALU.subtract)))
            products = []
            for m in range(NH):
                pe.after(done[m])
                for i in range(NT):
                    ins = nc.tensor.matmul(bank(i)[:, 0:D], hq[:, m, P * i:P * (i + 1)], w2q[:, m, :],
                                           start=(m == 0), stop=(m == NH - 1), skip_group_check=True)
                    if m == NH - 1:
                        products.append(pe.done(ins))
            for i in range(NT):
                dve.after(products[i])
                dve.done(nc.vector.scalar_tensor_tensor(out=x[:, i, :], in0=bank(i)[:, 0:D], scalar=inv[:, i:i + 1],
                                                        in1=x[:, i, :], op0=ALU.mult, op1=ALU.add))
                completed(i)
            turn_all()

        def wide_attention():
            pe.after(*turned_x)
            qT, kT = area.take(KD, T), area.take(KD, S)
            v = area.take(2, D)
            ring = Ring(8)
            for m in range(KD):
                for half in range(2):
                    slot = ring.take(pe)
                    for k in range(KD):
                        ins = nc.tensor.matmul(bank(slot), resident["wide_q"][:, k, P * m:P * (m + 1)],
                                               xT[:, k, 1 + HALF * half:1 + HALF * (half + 1)],
                                               start=(k == 0), stop=(k == KD - 1))
                    act.after(pe.done(ins))
                    t = act.done(nc.scalar.activation(qT[:, m, HALF * half:HALF * (half + 1)], bank(slot), ACT.Identity,
                                                      bias=resident["wide_qb"][:, m:m + 1]))
                    ring.release(slot, t)
                slot = ring.take(pe)
                for k in range(KD):
                    ins = nc.tensor.matmul(bank(slot)[:, 0:S], resident["wide_k"][:, k, P * m:P * (m + 1)], ctxT[:, k, :],
                                           start=(k == 0), stop=(k == KD - 1))
                act.after(pe.done(ins))
                t = act.done(nc.scalar.activation(kT[:, m, :], bank(slot)[:, 0:S], ACT.Identity,
                                                  bias=resident["wide_kb"][:, m:m + 1]))
                ring.release(slot, t)
            for i, n in enumerate(CTX):
                slot = ring.take(pe)
                t = project(bank(slot)[0:n, 0:D], lambda k: ctx_tile(i, k), n, resident["wide_v"])
                add_bias(v[0:n, i, :], bank(slot)[0:n, 0:D], resident["wide_vb"][0:n, :], t, ring, slot)
            pe.after(act.now(), dve.now())
            E = area.take(2, S)
            ET = area.take(2, 2, P)
            top, rsum = small[:, 400:408], small[:, 408:416]
            scale = D ** -0.5
            exponentials, turned, read, placed = {}, {}, {}, {}

            def scores(i):
                s_bank = bank(i % 2)
                pe.after(exponentials.get(i - 2))
                for k in range(KD):
                    ins = nc.tensor.matmul(s_bank[:, 0:S], qT[:, k, P * i:P * (i + 1)], kT[:, k, :],
                                           start=(k == 0), stop=(k == KD - 1))
                dve.after(pe.done(ins))
                dve.own(nc.vector.tensor_reduce(top[:, i:i + 1], s_bank[:, 0:S], AX.X, ALU.max))
                t = dve.done(nc.vector.tensor_scalar(top[:, i:i + 1], top[:, i:i + 1], -scale, None, ALU.mult))
                act.after(t, read.get(i - 2))
                exponentials[i] = act.done(nc.scalar.activation(E[:, i % 2, :], s_bank[:, 0:S], ACT.Exp,
                                                                bias=top[:, i:i + 1], scale=scale,
                                                                accum_out=rsum[:, i:i + 1]))

            def turn(i):
                e, t_bank = i % 2, bank(2 + i % 2)
                pe.after(exponentials[i], turned.get(i - 2))
                nc.tensor.transpose(t_bank[:, 0:P], E[:, e, 0:P], ident[:, :])
                read[i] = pe.done(nc.tensor.transpose(t_bank[0:CTX[1], P:2 * P], E[:, e, P:S], ident[:, :]))
                act.after(read[i], placed.get(i - 2))
                act.done(nc.scalar.copy(ET[:, e, 0, :], t_bank[:, 0:P]))
                turned[i] = act.done(nc.scalar.copy(ET[0:CTX[1], e, 1, :], t_bank[0:CTX[1], P:2 * P]))

            def values(i):
                e, o_bank = i % 2, bank(4 + i % 2)
                pe.after(turned[i], added.get(i - 2))
                for j, n in enumerate(CTX):
                    ins = nc.tensor.matmul(o_bank[:, 0:D], ET[0:n, e, j, :], v[0:n, j, :], start=(j == 0), stop=(j == 1))
                placed[i] = pe.done(ins)
                dve.after(exponentials[i])
                dve.own(nc.vector.reciprocal(rsum[:, i:i + 1], rsum[:, i:i + 1]))
                dve.after(placed[i])
                added[i] = dve.done(nc.vector.scalar_tensor_tensor(out=x[:, i, :], in0=o_bank[:, 0:D],
                                                                   scalar=rsum[:, i:i + 1], in1=x[:, i, :],
                                                                   op0=ALU.mult, op1=ALU.add))
                completed(i)

            added = {}
            for i in range(NT + 2):
                if i < NT:
                    scores(i)
                if 0 <= i - 1 < NT:
                    turn(i - 1)
                if 0 <= i - 2:
                    values(i - 2)
            turn_all()

        def experts(b):
            pe.after(*turned_x)
            work_scope.close()
            n_rounded = 2 * 2 * 3 * D + 2 * KD * T + 2 * 4 * HALF
            plain = ctx.enter_context(nc.sbuf_tensor("expert_work", [P, words - n_rounded], F32))
            rounded = Area(ctx.enter_context(nc.sbuf_tensor("rounded", [P, n_rounded], F32R)), n_rounded)
            area = Area(plain, words - n_rounded)
            logits, onehot, comb = area.take(NT, NE), area.take(NT, NE), area.take(NT, NE)
            best = area.take(NT, 8)
            index = area.take(NT, 8).bitcast(U32)
            p = area.take(4, NT)
            combT = area.take(T)
            raw = [area.take(3 * D) for _ in range(2)]
            high, low = ([rounded.take(3 * D) for _ in range(2)] for _ in range(2))
            row = [area.take(T) for _ in range(2)]
            x_high, x_low = rounded.take(KD, T), rounded.take(KD, T)
            silu, full = area.take(2, HALF), area.take(2, HALF)
            hid_high, hid_low = rounded.take(4, HALF), rounded.take(4, HALF)
            out = banks(4, 4).rearrange("p k (two d) -> p (k two) d", two=2)
            pair = Ring(2, 2)
            number = [0]
            silu_free, full_free, hid_free = [None] * 2, [None] * 2, [None] * 4
            waiting = []

            def load_weights(parity, e):
                wg, wu = (raw[parity][:, k * D:(k + 1) * D].rearrange("p (a e) -> p a e", a=KD) for k in range(2))
                load(wg, io["w_gate"][bass.ds(e, 1)].rearrange("a k p e -> p (a k) e"), sem_expert[parity])
                load(wu, io["w_up"][bass.ds(e, 1)].rearrange("a k p e -> p (a k) e"), sem_expert[parity])
                return load(raw[parity][:, 2 * D:], io["w_down"][bass.ds(e, 1)].rearrange("a p d -> p (a d)"),
                            sem_expert[parity])

            def load_row(parity, e):
                return load(row[parity], io["combine"][bass.ds(e, 1), :].broadcast_to([P, T]), sem_row[parity])

            def cut(parity, columns, sources, *tokens):
                hi, lo = high[parity][:, columns], low[parity][:, columns]
                n = (columns.stop - columns.start) // len(sources)
                pool.after(*tokens)
                for j, source in enumerate(sources):
                    shape = lambda v: v[:, j * n:(j + 1) * n] if len(source.shape) == 2 else \
                        v[:, j * n:(j + 1) * n].rearrange("p (a e) -> p a e", a=KD)
                    t = pool.own(nc.gpsimd.tensor_copy(shape(hi), source))
                    t = pool.own(nc.gpsimd.tensor_tensor(shape(lo), source, shape(hi.bitcast(F32)), ALU.subtract))
                return t

            def product(dst, a_parts, b_parts, start, stop):
                for n, (i, j) in enumerate(((0, 0), (0, 1), (1, 0))):
                    ins = nc.tensor.matmul(dst, a_parts[i], b_parts[j],
                                           start=start and n == 0, stop=stop and n == 2, skip_group_check=True)
                return ins

            def down():
                k, half, parity, ready, first, last = waiting.pop(0)
                pe.after(*ready)
                for i in range(4):
                    tile = 4 * half + i
                    ins = product(out[:, tile, :], [v[:, k, P * i:P * (i + 1)] for v in (hid_high, hid_low)],
                                  [v[parity][:, 2 * D:] for v in (high, low)], first and tile % 2 == 0, last)
                hid_free[k] = pe.done(ins)

            def unit(half, parity, gate_up, down_cut, weighted=None, first=False, last=False):
                k = number[0] % 4
                number[0] += 1
                slot = pair.take(pe)
                at = pair.place(slot)
                pe.after(gate_up)
                for j in range(2):
                    for a in range(KD):
                        w0 = j * D + a * ED
                        ins = product(bank(at + j), [v[parity][:, w0:w0 + ED] for v in (high, low)],
                                      [v[:, a, HALF * half:HALF * (half + 1)] for v in (x_high, x_low)],
                                      a == 0, a == KD - 1)
                    if j == 0:
                        act.after(pe.done(ins), silu_free[half])
                activated = act.done(nc.scalar.activation(silu[:, half, :], bank(at), ACT.Silu))
                multiplied = pe.done(ins)
                if len(waiting) == 2:
                    down()
                dve.after(activated, multiplied, full_free[half])
                value = full[:, half, :]
                t = dve.own(nc.vector.tensor_tensor(value, silu[:, half, :], bank(at + 1), ALU.mult))
                pair.release(slot, t)
                silu_free[half] = t
                if weighted is not None:
                    dve.after(weighted)
                    t = dve.own(nc.vector.tensor_tensor(value, value, row[parity][:, HALF * half:HALF * (half + 1)], ALU.mult))
                act.after(t, hid_free[k])
                rounded = act.done(nc.scalar.copy(hid_high[:, k, :], value))
                dve.after(rounded, hid_free[k])
                full_free[half] = t = dve.done(nc.vector.tensor_tensor(hid_low[:, k, :], value,
                                                                      hid_high[:, k, :].bitcast(F32), ALU.subtract))
                waiting.append((k, half, parity, (t, down_cut), first, last))

            sp_after(turned_x[-1])
            loaded_first = load_weights(1, 0)
            load_weights(0, 1)
            shared = lambda j: ([resident[name][:, :, ED * j:ED * (j + 1)] for name in ("sh_gate", "sh_up")],
                                [resident["sh_down"][:, j, :]])
            GATE_UP, DOWN = slice(0, 2 * D), slice(2 * D, 3 * D)
            pool.after(turned_x[-1])
            shared_cut = cut(0, GATE_UP, shared(0)[0])
            shared_down = cut(0, DOWN, shared(0)[1])
            act.after(*turned_x)
            for half in range(2):
                at = slice(HALF * half, HALF * (half + 1))
                t = act.done(nc.scalar.copy(x_high[:, :, at], xT[:, :, 1 + at.start:1 + at.stop]))
                dve.after(t)
                x_cut = dve.done(nc.vector.tensor_tensor(x_low[:, :, at], xT[:, :, 1 + at.start:1 + at.stop],
                                                         x_high[:, :, at].bitcast(F32), ALU.subtract))

            for i in range(NT):
                for k in range(KD):
                    ins = nc.tensor.matmul(bank(4)[:, NE * i:NE * (i + 1)], x_tile(i, k), resident["router"][:, k, :],
                                           start=(k == 0), stop=(k == KD - 1))
            dve.after(pe.done(ins))
            t = dve.own(nc.vector.tensor_tensor(logits, bank(4)[:, 0:NT * NE].rearrange("p (i e) -> p i e", e=NE),
                                                spread(resident["router_b"][:, :], 1, NT), ALU.add))
            for i in range(NT):
                t = dve.done(nc.vector.max(best[:, i, :], logits[:, i, :]))
            dve.after(t)
            t = dve.done(nc.vector.tensor_tensor(p[:, 0, :], best[:, :, 1], best[:, :, 0], ALU.subtract))
            act.after(t)
            exponential = act.done(nc.scalar.activation(p[:, 1, :], p[:, 0, :], ACT.Exp))
            for i in range(NT):
                t = dve.done(nc.vector.max_index(index[:, i, :], best[:, i, :], logits[:, i, :]))
            pe.after(x_cut)
            unit(0, 0, shared_cut, shared_down, first=True)
            dve.after(t, exponential)
            chosen = area.take(2, NT)
            dve.done(nc.vector.tensor_copy(chosen, index[:, :, 0:2].rearrange("p i two -> p two i")))
            dve.own(nc.vector.tensor_scalar(p[:, 0, :], p[:, 1, :], 1.0, None, ALU.add))
            dve.own(nc.vector.reciprocal(p[:, 2, :], p[:, 0, :]))
            dve.own(nc.vector.tensor_tensor(p[:, 3, :], p[:, 1, :], p[:, 2, :], ALU.mult))
            unit(1, 0, shared_cut, shared_down, first=True)
            for i in range(NT):
                for j, o in ((0, comb), (1, onehot)):
                    t = dve.done(nc.vector.tensor_scalar(o[:, i, :], resident["iota"][:, :], chosen[:, j, i:i + 1],
                                                         p[:, 2 + j, i:i + 1], ALU.is_equal, ALU.mult))
            dve.after(t)
            t = dve.own(nc.vector.tensor_tensor(comb, comb, onehot, ALU.add))
            slot = pair.take(pe)
            turned = banks(pair.place(slot), 2).rearrange("p a b -> p (a b)")
            pe.after(t)
            for i in range(NT):
                ins = nc.tensor.transpose(turned[0:NE, P * i:P * (i + 1)], comb[:, i, :], ident[:, :])
            act.after(pe.done(ins))
            t = act.done(nc.scalar.copy(combT[0:NE, :], turned[0:NE, :]))
            pair.release(slot, t)
            sp_after(t)
            sp_after(load(io["combine"], combT[0:NE, :], sem_comb))
            row_ready = load_row(1, 0)
            load_row(0, 1)

            def expert(parity, loaded, row_loaded, two_later, fresh=False):
                sources = [raw[parity][:, k * D:(k + 1) * D] for k in range(2)]
                gate_up = cut(parity, GATE_UP, sources, loaded, None if fresh else pe.back(6))
                down_cut = cut(parity, DOWN, [raw[parity][:, 2 * D:]], None if fresh else pe.now())
                for half in range(2):
                    unit(half, parity, gate_up, down_cut, row_loaded)
                if two_later is not None:
                    sp_after(down_cut)
                    load_weights(parity, two_later)
                    sp_after(dve.now())
                    load_row(parity, two_later)

            def units_before():
                hid_free[:] = [pe.back(3), pe.now(), None, None] if number[0] % 4 == 0 else [None, None, pe.back(3), pe.now()]
                pair.free = [dve.back(5), dve.back(2)][::1 if pair.at % 2 == 0 else -1]
                silu_free[:] = [dve.back(5), dve.back(2)]
                full_free[:] = [dve.back(3), dve.now()]
                for n, ready in ((0, dve.back(3)), (1, dve.now())):
                    k, half, parity, _, first, last = waiting[n]
                    waiting[n] = (k, half, parity, (ready, pool.now()), first, last)

            expert(1, loaded_first, row_ready, 2, fresh=True)
            with c.loop((NE - 2) // 2) as j:
                units_before()
                for parity in range(2):
                    loaded, row_loaded = c.add(sem_expert[parity], 0), c.add(sem_row[parity], 0)
                    expert(parity, loaded, row_loaded, (j * 2 + 3 + parity) % NE)
            units_before()
            expert(0, c.add(sem_expert[0], 0), c.add(sem_row[0], 0), None)
            gate_up = cut(1, GATE_UP, shared(1)[0], pe.back(6))
            down_cut = cut(1, DOWN, shared(1)[1], pe.now())
            for half in range(2):
                unit(half, 1, gate_up, down_cut, last=True)
            done = []
            for half in range(2):
                down()
                done.append(pe.now())
            sp_after(c.add(sem_expert[1], 0), c.add(sem_row[1], 0))
            for half in range(2):
                dve.after(done[half])
                i0, i1 = NT // 2 * half, NT // 2 * (half + 1)
                for i in range(i0, i1):
                    t = dve.done(nc.vector.tensor_tensor(xn[:, i, :], x[:, i, :], out[:, i, :], ALU.add))
                sp_after(t)
                load(io["out"][bass.ds(b, 1), P * i0:P * i1, :].rearrange("b (i p) d -> p (b i) d", p=P),
                     xn[:, i0:i1, :], sem_out)
                loaded = load_x((b + 1) % B, i0, i1)
            sp_after(load_context((b + 1) % B), loaded, c.add(sem_out, 0))

        area.reset()
        sp_after(first_loaded)
        with c.fresh_loop(B, owned) as b:
            for k in range(KD):
                for i, n in enumerate(CTX):
                    ins = nc.tensor.transpose(bank(7)[:, k * 256 + P * i:k * 256 + P * i + n],
                                              ctx_rows[0:n, i, P * k:P * (k + 1)], ident[0:n, 0:n])
            act.after(pe.done(ins))
            act.done(nc.scalar.copy(ctxT[:, :, :], bank(7).rearrange("p (k s) -> p k s", k=KD)[:, :, 0:S]))

            for i in range(NT):
                completed(i)
            turn_all()
            qkv = area.take(NT, 3 * D)
            mark = area.at
            gated_projections(qkv)
            area.at = mark
            oT = area.take(NG, T)
            attention(qkv[:, :, 0:D], qkv[:, :, D:2 * D], qkv[:, :, 2 * D:3 * D], FULL, True, oT,
                      resident["out0_b"])
            out_project(oT, resident["out0"], True)

            oT = area.take(NG, T)
            q = area.take(NT, D)
            kv = area.take(2, 2 * D)
            mark = area.at
            ring = ring_after_turns(8)
            kraw, qraw, t1, t2 = area.take(2, D), area.take(NT, D), area.take(NT * H, 8), area.take(NT * H, 8)
            for i in range(NT):
                slot = ring.take(pe)
                t = project(bank(slot)[:, 0:D], lambda k: x_tile(i, k), P, resident["cross_q"])
                add_bias(qraw[:, i, :], bank(slot)[:, 0:D], resident["cross_qb"][:, :], t, ring, slot)
            for i, n in enumerate(CTX):
                slot = ring.take(pe)
                t = project(bank(slot)[0:n, :], lambda k: ctx_tile(i, k), n, resident["cross_kv"])
                add_bias(kraw[0:n, i, :], bank(slot)[0:n, 0:D], resident["cross_kvb"][0:n, 0:D], t, ring, slot)
                dve.after(add_bias(kv[0:n, i, D:2 * D], bank(slot)[0:n, D:2 * D], resident["cross_kvb"][0:n, D:2 * D], t, ring, slot))

            def rotate(who, ops, dst, src, i0, i1, n=P):
                even = lambda v, o: v[0:n, i0:i1, 0:D].rearrange("p i (h f two) -> p two i h f", f=8, two=2)[:, o]
                xe, xo = even(src, 0), even(src, 1)
                cos, sin = (spread(resident[name][0:n, i0:i1, :], 2, H) for name in ("cos", "sin"))
                a1, a2 = (v[0:n, H * i0:H * i1, :].rearrange("p (i h) f -> p i h f", h=H) for v in (t1, t2))
                for o, (u, v, op) in enumerate(((cos, sin, ALU.subtract), (sin, cos, ALU.add))):
                    who.done(ops.tensor_tensor(a1, xe, u, ALU.mult))
                    who.own(ops.tensor_tensor(a2, xo, v, ALU.mult))
                    who.own(ops.tensor_tensor(even(dst, o), a1, a2, op))

            queries = dve.back(4)
            pool.after(queries)
            rotate(pool, nc.gpsimd, q, qraw, 6, NT)
            for i, n in enumerate(CTX):
                rotate(dve, nc.vector, kv, kraw, i, i + 1, n)
            rotate(dve, nc.vector, q, qraw, 2, 6)
            rotate(dve, nc.vector, q, qraw, 0, 2)
            area.at = mark
            attention(q, kv[:, :, 0:D], kv[:, :, D:2 * D], CTX, True, oT, resident["cross_ob"])
            out_project(oT, resident["cross_o"], False)

            bit_ffn()

            qkv = area.take(NT, 3 * D)
            oT = area.take(NG, T)
            mark = area.at
            ring = ring_after_turns(8)
            for i in range(NT):
                for a, w in ((0, D), (D, 2 * D)):
                    slot = ring.take(pe)
                    t = project(bank(slot)[:, 0:w], lambda k: x_tile(i, k), P, resident["qkv1"][:, :, a:a + w])
                    add_bias(qkv[:, i, a:a + w], bank(slot)[:, 0:w], resident["qkv1_b"][:, a:a + w], t, ring, slot)
            area.at = mark
            attention(qkv[:, :, 0:D], qkv[:, :, D:2 * D], qkv[:, :, 2 * D:3 * D], FULL, False, oT,
                      resident["out1_b"])
            out_project(oT, resident["out1"], True)

            wide_attention()
            experts(b)


def tiles(w):
    return np.ascontiguousarray(w.reshape(w.shape[0] // P, P, -1).transpose(1, 0, 2))


def rows(v, n=P):
    return np.ascontiguousarray(np.tile(v.reshape(1, -1), (n, 1)))


def head_rows(w):
    n = w.shape[1]
    out = np.zeros((HG, HP, NG, n), np.float32)
    out[:, :DH] = w.reshape(NG, HG, DH, n).transpose(1, 2, 0, 3)
    return out.reshape(P, NG, n)


def constants():
    f = 1.0 / 10000.0 ** (np.arange(0, DH, 2, dtype=np.float32) / DH)
    angle = np.outer(np.arange(T, dtype=np.float32), f)
    pair_sum = np.zeros((P, 3, H), np.float32)
    slot = 0
    for p in range(6):
        for q in range(p, 6):
            for h in range(H):
                pair_sum[(slot % 7) * H + h, slot // 7, h] = 1.0 if p == q else 2.0
            slot += 1
    tri = np.where(np.arange(P)[None, :] <= np.arange(P)[:, None], 0.0, NEG).astype(np.float32)
    return {"ident": np.eye(P, dtype=np.float32), "tri": tri, "pair_sum": pair_sum,
            "iota": rows(np.arange(NE, dtype=np.float32)),
            "cos": tiles(np.cos(angle)), "sin": tiles(np.sin(angle))}


def kernel(**i):
    import concourse.bacc as bacc
    from concourse.bass_utils import run_bass_kernel_spmd

    i = {k: np.asarray(v) for k, v in i.items()}
    L0, X0, F0, L1, X1, E1 = ("L0_attn_", "L0_xattn_", "L0_ffn_", "L1_attn_", "L1_xattn_", "L1_ffn_")
    points = lambda w: w.reshape(D, H, 4).transpose(0, 2, 1).reshape(D, 4 * H)
    scalar = lambda v: rows(v.reshape(1, 1))
    logit = i[L0 + "decay_logits"]
    resident = {
        **constants(),
        "geo": tiles(np.concatenate([points(i[L0 + n]) for n in ("w1_write", "w2_write", "w1_read", "w2_read")], 1)),
        "qkv": tiles(i[L0 + "qkv_w"]), "qkv_b": rows(i[L0 + "qkv_b"]), "kv_geo": tiles(i[L0 + "kv_geo_w"]),
        "out0": head_rows(i[L0 + "out_w"]), "out0_b": rows(i[L0 + "out_b"]),
        "kv_gate": scalar(i[L0 + "kv_gate"]), "mem_scale": rows(i[L0 + "mem_scale"]), "logits": rows(logit),
        "logit_rows": np.ascontiguousarray(np.tile(logit, P // H).reshape(P, 1)),
        "cross_q": tiles(i[X0 + "Wq"]), "cross_qb": rows(i[X0 + "bq"]),
        "cross_kv": tiles(np.concatenate([i[X0 + "Wk"], i[X0 + "Wv"]], 1)),
        "cross_kvb": rows(np.concatenate([i[X0 + "bk"], i[X0 + "bv"]])),
        "cross_o": head_rows(i[X0 + "Wo"]), "cross_ob": rows(i[X0 + "bo"]),
        "conv_w": tiles(i[F0 + "conv_w"].reshape(HID, 3)), "conv_b": tiles(i[F0 + "conv_b"].reshape(HID, 1)).reshape(P, NH),
        "qkv1": tiles(i[L1 + "w_in"].T), "qkv1_b": rows(i[L1 + "b_in"]),
        "out1": head_rows(i[L1 + "w_out"].T), "out1_b": rows(i[L1 + "b_out"]),
        "wide_q": tiles(i[X1 + "Wq"].T), "wide_k": tiles(i[X1 + "Wk"].T), "wide_v": tiles(i[X1 + "Wv"].T),
        "wide_qb": tiles(i[X1 + "bq"].reshape(D, 1)).reshape(P, KD),
        "wide_kb": tiles(i[X1 + "bk"].reshape(D, 1)).reshape(P, KD), "wide_vb": rows(i[X1 + "bv"]),
        "router": tiles(i[E1 + "router_w"].T), "router_b": rows(i[E1 + "router_bias"]),
        "sh_gate": tiles(i[E1 + "sh_gate"].T), "sh_up": tiles(i[E1 + "sh_up"].T), "sh_down": tiles(i[E1 + "sh_down"].T),
    }
    arrays = {"r_" + k: v for k, v in resident.items()}
    arrays.update({
        "x": i["x"], "ctx": i["ctx_1024"], "w1T": tiles(i[F0 + "w1"].T), "w2T": tiles(i[F0 + "w2"].T),
        "w_gate": i[E1 + "gate_proj"].reshape(NE, KD, P, ED), "w_up": i[E1 + "up_proj"].reshape(NE, KD, P, ED),
        "w_down": i[E1 + "down_proj"],
    })
    arrays = {k: np.ascontiguousarray(v) for k, v in arrays.items()}

    def write(per_trip):
        nc = bacc.Bacc("TRN2", target_bir_lowering=False, num_devices=1)
        io = {k: nc.dram_tensor("in_" + k, v.shape, F32, kind="ExternalInput").ap() for k, v in arrays.items()}
        io["combine"] = nc.dram_tensor("combine", (NE, T), F32, kind="Internal").ap()
        io["out"] = nc.dram_tensor("out", (B, T, D), F32, kind="ExternalOutput").ap()
        build_program(nc, io, per_trip)
        return nc

    per_trip = {}
    write(per_trip)
    nc = write(per_trip)
    return run_bass_kernel_spmd(nc, [{"in_" + k: v for k, v in arrays.items()}], core_ids=[0]).results[0]["out"]
```
